# Optimizing a Trainium2 kernel written in Bass

```python
import numpy as np
import jax
import jax.numpy as jnp

def _softmax(x, axis=-1):
    return jax.nn.softmax(x, axis=axis)

def _gelu(x):
    return jax.nn.gelu(x, approximate=True)

def _silu(x):
    return jax.nn.silu(x)

def _sigmoid(x):
    return jax.nn.sigmoid(x)

def _layernorm(x, axis=-1, eps=1e-05):
    m = jnp.mean(x, axis=axis, keepdims=True)
    v = jnp.var(x, axis=axis, keepdims=True)
    return (x - m) / jnp.sqrt(v + eps)

def _scatter_add(tgt, idx, src, axis=0):
    return tgt.at[idx].add(src)

def _segment_sum(src, seg, n):
    return jax.ops.segment_sum(src, seg, n)
kernel_name = 'mk_decoder_postln_d1_seqx_r4_3765ed'

def setup_inputs(seed: int=0):
    np.random.seed(seed)
    _w = jnp.asarray

    def _rec_inputs():
        import jax
        import jax.numpy as jnp
        _rk = jax.random.key(seed)
        x = 0.0002417 + 0.9998 * jax.random.normal(jax.random.fold_in(_rk, 1), (32, 128, 256), jnp.float32)
        _lenS = 128 - jax.random.randint(jax.random.fold_in(_rk, 7), (32,), 0, max(1, 128 // 4) + 1, jnp.int32)
        _lenS2 = 128 - jax.random.randint(jax.random.fold_in(_rk, 8), (32,), 0, max(1, 128 // 4) + 1, jnp.int32)
        _ctx_1024P = jax.random.normal(jax.random.fold_in(_rk, 11), (32, 16, 256), jnp.float32)
        _ctx_1024c = jax.random.dirichlet(jax.random.fold_in(_rk, 511), 0.3 * jnp.ones((16,), jnp.float32), (32, 128))
        _ctx_1024t = jnp.einsum('bsk,bkd->bsd', _ctx_1024c, _ctx_1024P)
        _ctx_1024t = _ctx_1024t * jax.lax.rsqrt(jnp.mean(jnp.square(_ctx_1024t)) + 1e-12) * 0.953939
        ctx_1024 = 7.22013e-05 + 1.00017 * (_ctx_1024t + 0.3 * jax.random.normal(jax.random.fold_in(_rk, 611), (32, 128, 256), jnp.float32))
        return (x, ctx_1024)
    x, ctx_1024 = _rec_inputs()

    def _L0_attn_setup():
        import jax, jax.numpy as jnp
        import numpy as np
        import math
        N, S, E, H = (4, 1024, 256, 16)
        D = E // H
        key = jax.random.key(seed)
        ks = jax.random.split(key, 9)
        w = 1.0 / math.sqrt(E)
        mk = lambda k, shape: jax.random.normal(k, shape, jnp.float32) * w
        return {'x': jax.random.normal(ks[0], (N, S, E), jnp.float32), 'Wq': mk(ks[1], (E, E)), 'bq': mk(ks[2], (E,)), 'Wk': mk(ks[3], (E, E)), 'bk': mk(ks[4], (E,)), 'Wv': mk(ks[5], (E, E)), 'bv': mk(ks[6], (E,)), 'Wo': mk(ks[7], (E, E)), 'bo': mk(ks[8], (E,))}
    _L0_attn_all = _L0_attn_setup()
    _L0_attn_in = {k: v for k, v in _L0_attn_all.items() if k in ('Wq', 'bq', 'Wk', 'bk', 'Wv', 'bv', 'Wo', 'bo')}
    del _L0_attn_all

    def _L0_xattn_setup():
        import jax, jax.numpy as jnp
        import numpy as np
        D_MODEL = 256
        B, S = (4, 512)
        key = jax.random.key(seed)
        ks = jax.random.split(key, 10)
        s = 1.0 / np.sqrt(D_MODEL)
        return {'k': jax.random.normal(ks[0], (B, S, D_MODEL), jnp.float32), 'v': jax.random.normal(ks[1], (B, S, D_MODEL), jnp.float32), 'q': jax.random.normal(ks[2], (B, S, D_MODEL), jnp.float32), 'Wk': jax.random.normal(ks[3], (D_MODEL, D_MODEL), jnp.float32) * s, 'Wv': jax.random.normal(ks[4], (D_MODEL, D_MODEL), jnp.float32) * s, 'bv': jnp.zeros((D_MODEL,), jnp.float32), 'Wq': jax.random.normal(ks[5], (D_MODEL, D_MODEL), jnp.float32) * s, 'bq': jnp.zeros((D_MODEL,), jnp.float32), 'Wo': jax.random.normal(ks[6], (D_MODEL, D_MODEL), jnp.float32) * s, 'bo': jnp.zeros((D_MODEL,), jnp.float32)}
    _L0_xattn_all = _L0_xattn_setup()
    _L0_xattn_in = {k: v for k, v in _L0_xattn_all.items() if k in ('Wk', 'Wv', 'bv', 'Wq', 'bq', 'Wo', 'bo')}
    del _L0_xattn_all

    def _L0_ffn_setup():
        import jax, jax.numpy as jnp
        import numpy as np
        D_MODEL = 256
        N_HEADS = 16
        D_HEAD = D_MODEL // N_HEADS
        N_EXPERTS = 8
        TOP_K = 2
        D_FF = 512
        EPS = 1e-06

        def rmsnorm(x, w):
            return x * jax.lax.rsqrt(jnp.mean(x * x, axis=-1, keepdims=True) + EPS) * w

        def swiglu(x, w_gate, w_up, w_down):
            return jax.nn.silu(x @ w_gate) * (x @ w_up) @ w_down
        key = jax.random.key(seed)
        ks = jax.random.split(key, 16)
        s = 0.02
        B, S = (2, 512)
        return {'X': jax.random.normal(ks[0], (B, S, D_MODEL), dtype=jnp.float32), 'norm1_w': jnp.ones((D_MODEL,), jnp.float32), 'norm2_w': jnp.ones((D_MODEL,), jnp.float32), 'wq': jax.random.normal(ks[1], (D_MODEL, D_MODEL), jnp.float32) * s, 'wk': jax.random.normal(ks[2], (D_MODEL, D_MODEL), jnp.float32) * s, 'wv': jax.random.normal(ks[3], (D_MODEL, D_MODEL), jnp.float32) * s, 'wo': jax.random.normal(ks[4], (D_MODEL, D_MODEL), jnp.float32) * s, 'router_w': jax.random.normal(ks[5], (D_MODEL, N_EXPERTS), jnp.float32) * s, 'sh_gate': jax.random.normal(ks[6], (D_MODEL, D_FF), jnp.float32) * s, 'sh_up': jax.random.normal(ks[7], (D_MODEL, D_FF), jnp.float32) * s, 'sh_down': jax.random.normal(ks[8], (D_FF, D_MODEL), jnp.float32) * s, 'e_gate': jax.random.normal(ks[9], (N_EXPERTS, D_MODEL, D_FF), jnp.float32) * s, 'e_up': jax.random.normal(ks[10], (N_EXPERTS, D_MODEL, D_FF), jnp.float32) * s, 'e_down': jax.random.normal(ks[11], (N_EXPERTS, D_FF, D_MODEL), jnp.float32) * s}
    _L0_ffn_all = _L0_ffn_setup()
    _L0_ffn_in = {k: v for k, v in _L0_ffn_all.items() if k in ('norm1_w', 'norm2_w', 'wq', 'wk', 'wv', 'wo', 'router_w', 'sh_gate', 'sh_up', 'sh_down', 'e_gate', 'e_up', 'e_down')}
    del _L0_ffn_all
    return {'x': x, 'ctx_1024': ctx_1024, 'L0_attn_Wq': _L0_attn_in['Wq'], 'L0_attn_bq': _L0_attn_in['bq'], 'L0_attn_Wk': _L0_attn_in['Wk'], 'L0_attn_bk': _L0_attn_in['bk'], 'L0_attn_Wv': _L0_attn_in['Wv'], 'L0_attn_bv': _L0_attn_in['bv'], 'L0_attn_Wo': _L0_attn_in['Wo'], 'L0_attn_bo': _L0_attn_in['bo'], 'L0_xattn_Wk': _L0_xattn_in['Wk'], 'L0_xattn_Wv': _L0_xattn_in['Wv'], 'L0_xattn_bv': _L0_xattn_in['bv'], 'L0_xattn_Wq': _L0_xattn_in['Wq'], 'L0_xattn_bq': _L0_xattn_in['bq'], 'L0_xattn_Wo': _L0_xattn_in['Wo'], 'L0_xattn_bo': _L0_xattn_in['bo'], 'L0_ffn_norm1_w': _L0_ffn_in['norm1_w'], 'L0_ffn_norm2_w': _L0_ffn_in['norm2_w'], 'L0_ffn_wq': _L0_ffn_in['wq'], 'L0_ffn_wk': _L0_ffn_in['wk'], 'L0_ffn_wv': _L0_ffn_in['wv'], 'L0_ffn_wo': _L0_ffn_in['wo'], 'L0_ffn_router_w': _L0_ffn_in['router_w'], 'L0_ffn_sh_gate': _L0_ffn_in['sh_gate'], 'L0_ffn_sh_up': _L0_ffn_in['sh_up'], 'L0_ffn_sh_down': _L0_ffn_in['sh_down'], 'L0_ffn_e_gate': _L0_ffn_in['e_gate'], 'L0_ffn_e_up': _L0_ffn_in['e_up'], 'L0_ffn_e_down': _L0_ffn_in['e_down']}

def reference(x, ctx_1024, L0_attn_Wq, L0_attn_bq, L0_attn_Wk, L0_attn_bk, L0_attn_Wv, L0_attn_bv, L0_attn_Wo, L0_attn_bo, L0_xattn_Wk, L0_xattn_Wv, L0_xattn_bv, L0_xattn_Wq, L0_xattn_bq, L0_xattn_Wo, L0_xattn_bo, L0_ffn_norm1_w, L0_ffn_norm2_w, L0_ffn_wq, L0_ffn_wk, L0_ffn_wv, L0_ffn_wo, L0_ffn_router_w, L0_ffn_sh_gate, L0_ffn_sh_up, L0_ffn_sh_down, L0_ffn_e_gate, L0_ffn_e_up, L0_ffn_e_down):
    import jax
    import jax.numpy as jnp

    def _L0_attn_ref(x, Wq, bq, Wk, bk, Wv, bv, Wo, bo):
        import jax, jax.numpy as jnp
        import numpy as np
        import math
        N, S, E, H = (4, 1024, 256, 16)
        D = E // H
        n, s, e = x.shape
        h, d = (H, D)
        scale = 1.0 / math.sqrt(d)

        def proj(W, b):
            y = jnp.einsum('nse,fe->nsf', x, W) + b
            return y.reshape(n, s, h, d).transpose(0, 2, 1, 3)
        Q = proj(Wq, bq)
        K = proj(Wk, bk)
        V = proj(Wv, bv)
        scores = jnp.einsum('nqhd,nkhd->nhqk', Q, K) * scale
        attn = jax.nn.softmax(scores, axis=-1)
        out = jnp.einsum('nhql,nlhd->nqhd', attn, V)
        out = out.reshape(n, s, e)
        return jnp.einsum('nse,fe->nsf', out, Wo) + bo

    def _L0_xattn_ref(k, v, q, Wk, Wv, bv, Wq, bq, Wo, bo):
        import jax, jax.numpy as jnp
        import numpy as np
        D_MODEL = 256
        B, S = (4, 512)
        kp = jnp.einsum('bsd,ed->bse', k, Wk)
        vp = jnp.einsum('bsd,ed->bse', v, Wv) + bv
        qp = jnp.einsum('bsd,ed->bse', q, Wq) + bq
        scale = 1.0 / jnp.sqrt(jnp.float32(kp.shape[-1]))
        scores = jnp.einsum('bqd,bkd->bqk', qp, kp) * scale
        probs = jax.nn.softmax(scores, axis=-1)
        ctx = jnp.einsum('bqk,bkd->bqd', probs, vp)
        return jnp.einsum('bqd,ed->bqe', ctx, Wo) + bo

    def _L0_ffn_ref(X, norm1_w, norm2_w, wq, wk, wv, wo, router_w, sh_gate, sh_up, sh_down, e_gate, e_up, e_down):
        import jax, jax.numpy as jnp
        import numpy as np
        D_MODEL = 256
        N_HEADS = 16
        D_HEAD = D_MODEL // N_HEADS
        N_EXPERTS = 8
        TOP_K = 2
        D_FF = 512
        EPS = 1e-06

        def rmsnorm(x, w):
            return x * jax.lax.rsqrt(jnp.mean(x * x, axis=-1, keepdims=True) + EPS) * w

        def swiglu(x, w_gate, w_up, w_down):
            return jax.nn.silu(x @ w_gate) * (x @ w_up) @ w_down
        B, S, d = X.shape
        scale = 1.0 / jnp.sqrt(jnp.asarray(D_HEAD, X.dtype))
        h = rmsnorm(X, norm1_w)
        q = (h @ wq).reshape(B, S, N_HEADS, D_HEAD)
        k = (h @ wk).reshape(B, S, N_HEADS, D_HEAD)
        v = (h @ wv).reshape(B, S, N_HEADS, D_HEAD)
        scores = jnp.einsum('bshd,bthd->bhst', q, k) * scale
        attn = jax.nn.softmax(scores, axis=-1)
        ctx = jnp.einsum('bhst,bthd->bshd', attn, v).reshape(B, S, d)
        X = X + ctx @ wo
        h2 = rmsnorm(X, norm2_w).reshape(B * S, d)
        logits = h2 @ router_w
        probs = jax.nn.softmax(logits, axis=-1)
        topw, topi = jax.lax.top_k(probs, TOP_K)
        topw = jax.nn.softmax(topw, axis=-1)
        combine = jnp.sum(jax.nn.one_hot(topi, N_EXPERTS, dtype=h2.dtype) * topw[..., None], axis=1)
        shared = swiglu(h2, sh_gate, sh_up, sh_down)
        gate = jnp.einsum('td,edf->etf', h2, e_gate)
        up = jnp.einsum('td,edf->etf', h2, e_up)
        eout = jnp.einsum('etf,efd->etd', jax.nn.silu(gate) * up, e_down)
        spec = jnp.einsum('etd,te->td', eout, combine)
        moe_out = (shared + spec).reshape(B, S, d)
        return X + moe_out
    x = _layernorm(x + _L0_attn_ref(x, L0_attn_Wq, L0_attn_bq, L0_attn_Wk, L0_attn_bk, L0_attn_Wv, L0_attn_bv, L0_attn_Wo, L0_attn_bo), axis=-1)
    x = _layernorm(x + _L0_xattn_ref(ctx_1024, ctx_1024, x, L0_xattn_Wk, L0_xattn_Wv, L0_xattn_bv, L0_xattn_Wq, L0_xattn_bq, L0_xattn_Wo, L0_xattn_bo), axis=-1)
    x = _layernorm(x + _L0_ffn_ref(x, L0_ffn_norm1_w, L0_ffn_norm2_w, L0_ffn_wq, L0_ffn_wk, L0_ffn_wv, L0_ffn_wo, L0_ffn_router_w, L0_ffn_sh_gate, L0_ffn_sh_up, L0_ffn_sh_down, L0_ffn_e_gate, L0_ffn_e_up, L0_ffn_e_down), axis=-1)
    return x

_drawn_inputs = setup_inputs


def setup_inputs(seed=0):
    import zlib

    import numpy as np

    out = dict(_drawn_inputs(seed))
    spreads = {'L0_xattn_bv': (0.0, 0.1),
     'L0_xattn_bq': (0.0, 0.421),
     'L0_xattn_bo': (0.0, 0.1),
     'L0_ffn_norm1_w': (1.0, 0.6),
     'L0_ffn_norm2_w': (1.0, 0.6)}
    factors = {'L0_attn_bq': 3.464,
     'L0_attn_bk': 3.514,
     'L0_attn_bv': 2.76,
     'L0_ffn_wq': 8.0,
     'L0_ffn_wk': 8.0,
     'L0_ffn_router_w': 6.516,
     'L0_ffn_sh_gate': 4.099,
     'L0_ffn_sh_up': 4.045,
     'L0_ffn_sh_down': 4.048,
     'L0_ffn_e_gate': 5.833,
     'L0_ffn_e_up': 5.758,
     'L0_ffn_e_down': 5.761}
    for name, (base, spread) in spreads.items():
        noise = np.random.default_rng([zlib.crc32(name.encode()), seed]).standard_normal(out[name].shape)
        drawn = base * np.exp(spread * noise) if base else spread * noise
        out[name] = jnp.asarray(drawn.astype(out[name].dtype))
    for name, factor in factors.items():
        out[name] = (out[name] * factor).astype(out[name].dtype)
    return out
```

```python
from contextlib import ExitStack

import concourse.bass as bass
from concourse import mybir

F32 = mybir.dt.float32
F32R = mybir.dt.float32r
BF16 = mybir.dt.bfloat16
FP16 = mybir.dt.float16
ALU = mybir.AluOpType
ACT = mybir.ActivationFunctionType
AX = mybir.AxisListType

P = 128
B, S, D = 32, 128, 256
H, DH = 16, 16
DK = D // P
PAIRS = B // 2
TOK = 2 * S
HG = 4
NG = H // HG
HH = H // 2
VP = 3 * DH + 1
E, DFF = 8, 512
FT = DFF // P
NE = E + 1
GT = 512
NGT = B * S // GT

LAG = {0: -1, 1: 0, 2: 1, 3: 2, 4: 3}
FIRST_IT, LAST_IT = -1, PAIRS + 2
LOOP = (4, PAIRS - 1)

ORDER = [
    ("qk1_0", 1), ("qk1_1", 1), ("v1", 1), ("kx", 2), ("heads0", 1), ("turn_o1", 2), ("vx", 2), ("out1", 2),
    ("turn_h", 3), ("turn_o3", 4), ("q3_0", 3), ("k3_0", 3), ("heads1", 1), ("out3", 4), ("v3", 3), ("slot0", 3),
    ("turn_x1", 2), ("q3_1", 3), ("k3_1", 3), ("heads2", 1), ("qx", 2), ("slot1", 3), ("turn_h2", 4),
    ("prep_ctx", 1), ("prep_x", 0), ("sx", 2), ("heads3", 1), ("slot2", 3), ("turn_px", 2), ("logits", 4),
    ("last_heads", 1), ("pvx", 2), ("slot3", 3), ("turn_cx", 2), ("flush", 3), ("outx", 2),
]
NOT_WORK = ("slot", "flush", "prep", "heads", "last_heads")
WORK_JOBS = [(j, s) for j, s in ORDER if not j.startswith(NOT_WORK)]
NW = 3
BANK = {j: n % NW for n, (j, s) in enumerate(WORK_JOBS)}

DVE_OWN = {2: 4, 3: 4}


def pairs_done(stage, it):
    n = it - LAG[stage]
    return max(0, min(PAIRS, n)) if isinstance(it, int) else n


def active(stage, it):
    return not isinstance(it, int) or 0 <= it - LAG[stage] < PAIRS


def jobs_of(it):
    return [(j, s) for j, s in ORDER if active(s, it)]


def bank_uses(job, it):
    n = 0
    seen = False
    for j, s in WORK_JOBS:
        if j == job:
            seen = True
        if BANK[j] == BANK[job]:
            n = n + pairs_done(s, it)
            if not seen and active(s, it):
                n = n + 1
    return n


def bank_read(job, it):
    return bank_uses(job, it) + 1


def slots_before(it):
    return 4 * pairs_done(3, it)


def slots_of(it):
    names = [j for j, s in jobs_of(it) if j.startswith("slot")]
    return {int(j[4:]): n for n, j in enumerate(names)}


def for_iterations(engine, body):
    for it in range(FIRST_IT, LOOP[0]):
        body(it)
    with engine.Fori(LOOP[0], LOOP[1]) as it:
        body(it)
    for it in range(LOOP[1], LAST_IT + 1):
        body(it)


def wait_apart(engine, semaphore, value, passed):
    engine.wait_ge(semaphore, value)
    if not isinstance(value, int):
        engine.sem_inc(passed, 1)


class Own:

    def __init__(self, engine, sems, per_pair):
        self.engine, self.sems, self.per_pair = engine, sems, per_pair

    def begin(self, it):
        self.base = {s: (it - LAG[s]) * n for s, n in self.per_pair.items()}
        self.k = dict.fromkeys(self.per_pair, 0)

    def done(self, stage, instruction, passed=None):
        instruction.then_inc(self.sems[stage], 1)
        self.k[stage] += 1
        value = self.base[stage] + self.k[stage]
        if passed:
            wait_apart(self.engine, self.sems[stage], value, passed)
        else:
            self.engine.wait_ge(self.sems[stage], value)

    def end(self, it):
        for s, n in self.per_pair.items():
            assert not active(s, it) or self.k[s] == n, (s, self.k[s])


def phase_a(nc, t, scratch, sem):
    ctx = ExitStack()

    def sb(name, shape, dt=F32):
        return ctx.enter_context(nc.sbuf_tensor(name, shape, dt))

    with ctx:
        ident = sb("ident", [P, P])
        head_mask = sb("head_mask", [P, HG])
        half_power = sb("half_power", [P, 2])
        bias_qk1 = sb("bias_qk1", [P, 2 * D])
        bias_qx = sb("bias_qx", [P, DK])
        bias_v1 = sb("bias_v1", [P, D])
        bias_o1 = sb("bias_o1", [P, D])
        bias_vx = sb("bias_vx", [P, D])
        bias_ox = sb("bias_ox", [P, D])
        norm1 = sb("norm1", [P, DK])
        norm2 = sb("norm2", [P, DK])
        router = sb("router", [P, DK, E])
        QW = NG * P
        widths = {"wqk1": 2 * D, "wv1": D, "wo1": D, "wkx": D, "wvx": D, "wqx": D, "wox": D,
                  "wq3": QW, "wk3": QW, "wv3": D, "wo3": D}
        scales = {"wq3": DH ** -0.5, "wqx": D ** -0.5}
        w_hi = {n: sb(f"{n}_hi", [P, DK, w], F32R) for n, w in widths.items()}
        w_lo = {n: sb(f"{n}_lo", [P, DK, w], F32R) for n, w in widths.items()}

        key_blocks = sb("key_blocks", [P, 2, 2, 2, HG, S], F32R)
        probs = sb("probs", [P, 2, HH, S])
        probs_hi = sb("probs_hi", [P, HH, S], FP16)
        probs_lo = sb("probs_lo", [P, HH, S], FP16)
        neg_max = sb("neg_max", [P, 2, HH])
        rden = sb("rden", [P, HH])
        osum = sb("osum", [P, HH, DH])
        v_full = sb("v_full", [P, 2 * H, DH])
        v_rest = sb("v_rest", [P, 2 * H, DH])
        qk1 = sb("qk1", [P, 2, 2 * D])
        v1 = sb("v1", [P, 2, D])
        qk_prod = sb("qk_prod", [P, HH, H, DH])
        pv_prod = sb("pv_prod", [P, HH, DH, H])
        head_scores = sb("head_scores", [P, 2, HH, H])
        head_probs = sb("head_probs", [P, 2, HH, H])
        head_max = sb("head_max", [P, HH])
        head_den = sb("head_den", [P, HH])
        head_sum = sb("head_sum", [P, HH, DH])
        o1_rows = sb("o1_rows", [P, 2, D])
        q_rows = {s: sb(f"q_rows{s}", [P, NG, TOK], F32R) for s in (3,)}
        k_parts = {s: sb(f"k_parts{s}", [P, 2, NG, TOK], F32R) for s in (3,)}
        values = {s: sb(f"values{s}", [P, 2 * H, VP], BF16) for s in (3,)}
        att_out = {s: sb(f"att_out{s}", [P, 2, D]) for s in (1, 3)}
        x_t = sb("x_t", [P, DK, TOK])
        ctx_t = sb("ctx_t", [P, DK, TOK])
        parts = {n: (sb(f"{n}_hi", [P, DK, TOK], F32R), sb(f"{n}_lo", [P, DK, TOK], F32R))
                 for n in ("x", "ctx", "o1", "x1", "cx", "h", "o3")}
        x_res = sb("x_res", [P, 2, D])
        y1 = sb("y1", [P, 2, D])
        x1 = sb("x1", [P, 2, D])
        z2 = sb("z2", [P, 2, D])
        x2 = sb("x2", [P, 2, D])
        h_in = sb("h_in", [P, 2, D])
        x2_res = sb("x2_res", [P, 2, D])
        x3 = sb("x3", [P, 2, D])
        x2_x3 = sb("x2_x3", [P, 2, D])
        h2_in = sb("h2_in", [P, 2, D])
        h2_t = sb("h2_t", [P, DK, TOK])
        logit = sb("logit", [P, 2, E])
        kx_t = sb("kx_t", [P, DK, TOK])
        qx_t = sb("qx_t", [P, DK, TOK])
        vx = sb("vx", [P, 2, D])
        px = sb("px", [P, 2, S])
        px_t = sb("px_t", [P, 2, S])
        cx = sb("cx", [P, 2, D])
        neg_max_x = sb("neg_max_x", [P, 2])
        den_x = sb("den_x", [P, 2])
        rden_x = sb("rden_x", [P, 2])
        stats = sb("stats", [P, 2, 6])
        mean_var = {1: sb("mean_var1", [P, 2, 2]), 2: sb("mean_var2", [P, 2, 2])}
        var_eps = sb("var_eps", [P, 2])
        rstd = {n: sb(f"rstd_{n}", [P, 2]) for n in ("y1", "z2", "h", "h2")}
        squares = {n: sb(f"squares_{n}", [P, 2]) for n in ("h", "h2")}
        square_out = sb("square_out", [P, 2, D])
        raw = {n: probs[:, i, :, :].rearrange("p h n -> p (h n)").rearrange("p (d n) -> p d n", d=DK)
               for i, n in enumerate("ab")}

        scores = ctx.enter_context(nc.psum_tensor("scores", [P, HH * S], F32))
        probs_t = ctx.enter_context(nc.psum_tensor("probs_t", [P, HH * S], F32))
        pv = ctx.enter_context(nc.psum_tensor("pv", [P, 512], F32))
        work = [ctx.enter_context(nc.psum_tensor(f"work{i}", [P, 512], F32)) for i in range(NW)]

        const_loaded = sem("const_loaded")
        raw_loaded = {n: sem(f"raw_loaded_{n}") for n in raw}
        raw_hi_done, raw_lo_done = sem("raw_hi_done"), sem("raw_lo_done")
        bias_scaled = sem("bias_scaled")
        ones_set = sem("ones_set")
        x_loaded, ctx_loaded = sem("x_loaded"), sem("ctx_loaded")
        x_res_loaded, x2_res_loaded = sem("x_res_loaded"), sem("x2_res_loaded")
        x2_stored, sum_stored, h2_stored, logit_stored = (sem(n) for n in ("x2_stored", "sum_stored", "h2_stored", "logit_stored"))
        work_ready = [sem(f"work_ready{i}") for i in range(NW)]
        work_read = [sem(f"work_read{i}") for i in range(NW)]
        hi_done = {j: sem(f"hi_done_{j}") for j in
                   ("q3_0", "q3_1", "k3_0", "k3_1", "v3",
                    "turn_o1", "turn_x1", "turn_cx", "turn_h", "turn_o3", "prep_x", "prep_ctx")}
        lo_done = {j: sem(f"lo_done_{j}") for j in ("prep_x", "prep_ctx")}
        v_low_done = {s: sem(f"v_low_done{s}") for s in (3,)}
        v_rest_done = {s: sem(f"v_rest_done{s}") for s in (3,)}
        v_mid_done = {s: sem(f"v_mid_done{s}") for s in (3,)}
        qk_prod_done = sem("qk_prod_done")
        head_scores_done = sem("head_scores_done")
        head_max_done = sem("head_max_done")
        head_shifted = sem("head_shifted")
        head_exp_done = sem("head_exp_done")
        head_den_done = sem("head_den_done")
        pv_prod_done = sem("pv_prod_done")
        head_sum_done = sem("head_sum_done")
        head_out_done = sem("head_out_done")
        o1_stored, o1_loaded = sem("o1_stored"), sem("o1_loaded")
        blocks_done = sem("blocks_done")
        scores_done = sem("scores_done")
        max_done = sem("max_done")
        exp_done = sem("exp_done")
        turned = sem("turned")
        probs_hi_done = sem("probs_hi_done")
        probs_lo_done = sem("probs_lo_done")
        pv_done = sem("pv_done")
        out_done = sem("out_done")
        stat_done = {n: sem(f"stat_done_{n}") for n in rstd}
        rstd_done = {n: sem(f"rstd_done_{n}") for n in rstd}
        x1_done, x2_done, sum_done = sem("x1_done"), sem("x2_done"), sem("sum_done")
        h_done, h2_done = sem("h_done"), sem("h2_done")
        max_x_done, rden_x_done = sem("max_x_done"), sem("rden_x_done")
        dve_own = {s: sem(f"dve_own{s}") for s in DVE_OWN}
        pool_own = sem("pool_own")
        passed = {n: sem(f"passed_{n}") for n in ("sp", "dve", "pool")}

        CONSTS = 11

        split_order = list(widths)
        split_buffer = {n: "ab"[i % 2] for i, n in enumerate(split_order)}

        with nc.Block() as block:

            @block.sync
            def _(sp):
                consts = [(ident, "ident"), (head_mask, "head_mask"),
                          (bias_qx, "bias_qx"), (norm1, "norm1"), (norm2, "norm2")]
                for dst, name in consts:
                    sp.dma_start(dst[:, :], t[name]).then_inc(const_loaded, 16)
                sp.dma_start(router[:, :, :], t["router"]).then_inc(const_loaded, 16)
                for dst, name in ((bias_qk1, "bias_qk1"), (bias_v1, "bias_v1"), (bias_o1, "bias_o1"), (bias_vx, "bias_vx"), (bias_ox, "bias_ox")):
                    sp.dma_start(dst[:, :], t[name].partition_broadcast(P)).then_inc(const_loaded, 16)
                for i, n in enumerate(split_order):
                    b = split_buffer[n]
                    if i >= 2:
                        sp.wait_ge(raw_lo_done, i - 1)
                    sp.dma_start(raw[b][:, :, 0:widths[n]], t[n]).then_inc(raw_loaded[b], 16)

                o1_write = scratch["o1"].rearrange("b (h s d) -> s b h d", h=H, s=S)
                o1_read = scratch["o1"].rearrange("b (s e) -> s b e", s=S)

                def iteration(it):
                    for job, stage in jobs_of(it):
                        pair = it - LAG[stage]
                        if job == "turn_o1":
                            wait_apart(sp, x1_done, pair, passed["sp"])
                            wait_apart(sp, o1_stored, 32 * (pair + 1), passed["sp"])
                            sp.dma_start(o1_rows[:, :, :], o1_read[:, bass.ds(2 * pair, 2), :]).then_inc(o1_loaded, 16)
                            sp.dma_start(x_res[:, :, :], t["x"][:, bass.ds(2 * pair, 2), :]).then_inc(x_res_loaded, 16)
                        if job == "last_heads":
                            wait_apart(sp, head_out_done, 4 * (pair + 1), passed["sp"])
                            for a in range(2):
                                sp.dma_start(o1_write[:, bass.ds(2 * pair + a, 1), :, :].rearrange("s b h d -> s (b h) d"),
                                             att_out[1][:, a, :].rearrange("p (h d) -> p h d", h=H)).then_inc(o1_stored, 16)
                        if job == "turn_o3":
                            if not isinstance(pair, int) or pair > 0:
                                wait_apart(sp, sum_done, pair, passed["sp"])
                            wait_apart(sp, x2_stored, 16 * (pair + 1), passed["sp"])
                            sp.dma_start(x2_res[:, :, :], scratch["x2"][:, bass.ds(2 * pair, 2), :]).then_inc(x2_res_loaded, 16)
                        if job == "prep_ctx":
                            wait_apart(sp, lo_done["prep_ctx"], pair, passed["sp"])
                            sp.dma_start(ctx_t[:, :, :], t["ctx_t"][:, :, bass.ds(TOK * pair, TOK)]).then_inc(ctx_loaded, 16)
                        if job == "prep_x":
                            wait_apart(sp, lo_done["prep_x"], pair, passed["sp"])
                            sp.dma_start(x_t[:, :, :], t["x_t"][:, :, bass.ds(TOK * pair, TOK)]).then_inc(x_loaded, 16)
                        if job == "logits":
                            wait_apart(sp, sum_done, pair + 1, passed["sp"])
                            sp.dma_start(scratch["x2_x3"][:, bass.ds(2 * pair, 2), :], x2_x3[:, :, :]).then_inc(sum_stored, 16)
                            wait_apart(sp, work_read[BANK["turn_h2"]], bank_read("turn_h2", it), passed["sp"])
                            sp.dma_start(scratch["h2_t"][:, :, bass.ds(TOK * pair, TOK)], h2_t[:, :, :]).then_inc(h2_stored, 16)
                            wait_apart(sp, work_read[BANK["logits"]], bank_read("logits", it), passed["sp"])
                            sp.dma_start(scratch["logit"][:, bass.ds(2 * pair, 2), :], logit[:, :, :]).then_inc(logit_stored, 16)
                        if job == "outx":
                            wait_apart(sp, x2_done, pair + 1, passed["sp"])
                            sp.dma_start(scratch["x2"][:, bass.ds(2 * pair, 2), :], x2[:, :, :]).then_inc(x2_stored, 16)

                for_iterations(sp, iteration)
                for s in (x2_stored, sum_stored, h2_stored, logit_stored):
                    sp.wait_ge(s, 16 * PAIRS)

            @block.tensor
            def _(pe):
                def split_products(out, lhs, rhs, last):
                    (lh, ll), (rh, rl) = lhs, rhs
                    n = 0
                    for a, b in ((lh, rh), (lh, rl), (ll, rh)):
                        for dk in range(DK):
                            n += 1
                            mm = pe.matmul(out, a(dk), b(dk), start=(n == 1), stop=(n == 3 * DK))
                    return mm

                def to_rows(bank, weight, m0, source):
                    for m in range(2):
                        c = (m0 + m) * P
                        mm = split_products(bank[:, m * TOK:(m + 1) * TOK],
                                            [lambda dk, w=w: w[weight][:, dk, c:c + P] for w in (w_hi, w_lo)],
                                            [lambda dk, x=x: x[:, dk, :] for x in parts[source]], m == 1)
                    return mm

                def to_tokens(bank, weight, source):
                    for a in range(2):
                        mm = split_products(bank[:, a * D:(a + 1) * D],
                                            [lambda dk, x=x: x[:, dk, a * S:(a + 1) * S] for x in parts[source]],
                                            [lambda dk, w=w: w[weight][:, dk, :] for w in (w_hi, w_lo)], a == 1)
                    return mm

                def turn(bank, src):
                    for dk in range(DK):
                        for a in range(2):
                            mm = pe.transpose(bank[:, dk * TOK + a * S:dk * TOK + (a + 1) * S],
                                              src[:, a, dk * P:(dk + 1) * P], ident[:, :])
                    return mm

                pe.wait_ge(const_loaded, 16 * CONSTS)
                pe.wait_ge(raw_lo_done, len(split_order))
                pe.wait_ge(ones_set, 1)

                def wait_read(job, it):
                    pe.wait_ge(work_read[BANK[job]], bank_read(job, it))

                def work_job(job, stage, it):
                    pair = it - LAG[stage]
                    b = BANK[job]
                    bank = work[b]
                    uses = bank_uses(job, it)
                    if not isinstance(uses, int) or uses > 0:
                        pe.wait_ge(work_read[b], uses)
                    if job in ("qk1_0", "qk1_1"):
                        a = int(job[4])
                        if a == 0:
                            pe.wait_ge(lo_done["prep_x"], pair + 1)
                        mm = split_products(bank[:, :],
                                            [lambda dk, x=x: x[:, dk, a * S:(a + 1) * S] for x in parts["x"]],
                                            [lambda dk, w=w: w["wqk1"][:, dk, :] for w in (w_hi, w_lo)], True)
                    elif job == "v1":
                        mm = to_tokens(bank, "wv1", "x")
                    elif job in ("q3_0", "q3_1", "k3_0", "k3_1"):
                        if job == "q3_0":
                            wait_read("turn_h", it)
                        mm = to_rows(bank, "w" + job[:2], 2 * int(job[3]), "h")
                    elif job == "v3":
                        mm = to_tokens(bank, "wv3", "h")
                    elif job == "turn_o1":
                        pe.wait_ge(o1_loaded, 16 * (pair + 1))
                        mm = turn(bank, o1_rows)
                    elif job == "out1":
                        wait_read("turn_o1", it)
                        mm = to_tokens(bank, "wo1", "o1")
                    elif job == "turn_x1":
                        pe.wait_ge(x1_done, pair + 1)
                        mm = turn(bank, x1)
                    elif job == "kx":
                        pe.wait_ge(lo_done["prep_ctx"], pair + 1)
                        mm = to_rows(bank, "wkx", 0, "ctx")
                    elif job == "vx":
                        mm = to_tokens(bank, "wvx", "ctx")
                    elif job == "qx":
                        wait_read("turn_x1", it)
                        mm = to_rows(bank, "wqx", 0, "x1")
                    elif job == "sx":
                        wait_read("kx", it)
                        wait_read("qx", it)
                        for a in range(2):
                            for dk in range(DK):
                                mm = pe.matmul(bank[:, a * S:(a + 1) * S], qx_t[:, dk, a * S:(a + 1) * S],
                                               kx_t[:, dk, a * S:(a + 1) * S], start=(dk == 0), stop=(dk == DK - 1))
                    elif job == "turn_px":
                        wait_read("sx", it)
                        for a in range(2):
                            mm = pe.transpose(bank[:, a * S:(a + 1) * S], px[:, a, :], ident[:, :])
                    elif job == "pvx":
                        wait_read("turn_px", it)
                        wait_read("vx", it)
                        for a in range(2):
                            mm = pe.matmul(bank[:, a * D:(a + 1) * D], px_t[:, a, :], vx[:, a, :], start=True, stop=True)
                    elif job == "turn_cx":
                        wait_read("pvx", it)
                        mm = turn(bank, cx)
                    elif job == "outx":
                        wait_read("turn_cx", it)
                        mm = to_tokens(bank, "wox", "cx")
                    elif job == "turn_h":
                        pe.wait_ge(h_done, pair + 1)
                        mm = turn(bank, h_in)
                    elif job == "turn_o3":
                        pe.wait_ge(out_done, 4 * (pair + 1))
                        mm = turn(bank, att_out[3])
                    elif job == "out3":
                        wait_read("turn_o3", it)
                        mm = to_tokens(bank, "wo3", "o3")
                    elif job == "turn_h2":
                        pe.wait_ge(h2_done, pair + 1)
                        mm = turn(bank, h2_in)
                    elif job == "logits":
                        wait_read("turn_h2", it)
                        for a in range(2):
                            for dk in range(DK):
                                mm = pe.matmul(bank[:, a * E:(a + 1) * E], h2_t[:, dk, a * S:(a + 1) * S],
                                               router[:, dk, :], start=(dk == 0), stop=(dk == DK - 1))
                    mm.then_inc(work_ready[b], 1)

                def slot_scores(n, k, it):
                    g = slots_before(it) + k
                    stage, a, half = 3, n // 2, n % 2
                    pe.wait_ge(blocks_done, g + 1)
                    wait_read(f"q{stage}_{half}", it)
                    if not isinstance(g, int) or g > 0:
                        pe.wait_ge(exp_done, g)
                    for j in range(2):
                        for part in range(2):
                            mm = pe.matmul(scores[:, j * HG * S:(j + 1) * HG * S],
                                           q_rows[stage][:, 2 * half + j, a * S:(a + 1) * S],
                                           key_blocks[:, k % 2, part, j, :, :], start=(part == 0), stop=(part == 1))
                    mm.then_inc(scores_done, 1)

                def slot_turn(n, k, it):
                    g = slots_before(it) + k
                    pe.wait_ge(exp_done, g + 1)
                    if not isinstance(g, int) or g > 0:
                        pe.wait_ge(probs_lo_done, g)
                    for h in range(HH):
                        mm = pe.transpose(probs_t[:, h * S:(h + 1) * S], probs[:, k % 2, h, :], ident[:, :])
                    mm.then_inc(turned, 1)

                def slot_values(n, k, it):
                    g = slots_before(it) + k
                    stage, a, half = 3, n // 2, n % 2
                    pe.wait_ge(probs_lo_done, g + 1)
                    pe.wait_ge(v_low_done[stage], it - LAG[stage] + 1)
                    if not isinstance(g, int) or g > 0:
                        pe.wait_ge(out_done, g)
                    for h in range(HH):
                        v = values[stage][:, a * H + half * HH + h, :]
                        pe.matmul(pv[:, h * VP:(h + 1) * VP], probs_hi[:, h, :], v, start=True, stop=False)
                        mm = pe.matmul(pv[:, h * VP:(h + 1) * VP], probs_lo[:, h, :], v, start=False, stop=True)
                    mm.then_inc(pv_done, 1)

                def iteration(it):
                    slots = slots_of(it)
                    open_slots = []
                    for job, stage in jobs_of(it):
                        if job.startswith("slot"):
                            n = int(job[4:])
                            slot_scores(n, slots[n], it)
                            if open_slots:
                                slot_turn(*open_slots[-1])
                            if len(open_slots) > 1:
                                slot_values(*open_slots[-2])
                            open_slots.append((n, slots[n], it))
                        elif job == "flush":
                            slot_values(*open_slots[-2])
                            slot_turn(*open_slots[-1])
                            slot_values(*open_slots[-1])
                        elif not job.startswith(NOT_WORK):
                            work_job(job, stage, it)

                for_iterations(pe, iteration)

            @block.scalar
            def _(act):
                act.wait_ge(const_loaded, 16 * CONSTS)
                act.mul(bias_qx[:, :], bias_qx[:, :], D ** -0.5).then_inc(bias_scaled, 1)
                act.wait_ge(bias_scaled, 1)
                for i, n in enumerate(split_order):
                    b = split_buffer[n]
                    act.wait_ge(raw_loaded[b], 16 * (i // 2 + 1))
                    act.activation(w_hi[n][:, :, :], raw[b][:, :, 0:widths[n]], ACT.Copy,
                                   scale=scales.get(n, 1.0)).then_inc(raw_hi_done, 1)

                def ready(job, it):
                    act.wait_ge(work_ready[BANK[job]], bank_uses(job, it) + 1)

                def split_hi(job, stage, it):
                    src = {"turn_o1": "o1", "turn_x1": "x1", "turn_cx": "cx", "turn_o3": "o3"}[job]
                    ready(job, it)
                    act.activation(parts[src][0][:, :, :], work[BANK[job]][:, :].rearrange("p (d n) -> p d n", d=DK),
                                   ACT.Copy).then_inc(hi_done[job], 1)

                def norm_row(src, name, dst, done, pair):
                    for a in range(2):
                        ins = act.activation(square_out[:, a, :], src[:, a, :], ACT.Square,
                                             accum_out=squares[name][:, a:a + 1])
                    ins.then_inc(stat_done[name], 1)
                    act.wait_ge(rstd_done[name], pair + 1)
                    for a in range(2):
                        ins = act.activation(dst[:, a, :], src[:, a, :], ACT.Copy, scale=rstd[name][:, a:a + 1])
                    ins.then_inc(done, 1)

                def work_job(job, stage, it):
                    pair = it - LAG[stage]
                    bank = work[BANK[job]]
                    if job[:2] in ("q3", "k3"):
                        s, m = int(job[1]), int(job[3])
                        ready(job, it)
                        if job[0] == "q":
                            dst = q_rows[s][:, 2 * m:2 * m + 2, :]
                            act.wait_ge(scores_done, slots_before(it))
                        else:
                            dst = k_parts[s][:, 0, 2 * m:2 * m + 2, :]
                            act.wait_ge(blocks_done, slots_before(it))
                        src = bank[:, :].rearrange("p (g n) -> p g n", g=2)
                        act.activation(dst, src, ACT.Copy).then_inc(hi_done[job], 1)
                    elif job == "v3":
                        act.wait_ge(work_read[BANK[job]], bank_read(job, it))
                        act.wait_ge(pv_done, slots_before(it))
                        act.activation(values[stage][:, :, 0:DH], v_full[:, :, :], ACT.Copy).then_inc(hi_done[job], 1)
                    elif job in ("turn_o1", "turn_x1", "turn_cx", "turn_o3"):
                        split_hi(job, stage, it)
                    elif job == "turn_h":
                        ready(job, it)
                        for dk in range(DK):
                            ins = act.activation(parts["h"][0][:, dk, :], bank[:, dk * TOK:(dk + 1) * TOK], ACT.Copy,
                                                 scale=norm1[:, dk:dk + 1])
                        ins.then_inc(hi_done[job], 1)
                    elif job == "turn_h2":
                        ready(job, it)
                        if not isinstance(pair, int) or pair > 0:
                            act.wait_ge(h2_stored, 16 * pair)
                        for dk in range(DK):
                            ins = act.activation(h2_t[:, dk, :], bank[:, dk * TOK:(dk + 1) * TOK], ACT.Copy,
                                                 scale=norm2[:, dk:dk + 1])
                        ins.then_inc(work_read[BANK[job]], 1)
                    elif job == "kx":
                        ready(job, it)
                        act.activation(kx_t[:, :, :], bank[:, :].rearrange("p (d n) -> p d n", d=DK),
                                       ACT.Copy).then_inc(work_read[BANK[job]], 1)
                    elif job == "qx":
                        ready(job, it)
                        for dk in range(DK):
                            ins = act.activation(qx_t[:, dk, :], bank[:, dk * TOK:(dk + 1) * TOK], ACT.Identity,
                                                 bias=bias_qx[:, dk:dk + 1])
                        ins.then_inc(work_read[BANK[job]], 1)
                    elif job == "sx":
                        act.wait_ge(max_x_done, pair + 1)
                        for a in range(2):
                            ins = act.activation(px[:, a, :], bank[:, a * S:(a + 1) * S], ACT.Exp,
                                                 bias=neg_max_x[:, a:a + 1], accum_out=den_x[:, a:a + 1])
                        ins.then_inc(work_read[BANK[job]], 1)
                    elif job == "turn_px":
                        ready(job, it)
                        act.activation(px_t[:, :, :], bank[:, 0:TOK].rearrange("p (a n) -> p a n", a=2),
                                       ACT.Copy).then_inc(work_read[BANK[job]], 1)
                    elif job == "outx":
                        act.wait_ge(x2_done, pair + 1)
                        norm_row(x2, "h", h_in, h_done, pair)
                    elif job == "out3":
                        act.wait_ge(work_read[BANK[job]], bank_read(job, it))
                        norm_row(x3, "h2", h2_in, h2_done, pair)

                def prep(job, stage, it):
                    pair = it - LAG[stage]
                    name, src, loaded = ("x", x_t, x_loaded) if job == "prep_x" else ("ctx", ctx_t, ctx_loaded)
                    act.wait_ge(loaded, 16 * (pair + 1))
                    user = {"prep_x": "v1", "prep_ctx": "vx"}[job]
                    if not isinstance(pair, int) or pair > 0:
                        act.wait_ge(work_ready[BANK[user]], bank_uses(user, it) + 1)
                    act.activation(parts[name][0][:, :, :], src[:, :, :], ACT.Copy).then_inc(hi_done[job], 1)

                def slot_exp(n, k, it):
                    g = slots_before(it) + k
                    act.wait_ge(max_done, g + 1)
                    if not isinstance(g, int) or g > 1:
                        act.wait_ge(turned, g - 1)
                    for h in range(HH):
                        ins = act.activation(probs[:, k % 2, h, :], scores[:, h * S:(h + 1) * S], ACT.Exp,
                                             bias=neg_max[:, k % 2, h:h + 1])
                    ins.then_inc(exp_done, 1)

                def slot_hi(n, k, it):
                    g = slots_before(it) + k
                    act.wait_ge(turned, g + 1)
                    if not isinstance(g, int) or g > 0:
                        act.wait_ge(pv_done, g)
                    act.activation(probs_hi[:, :, :], probs_t[:, :].rearrange("p (h n) -> p h n", h=HH),
                                   ACT.Copy).then_inc(probs_hi_done, 1)

                def iteration(it):
                    slots = slots_of(it)
                    open_slots = []
                    for job, stage in jobs_of(it):
                        if job.startswith("slot"):
                            n = int(job[4:])
                            slot_exp(n, slots[n], it)
                            if open_slots:
                                slot_hi(*open_slots[-1])
                            open_slots.append((n, slots[n], it))
                        elif job == "flush":
                            slot_hi(*open_slots[-1])
                        elif job.startswith("prep"):
                            prep(job, stage, it)
                        elif job.startswith("heads"):
                            n, u = int(job[5]), 4 * (it - LAG[1]) + int(job[5])
                            act.wait_ge(head_shifted, u + 1)
                            act.activation(head_probs[:, n % 2, :, :], head_scores[:, n % 2, :, :], ACT.Exp,
                                           scale=DH ** -0.5).then_inc(head_exp_done, 1)
                        elif job != "last_heads":
                            work_job(job, stage, it)

                for_iterations(act, iteration)

            @block.vector
            def _(dve):
                own = Own(dve, dve_own, DVE_OWN)
                for i, n in enumerate(split_order):
                    b = split_buffer[n]
                    dve.wait_ge(raw_hi_done, i + 1)
                    dve.scalar_tensor_tensor(out=w_lo[n][:, :, :], in0=raw[b][:, :, 0:widths[n]],
                                             scalar=scales.get(n, 1.0), in1=w_hi[n][:, :, :].bitcast(F32),
                                             op0=ALU.mult, op1=ALU.subtract).then_inc(raw_lo_done, 1)
                for s in (3,):
                    dve.memset(values[s][:, :, VP - 1:VP], 1.0).then_inc(ones_set, 1)

                def both(bank, n=D):
                    return bank[:, :].rearrange("p (a n) -> p a n", a=2)

                def layer_norm(src, name, mv, dst, done, stage, pair):
                    for a in range(2):
                        ins = dve.bn_stats(stats[:, a, :], src[:, a, :])
                    own.done(stage, ins, passed["dve"])
                    for a in range(2):
                        ins = dve.bn_aggr(mv[:, a, :], stats[:, a, :])
                    ins.then_inc(stat_done[name], 1)
                    dve.wait_ge(rstd_done[name], pair + 1)
                    for a in range(2):
                        ins = dve.tensor_scalar(dst[:, a, :], src[:, a, :], mv[:, a, 0:1], rstd[name][:, a:a + 1],
                                                ALU.subtract, ALU.mult)
                    ins.then_inc(done, 1)

                def ready(job, it):
                    dve.wait_ge(work_ready[BANK[job]], bank_uses(job, it) + 1)

                def work_job(job, stage, it):
                    pair = it - LAG[stage]
                    b = BANK[job]
                    bank = work[b]
                    if job[:2] in ("q3", "k3"):
                        s, m = int(job[1]), int(job[3])
                        dve.wait_ge(hi_done[job], pair + 1)
                        src = bank[:, :].rearrange("p (g n) -> p g n", g=2)
                        rows = slice(P // 2, P) if job[0] == "q" else slice(0, P)
                        hi = (q_rows[s] if job[0] == "q" else k_parts[s][:, 0])[rows, 2 * m:2 * m + 2, :]
                        lo = hi if job[0] == "q" else k_parts[s][:, 1, 2 * m:2 * m + 2, :]
                        dve.tensor_tensor(lo, src[rows], hi.bitcast(F32), ALU.subtract).then_inc(work_read[b], 1)
                    elif job in ("qk1_0", "qk1_1"):
                        ready(job, it)
                        dve.tensor_tensor(qk1[:, int(job[4]), :], bank[:, :], bias_qk1[:, :], ALU.add)\
                           .then_inc(work_read[b], 1)
                    elif job == "v1":
                        ready(job, it)
                        dve.tensor_tensor(v1[:, :, :], both(bank), bias_v1[:, :].unsqueeze(1).to_broadcast([P, 2, D]),
                                          ALU.add).then_inc(work_read[b], 1)
                    elif job == "v3":
                        ready(job, it)
                        src = both(bank)
                        dst = v_full[:, :, :].rearrange("p (a h) d -> p a (h d)", a=2)
                        dve.tensor_copy(dst, src).then_inc(work_read[b], 1)
                        dve.wait_ge(hi_done[job], pair + 1)
                        dve.tensor_tensor(v_rest[:, :, :], v_full[:, :, :], values[stage][:, :, 0:DH],
                                          ALU.subtract).then_inc(v_rest_done[stage], 1)
                        dve.wait_ge(v_mid_done[stage], pair + 1)
                        dve.tensor_tensor(values[stage][:, :, 2 * DH:3 * DH], v_rest[:, :, :],
                                          values[stage][:, :, DH:2 * DH], ALU.subtract).then_inc(v_low_done[stage], 1)
                    elif job in ("turn_o1", "turn_x1", "turn_cx", "turn_o3"):
                        src = {"turn_o1": "o1", "turn_x1": "x1", "turn_cx": "cx", "turn_o3": "o3"}[job]
                        dve.wait_ge(hi_done[job], pair + 1)
                        hi, lo = parts[src]
                        dve.tensor_tensor(lo[:, :, :], bank[:, :].rearrange("p (d n) -> p d n", d=DK),
                                          hi[:, :, :].bitcast(F32), ALU.subtract).then_inc(work_read[b], 1)
                    elif job == "turn_h":
                        dve.wait_ge(hi_done[job], pair + 1)
                        hi, lo = parts["h"]
                        for dk in range(DK):
                            ins = dve.scalar_tensor_tensor(out=lo[:, dk, :], in0=bank[:, dk * TOK:(dk + 1) * TOK],
                                                           scalar=norm1[:, dk:dk + 1], in1=hi[:, dk, :].bitcast(F32),
                                                           op0=ALU.mult, op1=ALU.subtract)
                        ins.then_inc(work_read[b], 1)
                    elif job == "out1":
                        ready(job, it)
                        dve.wait_ge(x_res_loaded, 16 * (pair + 1))
                        dve.tensor_tensor(y1[:, :, :], both(bank), x_res[:, :, :], ALU.add).then_inc(work_read[b], 1)
                        dve.wait_ge(work_read[b], bank_read(job, it))
                        own.done(stage, dve.tensor_tensor(y1[:, :, :], y1[:, :, :],
                                                          bias_o1[:, :].unsqueeze(1).to_broadcast([P, 2, D]), ALU.add))
                        layer_norm(y1, "y1", mean_var[1], x1, x1_done, stage, pair)
                    elif job == "outx":
                        ready(job, it)
                        dve.tensor_tensor(z2[:, :, :], both(bank), x1[:, :, :], ALU.add).then_inc(work_read[b], 1)
                        dve.wait_ge(work_read[b], bank_read(job, it))
                        own.done(stage, dve.tensor_tensor(z2[:, :, :], z2[:, :, :],
                                                          bias_ox[:, :].unsqueeze(1).to_broadcast([P, 2, D]), ALU.add))
                        if not isinstance(pair, int) or pair > 0:
                            dve.wait_ge(x2_stored, 16 * pair)
                        layer_norm(z2, "z2", mean_var[2], x2, x2_done, stage, pair)
                    elif job == "out3":
                        ready(job, it)
                        dve.wait_ge(x2_res_loaded, 16 * (pair + 1))
                        dve.tensor_tensor(x3[:, :, :], both(bank), x2_res[:, :, :], ALU.add).then_inc(work_read[b], 1)
                        if not isinstance(pair, int) or pair > 0:
                            dve.wait_ge(sum_stored, 16 * pair)
                        dve.wait_ge(work_read[b], bank_read(job, it))
                        dve.tensor_tensor(x2_x3[:, :, :], x3[:, :, :], x2_res[:, :, :], ALU.add).then_inc(sum_done, 1)
                    elif job == "vx":
                        ready(job, it)
                        dve.tensor_tensor(vx[:, :, :], both(bank), bias_vx[:, :].unsqueeze(1).to_broadcast([P, 2, D]),
                                          ALU.add).then_inc(work_read[b], 1)
                    elif job == "sx":
                        ready(job, it)
                        dve.tensor_reduce(neg_max_x[:, :], bank[:, 0:TOK].rearrange("p (a n) -> p a n", a=2), AX.X, ALU.max,
                                          negate=True).then_inc(max_x_done, 1)
                        dve.wait_ge(work_read[b], bank_read(job, it))
                        dve.reciprocal(rden_x[:, :], den_x[:, :]).then_inc(rden_x_done, 1)
                    elif job == "pvx":
                        ready(job, it)
                        dve.wait_ge(rden_x_done, pair + 1)
                        for a in range(2):
                            ins = dve.tensor_scalar(cx[:, a, :], bank[:, a * D:(a + 1) * D], rden_x[:, a:a + 1], None, ALU.mult)
                        ins.then_inc(work_read[b], 1)
                    elif job == "logits":
                        ready(job, it)
                        if not isinstance(pair, int) or pair > 0:
                            dve.wait_ge(logit_stored, 16 * pair)
                        dve.tensor_copy(logit[:, :, :], bank[:, 0:2 * E].rearrange("p (a n) -> p a n", a=2))\
                           .then_inc(work_read[b], 1)

                def prep(job, stage, it):
                    pair = it - LAG[stage]
                    name, src = ("x", x_t) if job == "prep_x" else ("ctx", ctx_t)
                    dve.wait_ge(hi_done[job], pair + 1)
                    hi, lo = parts[name]
                    dve.tensor_tensor(lo[:, :, :], src[:, :, :], hi[:, :, :].bitcast(F32), ALU.subtract)\
                       .then_inc(lo_done[job], 1)

                def slot_max(n, k, it):
                    g = slots_before(it) + k
                    dve.wait_ge(scores_done, g + 1)
                    dve.tensor_reduce(neg_max[:, k % 2, :], scores[:, :].rearrange("p (h n) -> p h n", h=HH), AX.X,
                                      ALU.max, negate=True).then_inc(max_done, 1)

                def slot_lo(n, k, it):
                    g = slots_before(it) + k
                    dve.wait_ge(probs_hi_done, g + 1)
                    dve.tensor_tensor(probs_lo[:, :, :], probs_t[:, :].rearrange("p (h n) -> p h n", h=HH),
                                      probs_hi[:, :, :], ALU.subtract).then_inc(probs_lo_done, 1)

                def slot_out(n, k, it):
                    g = slots_before(it) + k
                    stage, a, half = 3, n // 2, n % 2
                    dve.wait_ge(pv_done, g + 1)
                    src = pv[:, 0:HH * VP].rearrange("p (h c) -> p h c", h=HH)
                    dve.reciprocal(rden[:, :].unsqueeze(2), src[:, :, VP - 1:VP])
                    own.done(stage, dve.tensor_reduce(
                        osum[:, :, :], src[:, :, 0:3 * DH].rearrange("p h (c d) -> p h d c", c=3), AX.X, ALU.add))
                    dve.tensor_tensor(att_out[stage][:, a, half * P:(half + 1) * P].rearrange("p (h d) -> p h d", h=HH),
                                      osum[:, :, :], rden[:, :].unsqueeze(2).to_broadcast([P, HH, DH]),
                                      ALU.mult).then_inc(out_done, 1)

                def head_shift(n, it):
                    u = 4 * (it - LAG[1]) + n
                    s = head_scores[:, n % 2, :, :]
                    dve.wait_ge(qk_prod_done, u + 1)
                    dve.tensor_reduce(s, qk_prod[:, :, :, :], AX.X, ALU.add).then_inc(head_scores_done, 1)
                    dve.wait_ge(head_scores_done, u + 1)
                    dve.tensor_reduce(head_max[:, :], s, AX.X, ALU.max).then_inc(head_max_done, 1)
                    dve.wait_ge(head_max_done, u + 1)
                    dve.tensor_tensor(s, s, head_max[:, :].unsqueeze(2).to_broadcast([P, HH, H]),
                                      ALU.subtract).then_inc(head_shifted, 1)

                def head_output(n, it):
                    u = 4 * (it - LAG[1]) + n
                    a, half = n // 2, n % 2
                    if not isinstance(u, int) or u > 0:
                        wait_apart(dve, head_out_done, u, passed["dve"])
                    dve.wait_ge(head_exp_done, u + 1)
                    dve.tensor_reduce(head_den[:, :], head_probs[:, n % 2, :, :], AX.X, ALU.add).then_inc(head_den_done, 1)
                    dve.wait_ge(head_den_done, 2 * u + 1)
                    dve.reciprocal(head_den[:, :], head_den[:, :]).then_inc(head_den_done, 1)
                    dve.wait_ge(pv_prod_done, u + 1)
                    dve.tensor_reduce(head_sum[:, :, :], pv_prod[:, :, :, :], AX.X, ALU.add).then_inc(head_sum_done, 1)
                    if n == 0 and not (isinstance(u, int) and u == 0):
                        dve.wait_ge(o1_stored, 8 * u)
                    dve.wait_ge(head_den_done, 2 * u + 2)
                    dve.wait_ge(head_sum_done, u + 1)
                    dve.tensor_tensor(att_out[1][:, a, half * P:(half + 1) * P].rearrange("p (h d) -> p h d", h=HH),
                                      head_sum[:, :, :], head_den[:, :].unsqueeze(2).to_broadcast([P, HH, DH]),
                                      ALU.mult).then_inc(head_out_done, 1)

                def iteration(it):
                    own.begin(it)
                    slots = slots_of(it)
                    open_slots = []
                    for job, stage in jobs_of(it):
                        if job.startswith("slot"):
                            n = int(job[4:])
                            if len(open_slots) > 1:
                                slot_lo(*open_slots[-2])
                            slot_max(n, slots[n], it)
                            if len(open_slots) > 1:
                                slot_out(*open_slots[-2])
                            open_slots.append((n, slots[n], it))
                        elif job == "flush":
                            slot_lo(*open_slots[-2])
                            slot_out(*open_slots[-2])
                            slot_lo(*open_slots[-1])
                            slot_out(*open_slots[-1])
                        elif job.startswith("prep"):
                            prep(job, stage, it)
                        elif job.startswith("heads"):
                            n = int(job[5])
                            head_shift(n, it)
                            if n > 0:
                                head_output(n - 1, it)
                        elif job == "last_heads":
                            head_output(3, it)
                        else:
                            work_job(job, stage, it)
                    own.end(it)

                for_iterations(dve, iteration)

            @block.gpsimd
            def _(pool):
                pool.memset(half_power[:, :], -0.5).then_inc(pool_own, 1)
                pool.wait_ge(const_loaded, 16 * CONSTS)
                pool.wait_ge(pool_own, 1)
                roots = [0]

                def root(name, src, scale, eps, pair, stage, it, order):
                    wait_apart(pool, stat_done[name], pair + 1, passed["pool"])
                    pool.tensor_scalar(var_eps[:, :], src, scale, eps, ALU.mult, ALU.add).then_inc(pool_own, 1)
                    pool.wait_ge(pool_own, order)
                    pool.tensor_tensor(rstd[name][:, :], var_eps[:, :], half_power[:, :], ALU.pow)\
                        .then_inc(rstd_done[name], 1)

                def roots_before(name, it):
                    per = [("y1", 2), ("h2", 4), ("z2", 2), ("h", 2)]
                    n = 2
                    seen = False
                    for other, s in per:
                        if other == name:
                            seen = True
                        n = n + pairs_done(s, it)
                        if not seen and active(s, it):
                            n = n + 1
                    return n

                def mask_slot(n, k, it):
                    g = slots_before(it) + k
                    stage, a, half = 3, n // 2, n % 2
                    job = f"k{stage}_{half}"
                    wait_apart(pool, work_read[BANK[job]], bank_read(job, it), passed["pool"])
                    if not isinstance(g, int) or g > 1:
                        wait_apart(pool, scores_done, g - 1, passed["pool"])
                    for j in range(HG):
                        for part in range(2):
                            ins = pool.tensor_scalar(
                                key_blocks[:, k % 2, part, :, j, :],
                                k_parts[stage][:, part, 2 * half:2 * half + 2, a * S:(a + 1) * S].bitcast(F32),
                                head_mask[:, j:j + 1], 1.0, ALU.mult, ALU.mult)
                    ins.then_inc(blocks_done, 1)

                def middle(stage, it):
                    pair = it - LAG[stage]
                    wait_apart(pool, v_rest_done[stage], pair + 1, passed["pool"])
                    pool.tensor_copy(values[stage][:, :, DH:2 * DH], v_rest[:, :, :]).then_inc(v_mid_done[stage], 1)

                def qk_products(n, it):
                    u = 4 * (it - LAG[1]) + n
                    a, half = n // 2, n % 2
                    job = f"qk1_{a}"
                    wait_apart(pool, work_read[BANK[job]], bank_read(job, it), passed["pool"])
                    if not isinstance(u, int) or u > 0:
                        wait_apart(pool, head_scores_done, u, passed["pool"])
                    q = qk1[:, a, half * P:(half + 1) * P].rearrange("p (h d) -> p h d", h=HH)
                    k = qk1[:, a, D:2 * D].rearrange("p (h d) -> p h d", h=H)
                    pool.tensor_tensor(qk_prod[:, :, :, :], q.unsqueeze(2).to_broadcast([P, HH, H, DH]),
                                       k.unsqueeze(1).to_broadcast([P, HH, H, DH]), ALU.mult).then_inc(qk_prod_done, 1)

                def pv_products(n, it):
                    u = 4 * (it - LAG[1]) + n
                    a = n // 2
                    wait_apart(pool, work_read[BANK["v1"]], bank_read("v1", it), passed["pool"])
                    wait_apart(pool, head_exp_done, u + 1, passed["pool"])
                    if not isinstance(u, int) or u > 0:
                        wait_apart(pool, head_sum_done, u, passed["pool"])
                    v = v1[:, a, :].rearrange("p (h d) -> p d h", h=H)
                    pool.tensor_tensor(pv_prod[:, :, :, :], head_probs[:, n % 2, :, :].unsqueeze(2).to_broadcast([P, HH, DH, H]),
                                       v.unsqueeze(1).to_broadcast([P, HH, DH, H]), ALU.mult).then_inc(pv_prod_done, 1)

                def iteration(it):
                    slots = slots_of(it)
                    ahead = {"k3_0": [0], "k3_1": [1], "slot1": [2], "slot2": [3]}
                    for job, stage in jobs_of(it):
                        pair = it - LAG[stage]
                        for n in ahead.get(job, ()):
                            mask_slot(n, slots[n], it)
                        if job == "out1":
                            root("y1", mean_var[1][:, :, 1], 1.0, 1e-5, pair, stage, it, roots_before("y1", it))
                        elif job == "out3":
                            root("h2", squares["h2"][:, :], 1.0 / D, 1e-6, pair, stage, it, roots_before("h2", it))
                        elif job == "outx":
                            root("z2", mean_var[2][:, :, 1], 1.0, 1e-5, pair, stage, it, roots_before("z2", it))
                            root("h", squares["h"][:, :], 1.0 / D, 1e-6, pair, stage, it, roots_before("h", it))
                        elif job == "v3":
                            middle(stage, it)
                        elif job.startswith("heads"):
                            n = int(job[5])
                            qk_products(n, it)
                            if n > 0:
                                pv_products(n - 1, it)
                        elif job == "last_heads":
                            pv_products(3, it)

                for_iterations(pool, iteration)


def phase_b(nc, t, scratch, sem, out):
    ctx = ExitStack()
    NT = B
    TG = GT // P

    def sb(name, shape, dt=F32):
        return ctx.enter_context(nc.sbuf_tensor(name, shape, dt))

    with ctx:
        tok_hi = sb("tok_hi", [P, DK, B * S], F32R)
        tok_lo = sb("tok_lo", [P, DK, B * S], F32R)
        acc = sb("acc", [P, NT, D])
        WC = DK * DFF
        w_raw = sb("w_raw", [P, 3, WC])
        w_hi = sb("we_hi", [P, 2, 3, WC], F32R)
        w_lo = sb("we_lo", [P, 2, 3, WC], F32R)
        silu = sb("silu", [P, 2, GT])
        prod = sb("prod", [P, 2, GT])
        act_hi = sb("act_hi", [P, 2, FT, GT], F32R)
        act_lo = sb("act_lo", [P, 2, FT, GT], F32R)
        h_raw = [x[:, :, :] for x in (silu, prod)]
        combine = sb("combine", [P, NT, NE])
        logit = sb("logit_all", [P, NT, E])
        iota = sb("iota", [P, NT, E])
        pr = sb("pr", [P, NT, E])
        eq = sb("eq", [P, NT, E])
        one_hot = [sb(f"one_hot{i}", [P, NT, E]) for i in range(2)]
        rows = {n: sb(f"row_{n}", [P, NT]) for n in ("max", "sum", "top1", "top2", "at", "ratio", "den", "w1", "w2")}
        stats = sb("stats_b", [P, NT, 6])
        mean_var = sb("mean_var_b", [P, NT, 2])
        var_eps = sb("var_eps_b", [P, NT])
        rstd = sb("rstd_b", [P, NT])
        half_power = sb("half_power_b", [P, NT])

        gate = [ctx.enter_context(nc.psum_tensor(f"gate{i}", [P, GT], F32)) for i in range(2)]
        up = [ctx.enter_context(nc.psum_tensor(f"up{i}", [P, GT], F32)) for i in range(2)]
        down = [ctx.enter_context(nc.psum_tensor(f"down{i}", [P, 512], F32)) for i in range(4)]

        loaded, w_loaded = sem("b_loaded"), sem("w_loaded")
        h_loaded = [sem(f"h_loaded{i}") for i in range(2)]
        h_hi_done, h_lo_done = sem("h_hi_done"), sem("h_lo_done")
        w_hi_done, w_lo_done = sem("w_hi_done"), sem("w_lo_done")
        gate_up_ready, silu_done, prod_done = sem("gate_up_ready"), sem("silu_done"), sem("prod_done")
        act_hi_done, act_lo_done = sem("act_hi_done"), sem("act_lo_done")
        down_ready, down_added = sem("down_ready"), sem("down_added")
        passed_sp = sem("passed_sp_b")
        route, route_max, route_exp, ratio_ready, ratio_exp = (
            sem(n) for n in ("route", "route_max", "route_exp", "ratio_ready", "ratio_exp"))
        pool_own_b, var_done, rstd_b_done, norm_done, out_stored = (
            sem(n) for n in ("pool_own_b", "var_done", "rstd_b_done", "norm_done", "out_stored"))

        def experts(engine, body):
            body(0, 1, True, True)
            with engine.Fori(0, E // 2 - 1) as i:
                body(2 * i + 1, 0, False, True)
                body(2 * i + 2, 1, False, True)
            body(E - 1, 0, False, True)
            body(E, 1, False, False)

        with nc.Block() as block:

            @block.sync
            def _(sp):
                sp.dma_start(logit[:, :, :], scratch["logit"]).then_inc(loaded, 16)
                sp.dma_start(iota[:, :, :], t["iota"]).then_inc(loaded, 16)
                for k, n in enumerate(("w_gate", "w_up", "w_down")):
                    sp.dma_start(w_raw[:, k, :], t[n][0, :, :]).then_inc(w_loaded, 16)
                for g in range(NGT):
                    if g >= 2:
                        sp.wait_ge(h_lo_done, g - 1)
                    sp.dma_start(h_raw[g % 2], scratch["h2_t"][:, :, g * GT:(g + 1) * GT]).then_inc(h_loaded[g % 2], 16)
                    if g == 0:
                        sp.dma_start(acc[:, :, :], scratch["x2_x3"]).then_inc(loaded, 16)

                def expert(x, par, first, more):
                    if more:
                        wait_apart(sp, w_lo_done, 3 * (x + 1), passed_sp)
                        for k, n in enumerate(("w_gate", "w_up", "w_down")):
                            src = t[n][x + 1, :, :] if isinstance(x, int) else t[n][bass.ds(x + 1, 1), :, :].rearrange("a p n -> (a p) n")
                            sp.dma_start(w_raw[:, k, :], src).then_inc(w_loaded, 16)

                experts(sp, expert)
                for n in range(NGT):
                    sp.wait_ge(norm_done, n + 1)
                    sp.dma_start(out[:, n * TG:(n + 1) * TG, :], acc[:, n * TG:(n + 1) * TG, :]).then_inc(out_stored, 16)
                sp.wait_ge(out_stored, 16 * NGT)

            @block.tensor
            def _(pe):
                def piece(w, par, kind, i, c, n):
                    width = DFF if kind < 2 else D
                    return w[:, par, kind, i * width + c:i * width + c + n]

                def gate_up(x, par, g, f):
                    k = (x * NGT + g) * FT + f
                    if not isinstance(k, int) or k > 1:
                        pe.wait_ge(prod_done, k - 1)
                    for kind, bank in ((0, gate[f % 2]), (1, up[f % 2])):
                        n = 0
                        for wp, hp in ((w_hi, tok_hi), (w_hi, tok_lo), (w_lo, tok_hi)):
                            for dk in range(DK):
                                n += 1
                                mm = pe.matmul(bank[:, :], piece(wp, par, kind, dk, f * P, P),
                                               hp[:, dk, g * GT:(g + 1) * GT], start=(n == 1), stop=(n == 3 * DK))
                    mm.then_inc(gate_up_ready, 1)

                def down_tile(x, par, g, j):
                    step = x * NGT + g
                    if j == 0:
                        pe.wait_ge(act_lo_done, FT * (step + 1))
                    if not isinstance(step, int) or step > 0:
                        pe.wait_ge(down_added, FT * (step - 1) + j + 1)
                    n = 0
                    for ap, wp in ((act_hi, w_hi), (act_hi, w_lo), (act_lo, w_hi)):
                        for f in range(FT):
                            n += 1
                            mm = pe.matmul(down[j][:, 0:D], ap[:, g % 2, f, j * P:(j + 1) * P],
                                           piece(wp, par, 2, f, 0, D), start=(n == 1), stop=(n == 3 * FT))
                    mm.then_inc(down_ready, 1)

                def expert(x, par, first, more):
                    pe.wait_ge(w_lo_done, 3 * (x + 1))
                    for g in range(NGT):
                        if first:
                            pe.wait_ge(h_lo_done, g + 1)
                        last = None if first and g == 0 else (x, par, g - 1) if g else (x - 1, 1 - par, NGT - 1)
                        for f in range(FT):
                            gate_up(x, par, g, f)
                            if last:
                                for j in ((), (0,), (1,), (2, 3))[f]:
                                    down_tile(*last, j)

                experts(pe, expert)
                for j in range(TG):
                    down_tile(E, 1, NGT - 1, j)

            @block.scalar
            def _(act):
                def split_weights(x, par, k):
                    act.wait_ge(w_loaded, 48 * (x + 1))
                    act.activation(w_hi[:, par, k, :], w_raw[:, k, :], ACT.Copy).then_inc(w_hi_done, 1)

                for k in range(3):
                    split_weights(0, 1, k)
                for g in range(NGT):
                    act.wait_ge(h_loaded[g % 2], 16 * (g // 2 + 1))
                    act.activation(tok_hi[:, :, g * GT:(g + 1) * GT], h_raw[g % 2], ACT.Copy).then_inc(h_hi_done, 1)
                act.wait_ge(route_max, 1)
                act.activation(pr[:, :, :], logit[:, :, :], ACT.Exp).then_inc(route_exp, 1)
                act.wait_ge(ratio_ready, 1)
                act.activation(rows["ratio"][:, :], rows["ratio"][:, :], ACT.Exp).then_inc(ratio_exp, 1)
                act.wait_ge(h_lo_done, NGT)

                def expert(x, par, first, more):
                    for g in range(NGT):
                        step = x * NGT + g
                        for f in range(FT):
                            k = step * FT + f
                            act.wait_ge(gate_up_ready, k + 1)
                            act.activation(silu[:, f % 2, :], gate[f % 2][:, :], ACT.Silu).then_inc(silu_done, 1)
                            act.wait_ge(prod_done, k + 1)
                            if f == 0 and not (isinstance(step, int) and step < 2):
                                act.wait_ge(down_ready, TG * (step - 1))
                            act.activation(act_hi[:, g % 2, f, :], prod[:, f % 2, :], ACT.Copy).then_inc(act_hi_done, 1)
                        if more and 1 <= g <= 3:
                            if g == 1 and not (isinstance(x, int) and x == 0):
                                act.wait_ge(down_ready, TG * x * NGT)
                            split_weights(x + 1, 1 - par, g - 1)

                experts(act, expert)

            @block.vector
            def _(dve):
                own = [0]

                def step_of_route(instruction):
                    own[0] += 1
                    instruction.then_inc(route, 1)
                    dve.wait_ge(route, own[0])

                def low_weights(x, par, k):
                    dve.wait_ge(w_hi_done, 3 * x + k + 1)
                    dve.tensor_tensor(w_lo[:, par, k, :], w_raw[:, k, :], w_hi[:, par, k, :].bitcast(F32),
                                      ALU.subtract).then_inc(w_lo_done, 1)

                for k in range(3):
                    low_weights(0, 1, k)
                for g in range(NGT):
                    dve.wait_ge(h_hi_done, g + 1)
                    cols = slice(g * GT, (g + 1) * GT)
                    dve.tensor_tensor(tok_lo[:, :, cols], h_raw[g % 2], tok_hi[:, :, cols].bitcast(F32),
                                      ALU.subtract).then_inc(h_lo_done, 1)

                def wide(x):
                    return x[:, :].unsqueeze(2).to_broadcast([P, NT, E])

                dve.wait_ge(loaded, 48)
                step_of_route(dve.tensor_reduce(rows["max"][:, :], logit[:, :, :], AX.X, ALU.max))
                dve.tensor_tensor(logit[:, :, :], logit[:, :, :], wide(rows["max"]), ALU.subtract).then_inc(route_max, 1)
                dve.wait_ge(route_exp, 1)
                step_of_route(dve.tensor_reduce(rows["sum"][:, :], pr[:, :, :], AX.X, ALU.add))
                step_of_route(dve.reciprocal(rows["sum"][:, :], rows["sum"][:, :]))
                step_of_route(dve.tensor_tensor(pr[:, :, :], pr[:, :, :], wide(rows["sum"]), ALU.mult))
                for n, top in enumerate(("top1", "top2")):
                    step_of_route(dve.tensor_reduce(rows[top][:, :], pr[:, :, :], AX.X, ALU.max))
                    step_of_route(dve.tensor_tensor(eq[:, :, :], pr[:, :, :], wide(rows[top]), ALU.is_equal))
                    step_of_route(dve.scalar_tensor_tensor(out=eq[:, :, :], in0=eq[:, :, :], scalar=-float(E),
                                                           in1=iota[:, :, :], op0=ALU.mult, op1=ALU.add))
                    step_of_route(dve.tensor_reduce(rows["at"][:, :], eq[:, :, :], AX.X, ALU.min))
                    step_of_route(dve.tensor_tensor(one_hot[n][:, :, :], eq[:, :, :], wide(rows["at"]), ALU.is_equal))
                    if n == 0:
                        step_of_route(dve.scalar_tensor_tensor(out=pr[:, :, :], in0=one_hot[0][:, :, :], scalar=-2.0,
                                                               in1=pr[:, :, :], op0=ALU.mult, op1=ALU.add))
                dve.tensor_tensor(rows["ratio"][:, :], rows["top2"][:, :], rows["top1"][:, :], ALU.subtract)\
                   .then_inc(ratio_ready, 1)
                dve.wait_ge(ratio_exp, 1)
                step_of_route(dve.tensor_scalar(rows["den"][:, :], rows["ratio"][:, :], 1.0, None, ALU.add))
                step_of_route(dve.reciprocal(rows["w1"][:, :], rows["den"][:, :]))
                step_of_route(dve.tensor_tensor(rows["w2"][:, :], rows["ratio"][:, :], rows["w1"][:, :], ALU.mult))
                step_of_route(dve.tensor_tensor(one_hot[0][:, :, :], one_hot[0][:, :, :], wide(rows["w1"]), ALU.mult))
                step_of_route(dve.tensor_tensor(one_hot[1][:, :, :], one_hot[1][:, :, :], wide(rows["w2"]), ALU.mult))
                dve.memset(combine[:, :, 0:1], 1.0)
                step_of_route(dve.tensor_tensor(combine[:, :, 1:NE], one_hot[0][:, :, :], one_hot[1][:, :, :], ALU.add))

                def product(x, g, f):
                    k = (x * NGT + g) * FT + f
                    dve.wait_ge(silu_done, k + 1)
                    if not isinstance(k, int) or k > 1:
                        dve.wait_ge(act_lo_done, k - 1)
                    dve.tensor_tensor(prod[:, f % 2, :], silu[:, f % 2, :], up[f % 2][:, :], ALU.mult)\
                       .then_inc(prod_done, 1)

                def add_tile(x, g, j):
                    step = x * NGT + g
                    n = g * TG + j
                    dve.wait_ge(down_ready, TG * step + j + 1)
                    weight = combine[:, n, x:x + 1] if isinstance(x, int) else combine[:, n, bass.ds(x, 1)]
                    dve.scalar_tensor_tensor(out=acc[:, n, :], in0=down[j][:, 0:D], scalar=weight, in1=acc[:, n, :],
                                             op0=ALU.mult, op1=ALU.add).then_inc(down_added, 1)

                def expert(x, par, first, more):
                    for g in range(NGT):
                        last = None if first and g == 0 else (x, g - 1) if g else (x - 1, NGT - 1)
                        for f in range(FT):
                            product(x, g, f)
                            if last:
                                for j in ((), (0,), (1,), (2, 3))[f]:
                                    add_tile(*last, j)
                        if more and 1 <= g <= 3:
                            low_weights(x + 1, 1 - par, g - 1)

                experts(dve, expert)
                for j in range(TG):
                    add_tile(E, NGT - 1, j)
                dve.wait_ge(down_added, TG * NGT * NE)
                for n in range(NT):
                    ins = dve.bn_stats(stats[:, n, :], acc[:, n, :])
                step_of_route(ins)
                for n in range(NT):
                    ins = dve.bn_aggr(mean_var[:, n, :], stats[:, n, :])
                ins.then_inc(var_done, 1)
                dve.wait_ge(rstd_b_done, 1)
                for n in range(NT):
                    ins = dve.tensor_scalar(acc[:, n, :], acc[:, n, :], mean_var[:, n, 0:1], rstd[:, n:n + 1],
                                            ALU.subtract, ALU.mult)
                    if n % TG == TG - 1:
                        ins.then_inc(norm_done, 1)

            @block.gpsimd
            def _(pool):
                pool.memset(half_power[:, :], -0.5).then_inc(pool_own_b, 1)

                def expert(x, par, first, more):
                    for g in range(NGT):
                        for f in range(FT):
                            k = (x * NGT + g) * FT + f
                            pool.wait_ge(act_hi_done, k + 1)
                            pool.tensor_tensor(act_lo[:, g % 2, f, :], prod[:, f % 2, :],
                                               act_hi[:, g % 2, f, :].bitcast(F32), ALU.subtract).then_inc(act_lo_done, 1)

                experts(pool, expert)
                pool.wait_ge(var_done, 1)
                pool.tensor_scalar(var_eps[:, :], mean_var[:, :, 1], 1.0, 1e-5, ALU.mult, ALU.add).then_inc(pool_own_b, 1)
                pool.wait_ge(pool_own_b, 2)
                pool.tensor_tensor(rstd[:, :], var_eps[:, :], half_power[:, :], ALU.pow).then_inc(rstd_b_done, 1)


def decoder(nc, t, out):
    scratch = {
        "o1": nc.dram_tensor("o1_scratch", (B, S * D), F32, kind="Internal").ap(),
        "x2": nc.dram_tensor("x2_scratch", (P, B, D), F32, kind="Internal").ap(),
        "x2_x3": nc.dram_tensor("x2_x3_scratch", (P, B, D), F32, kind="Internal").ap(),
        "h2_t": nc.dram_tensor("h2_scratch", (P, DK, B * S), F32, kind="Internal").ap(),
        "logit": nc.dram_tensor("logit_scratch", (P, B, E), F32, kind="Internal").ap(),
    }
    with ExitStack() as ctx:
        def sem(name):
            return ctx.enter_context(nc.semaphore(name))

        phase_a(nc, t, scratch, sem)
        phase_b(nc, t, scratch, sem, out)


def layout(inputs):
    import numpy as np

    def a(name):
        return np.asarray(inputs[name])

    def rows(w):
        return np.ascontiguousarray(w.reshape(-1, P, w.shape[-1]).transpose(1, 0, 2))

    def twice(w):
        w = w.reshape(*w.shape[:-1], NG, HG * DH)
        return np.concatenate([w, w], -1).reshape(*w.shape[:-2], NG * P)

    def column(v):
        return np.ascontiguousarray(v.reshape(-1, P).T)

    def transposed(x):
        return rows(x.reshape(B * S, D).T)

    def experts(shared, routed):
        w = np.concatenate([a(shared)[None], a(routed)])
        return np.ascontiguousarray(np.stack([rows(x).reshape(P, -1) for x in w]))

    p = np.arange(P)
    return {
        "x": np.ascontiguousarray(a("x").transpose(1, 0, 2)),
        "x_t": transposed(a("x")),
        "ctx_t": transposed(a("ctx_1024")),
        "ident": np.eye(P, dtype=np.float32),
        "head_mask": (p[:, None] % (P // 2) // DH == np.arange(HG)).astype(np.float32),
        "iota": np.ascontiguousarray(np.broadcast_to(np.arange(E, dtype=np.float32), (P, B, E))),
        "wqk1": rows(np.concatenate([a("L0_attn_Wq"), a("L0_attn_Wk")]).T),
        "wv1": rows(a("L0_attn_Wv").T), "wo1": rows(a("L0_attn_Wo").T),
        "wkx": rows(a("L0_xattn_Wk").T), "wvx": rows(a("L0_xattn_Wv").T),
        "wqx": rows(a("L0_xattn_Wq").T), "wox": rows(a("L0_xattn_Wo").T),
        "wq3": rows(twice(a("L0_ffn_wq"))), "wk3": rows(twice(a("L0_ffn_wk"))),
        "wv3": rows(a("L0_ffn_wv")), "wo3": rows(a("L0_ffn_wo")),
        "bias_qk1": np.concatenate([a("L0_attn_bq"), a("L0_attn_bk")]),
        "bias_v1": a("L0_attn_bv"), "bias_o1": a("L0_attn_bo"),
        "bias_qx": column(a("L0_xattn_bq")), "bias_vx": a("L0_xattn_bv"), "bias_ox": a("L0_xattn_bo"),
        "norm1": column(a("L0_ffn_norm1_w")), "norm2": column(a("L0_ffn_norm2_w")),
        "router": rows(a("L0_ffn_router_w")),
        "w_gate": experts("L0_ffn_sh_gate", "L0_ffn_e_gate"),
        "w_up": experts("L0_ffn_sh_up", "L0_ffn_e_up"),
        "w_down": experts("L0_ffn_sh_down", "L0_ffn_e_down"),
    }


def kernel(**inputs):
    import numpy as np
    import concourse.bacc as bacc
    from concourse.bass_utils import run_bass_kernel_spmd as run

    nc = bacc.Bacc("TRN2", target_bir_lowering=False, num_devices=1)
    arrays, t = {}, {}
    for name, x in layout(inputs).items():
        arrays[f"in_{name}"] = x
        t[name] = nc.dram_tensor(f"in_{name}", x.shape, mybir.dt.from_np(x.dtype), kind="ExternalInput").ap()
    out = nc.dram_tensor("out", (P, B, D), F32, kind="ExternalOutput").ap()
    decoder(nc, t, out)
    r = run(nc, [arrays], core_ids=[0])
    return np.ascontiguousarray(r.results[0]["out"].transpose(1, 0, 2))
```

```python
from contextlib import ExitStack

import concourse.bass as bass
from concourse import mybir

F32 = mybir.dt.float32
F32R = mybir.dt.float32r
BF16 = mybir.dt.bfloat16
FP16 = mybir.dt.float16
ALU = mybir.AluOpType
ACT = mybir.ActivationFunctionType
AX = mybir.AxisListType

P = 128
B, S, D = 32, 128, 256
H, DH = 16, 16
DK = D // P
PAIRS = B // 2
TOK = 2 * S
HG = 4
NG = H // HG
HH = H // 2
VP = 3 * DH + 1
E, DFF = 8, 512
FT = DFF // P
NE = E + 1
GT = 512
NGT = B * S // GT

SCHEDULE = {
    "sp": [("store_logit", 5), ("load_x2", 4), ("store_o1", 1), ("load_ctx", 1), ("load_o1", 1),
        ("load_x", 0), ("store_sum", 4), ("store_x2", 2), ("store_h2", 4)],
    "pe": [("logits", 5), ("values3", 4), ("qx", 2), ("sx", 2), ("q3_1", 3), ("k3_0", 3), ("v3", 3),
        ("k3_1", 3), ("q3_0", 3), ("turn_px", 2), ("pvx", 2), ("turn_o3", 4), ("turn_cx", 2), ("slot0", 3),
        ("turn0", 3), ("outx", 2), ("slot1", 3), ("values0", 3), ("out3", 4), ("turn1", 3), ("slot2", 3),
        ("turn_o1", 1), ("values1", 3), ("v1", 0), ("qk1_0", 0), ("qk1_1", 0), ("out1", 1), ("turn_h2", 4),
        ("slot3", 3), ("turn2", 3), ("kx", 1), ("vx", 1), ("values2", 3), ("turn3", 3), ("turn_x1", 1),
        ("turn_h", 2)],
    "act": [("head_exp1", 1), ("turn_h", 3), ("logits", 5), ("qx", 2), ("sx", 2), ("q3_1", 3),
        ("head_exp2", 1), ("k3_0", 3), ("v3", 3), ("mask0", 3), ("v3_hi", 3), ("k3_1", 3), ("mask1", 3),
        ("q3_0", 3), ("turn_px", 2), ("head_exp3", 1), ("pvx", 2), ("v3_mid", 3), ("turn_o3", 4),
        ("turn_cx", 2), ("mask2", 3), ("exp0", 3), ("hi0", 3), ("mask3", 3), ("exp1", 3), ("hi1", 3),
        ("ctx_hi", 1), ("x_hi", 0), ("turn_o1", 1), ("square_h2", 4), ("v1", 0), ("norm_h2", 4),
        ("qk1_0", 0), ("qk1_1", 0), ("exp2", 3), ("square_h", 2), ("turn_h2", 4), ("hi2", 3),
        ("head_exp0", 0), ("kx", 1), ("exp3", 3), ("vx", 1), ("norm_h", 2), ("hi3", 3), ("turn_x1", 1)],
    "dve": [("lo3", 4), ("turn_x1", 2), ("head_output0", 1), ("turn_h", 3), ("sx", 2), ("head_shift2", 1),
        ("recip_x", 2), ("q3_1", 3), ("heads_out3", 4), ("head_output1", 1), ("k3_0", 3),
        ("head_shift3", 1), ("k3_1", 3), ("q3_0", 3), ("v3_rest", 3), ("head_output2", 1), ("v3_mid", 3),
        ("max0", 3), ("turn_cx", 2), ("turn_o3", 4), ("head_output3", 1), ("lo0", 3), ("max1", 3),
        ("heads_out0", 3), ("outx", 2), ("out3", 4), ("lo1", 3), ("x_lo", 0), ("max2", 3),
        ("heads_out1", 3), ("turn_o1", 1), ("ctx_lo", 1), ("norm_x2", 2), ("out1", 1), ("head_shift0", 0),
        ("max3", 3), ("lo2", 3), ("norm_x1", 1), ("heads_out2", 3), ("head_shift1", 0)],
    "pool": [("qk_products2", 1), ("pv_products1", 1), ("qk_products3", 1), ("pv_products2", 1),
        ("mask0", 3), ("pv_products3", 1), ("mask1", 3), ("mask2", 3), ("mask3", 3), ("root_z2", 2),
        ("root_h2", 4), ("qk_products0", 0), ("root_y1", 1), ("root_h", 2), ("qk_products1", 0),
        ("pv_products0", 0)],
}
NW = 3
BANK = {
    "v1": 0, "qk1_0": 1, "qk1_1": 0, "turn_h": 0, "q3_1": 0, "k3_0": 1, "v3": 0, "k3_1": 2, "q3_0": 0,
    "turn_o1": 2, "out1": 1, "kx": 0, "vx": 1, "turn_x1": 1, "qx": 1, "sx": 1, "turn_px": 1, "pvx": 1,
    "turn_cx": 0, "outx": 0, "turn_o3": 2, "out3": 1, "turn_h2": 0, "logits": 2
}
LAG = {job: lag for job, lag in SCHEDULE["pe"]}
MAX_LAG = max(lag for steps in SCHEDULE.values() for _, lag in steps)
LOOP = (MAX_LAG + 1, PAIRS)


def active(lag, it):
    return not isinstance(it, int) or 0 <= it - lag < PAIRS


def bank_count(job, it, lag):
    back = lag - LAG[job]
    at = it - back
    n = 1
    seen = False
    for j, l in SCHEDULE["pe"]:
        if j == job:
            seen = True
        if BANK.get(j) == BANK[job]:
            if isinstance(it, int):
                n = n + max(0, min(PAIRS, at - l)) + (not seen and active(l, at))
            else:
                assert LOOP[0] - back - l >= 0 and LOOP[1] - back - l <= PAIRS, (job, j)
                n = n + (at - l) + (not seen)
    return n


def later(pair):
    return not isinstance(pair, int) or pair > 0


def for_iterations(engine, step, schedule):
    def body(it):
        for job, lag in schedule:
            if active(lag, it):
                step(job, it - lag, it, lag)

    for it in range(LOOP[0]):
        body(it)
    with engine.Fori(LOOP[0], LOOP[1]) as it:
        body(it)
    for it in range(LOOP[1], PAIRS + MAX_LAG):
        body(it)


def wait_apart(engine, semaphore, value, passed):
    engine.wait_ge(semaphore, value)
    if not isinstance(value, int):
        engine.sem_inc(passed, 1)


BIAS_ROWS = 3
BIAS_OF = {"qk1": (0, 0), "v1": (1, 0), "o1": (1, D), "vx": (2, 0), "ox": (2, D)}


def phase_a(nc, t, scratch, sem):
    ctx = ExitStack()

    def sb(name, shape, dt=F32):
        return ctx.enter_context(nc.sbuf_tensor(name, shape, dt))

    with ctx:
        ident = sb("ident", [P, P])
        head_mask = sb("head_mask", [P, HG])
        half_power = sb("half_power", [P, 2])
        bias_hi = sb("bias_hi", [BIAS_ROWS, 2 * D], F32R)
        bias_lo = sb("bias_lo", [BIAS_ROWS, 2 * D], F32R)
        select = sb("select", [BIAS_ROWS, BIAS_ROWS, P], F32R)
        bias_qx = sb("bias_qx", [P, DK])
        norm1 = sb("norm1", [P, DK])
        norm2 = sb("norm2", [P, DK])
        router = sb("router", [P, DK, E])
        QW = NG * P
        widths = {"wqk1": 2 * D, "wv1": D, "wo1": D, "wkx": D, "wvx": D, "wqx": D, "wox": D,
                  "wq3": QW, "wk3": QW, "wv3": D, "wo3": D}
        scales = {"wq3": DH ** -0.5, "wqx": D ** -0.5}
        w_hi = {n: sb(f"{n}_hi", [P, DK, w], F32R) for n, w in widths.items()}
        w_lo = {n: sb(f"{n}_lo", [P, DK, w], F32R) for n, w in widths.items()}

        key_blocks = sb("key_blocks", [P, 2, 2, 2, HG, S], F32R)
        probs = sb("probs", [P, 2, HH, S])
        probs_hi = sb("probs_hi", [P, HH, S], FP16)
        probs_lo = sb("probs_lo", [P, HH, S], FP16)
        neg_max = sb("neg_max", [P, 2, HH])
        rden = sb("rden", [P, HH])
        osum = sb("osum", [P, HH, DH])
        v_full = sb("v_full", [P, 2 * H, DH])
        v_rest = sb("v_rest", [P, 2 * H, DH])
        qk1 = sb("qk1", [P, 2, 2 * D])
        v1 = sb("v1", [P, 2, D])
        qk_prod = sb("qk_prod", [P, HH, H, DH])
        pv_prod = sb("pv_prod", [P, HH, DH, H])
        head_scores = sb("head_scores", [P, 2, HH, H])
        head_probs = sb("head_probs", [P, 2, HH, H])
        head_max = sb("head_max", [P, HH])
        head_den = sb("head_den", [P, HH])
        head_sum = sb("head_sum", [P, HH, DH])
        o1_rows = sb("o1_rows", [P, 2, D])
        q_rows = {s: sb(f"q_rows{s}", [P, NG, TOK], F32R) for s in (3,)}
        k_parts = {s: sb(f"k_parts{s}", [P, 2, NG, TOK], F32R) for s in (3,)}
        values = {s: sb(f"values{s}", [P, 2 * H, VP], BF16) for s in (3,)}
        att_out = {s: sb(f"att_out{s}", [P, 2, D]) for s in (1, 3)}
        x_t = sb("x_t", [P, DK, TOK])
        ctx_t = sb("ctx_t", [P, DK, TOK])
        parts = {n: (sb(f"{n}_hi", [P, DK, TOK], F32R), sb(f"{n}_lo", [P, DK, TOK], F32R))
                 for n in ("x", "ctx", "o1", "x1", "cx", "h", "o3")}
        x_res = sb("x_res", [P, 2, D])
        y1 = sb("y1", [P, 2, D])
        x1 = sb("x1", [P, 2, D])
        z2 = sb("z2", [P, 2, D])
        x2 = sb("x2", [P, 2, D])
        h_in = sb("h_in", [P, 2, D])
        x2_res = sb("x2_res", [P, 2, D])
        x3 = sb("x3", [P, 2, D])
        x2_x3 = sb("x2_x3", [P, 2, D])
        h2_in = sb("h2_in", [P, 2, D])
        h2_t = sb("h2_t", [P, DK, TOK])
        logit = sb("logit", [P, 2, E])
        kx_t = sb("kx_t", [P, DK, TOK])
        qx_t = sb("qx_t", [P, DK, TOK])
        vx = sb("vx", [P, 2, D])
        px = sb("px", [P, 2, S])
        px_t = sb("px_t", [P, 2, S])
        cx = sb("cx", [P, 2, D])
        neg_max_x = sb("neg_max_x", [P, 2])
        den_x = sb("den_x", [P, 2])
        rden_x = sb("rden_x", [P, 2])
        stats = {n: sb(f"stats_{n}", [P, 2, 6]) for n in ("y1", "z2")}
        mean_var = {n: sb(f"mean_var_{n}", [P, 2, 2]) for n in ("y1", "z2")}
        var_eps = {n: sb(f"var_eps_{n}", [P, 2]) for n in ("y1", "z2", "h", "h2")}
        rstd = {n: sb(f"rstd_{n}", [P, 2]) for n in ("y1", "z2", "h", "h2")}
        squares = {n: sb(f"squares_{n}", [P, 2]) for n in ("h", "h2")}
        square_out = sb("square_out", [P, 2, D])
        raw = {n: probs[:, i, :, :].rearrange("p h n -> p (h n)").rearrange("p (d n) -> p d n", d=DK)
               for i, n in enumerate("ab")}

        raw_bias = qk_prod[0:BIAS_ROWS, :, :, :].rearrange("p h k d -> p (h k d)")[:, 0:2 * D]
        raw_select = pv_prod[0:BIAS_ROWS, :, :, :].rearrange("p h d k -> p (h d k)")[:, 0:BIAS_ROWS * P]\
            .rearrange("p (r n) -> p r n", r=BIAS_ROWS)

        scores = ctx.enter_context(nc.psum_tensor("scores", [P, HH * S], F32))
        probs_t = ctx.enter_context(nc.psum_tensor("probs_t", [P, HH * S], F32))
        pv = ctx.enter_context(nc.psum_tensor("pv", [P, 512], F32))
        work = [ctx.enter_context(nc.psum_tensor(f"work{i}", [P, 512], F32)) for i in range(NW)]

        const_loaded = sem("const_loaded")
        raw_loaded = {n: sem(f"raw_loaded_{n}") for n in raw}
        raw_hi_done, raw_lo_done = sem("raw_hi_done"), sem("raw_lo_done")
        bias_scaled = sem("bias_scaled")
        ones_set = sem("ones_set")
        x_loaded, ctx_loaded = sem("x_loaded"), sem("ctx_loaded")
        x2_res_loaded = sem("x2_res_loaded")
        x2_stored, sum_stored, h2_stored, logit_stored = (sem(n) for n in ("x2_stored", "sum_stored", "h2_stored", "logit_stored"))
        work_ready = [sem(f"work_ready{i}") for i in range(NW)]
        work_read = [sem(f"work_read{i}") for i in range(NW)]
        hi_done = {j: sem(f"hi_done_{j}") for j in
                   ("q3_0", "q3_1", "k3_0", "k3_1", "v3",
                    "turn_o1", "turn_x1", "turn_cx", "turn_h", "turn_o3", "x", "ctx")}
        lo_done = {j: sem(f"lo_done_{j}") for j in ("x", "ctx")}
        v_low_done = sem("v_low_done")
        v_rest_done = sem("v_rest_done")
        v_mid_done = sem("v_mid_done")
        qk_prod_done = sem("qk_prod_done")
        head_scores_done = sem("head_scores_done")
        head_max_done = sem("head_max_done")
        head_shifted = sem("head_shifted")
        head_exp_done = sem("head_exp_done")
        head_den_done = sem("head_den_done")
        pv_prod_done = sem("pv_prod_done")
        head_sum_done = sem("head_sum_done")
        head_out_done = sem("head_out_done")
        o1_stored, o1_loaded = sem("o1_stored"), sem("o1_loaded")
        mask_hi_done = sem("mask_hi_done")
        mask_lo_done = sem("mask_lo_done")
        scores_done = sem("scores_done")
        max_done = sem("max_done")
        exp_done = sem("exp_done")
        turned = sem("turned")
        probs_hi_done = sem("probs_hi_done")
        probs_lo_done = sem("probs_lo_done")
        pv_done = sem("pv_done")
        out_done = sem("out_done")
        stat_done = {n: sem(f"stat_done_{n}") for n in rstd}
        stats_done = {n: sem(f"stats_done_{n}") for n in stats}
        eps_done = {n: sem(f"eps_done_{n}") for n in rstd}
        rstd_done = {n: sem(f"rstd_done_{n}") for n in rstd}
        x1_done, x2_done, sum_done = sem("x1_done"), sem("x2_done"), sem("sum_done")
        h_done, h2_done = sem("h_done"), sem("h2_done")
        max_x_done, rden_x_done = sem("max_x_done"), sem("rden_x_done")
        osum_done = sem("osum_done")
        power_set = sem("power_set")
        passed = {n: sem(f"passed_{n}") for n in ("sp", "dve", "pool")}

        CONSTS = 8

        split_order = list(widths)
        split_buffer = {n: "ab"[i % 2] for i, n in enumerate(split_order)}

        with nc.Block() as block:

            @block.sync
            def _(sp):
                consts = [(ident, "ident"), (head_mask, "head_mask"), (bias_qx, "bias_qx"), (norm1, "norm1"),
                          (norm2, "norm2")]
                for dst, name in consts:
                    sp.dma_start(dst[:, :], t[name]).then_inc(const_loaded, 16)
                sp.dma_start(router[:, :, :], t["router"]).then_inc(const_loaded, 16)
                sp.dma_start(raw_bias, t["bias_rows"]).then_inc(const_loaded, 16)
                sp.dma_start(raw_select, t["select"]).then_inc(const_loaded, 16)
                for i, n in enumerate(split_order):
                    b = split_buffer[n]
                    if i >= 2:
                        sp.wait_ge(raw_lo_done, i - 1)
                    sp.dma_start(raw[b][:, :, 0:widths[n]], t[n]).then_inc(raw_loaded[b], 16)
                o1_write = scratch["o1"].rearrange("b (h s d) -> s b h d", h=H, s=S)
                o1_read = scratch["o1"].rearrange("b (s e) -> s b e", s=S)

                def wait(semaphore, value):
                    wait_apart(sp, semaphore, value, passed["sp"])

                def step(job, pair, it, lag):
                    rows = bass.ds(2 * pair, 2)
                    if job == "load_x":
                        if later(pair):
                            wait(lo_done["x"], pair)
                        sp.dma_start(x_t[:, :, :], t["x_t"][:, :, bass.ds(TOK * pair, TOK)]).then_inc(x_loaded, 16)
                    elif job == "store_o1":
                        wait(head_out_done, 4 * (pair + 1))
                        for a in range(2):
                            sp.dma_start(o1_write[:, bass.ds(2 * pair + a, 1), :, :].rearrange("s b h d -> s (b h) d"),
                                         att_out[1][:, a, :].rearrange("p (h d) -> p h d", h=H)).then_inc(o1_stored, 16)
                    elif job == "load_o1":
                        if later(pair):
                            wait(stat_done["y1"], pair)
                        sp.dma_start(x_res[:, :, :], t["x"][:, rows, :]).then_inc(o1_loaded, 16)
                        wait(o1_stored, 32 * (pair + 1))
                        sp.dma_start(o1_rows[:, :, :], o1_read[:, rows, :]).then_inc(o1_loaded, 16)
                    elif job == "load_ctx":
                        if later(pair):
                            wait(lo_done["ctx"], pair)
                        sp.dma_start(ctx_t[:, :, :], t["ctx_t"][:, :, bass.ds(TOK * pair, TOK)]).then_inc(ctx_loaded, 16)
                    elif job == "load_x2":
                        if later(pair):
                            wait(sum_done, pair)
                        wait(x2_stored, 16 * (pair + 1))
                        sp.dma_start(x2_res[:, :, :], scratch["x2"][:, rows, :]).then_inc(x2_res_loaded, 16)
                    elif job == "store_x2":
                        wait(x2_done, pair + 1)
                        sp.dma_start(scratch["x2"][:, rows, :], x2[:, :, :]).then_inc(x2_stored, 16)
                    elif job == "store_sum":
                        wait(sum_done, pair + 1)
                        sp.dma_start(scratch["x2_x3"][:, rows, :], x2_x3[:, :, :]).then_inc(sum_stored, 16)
                    elif job == "store_h2":
                        wait(work_read[BANK["turn_h2"]], bank_count("turn_h2", it, lag))
                        sp.dma_start(scratch["h2_t"][:, :, bass.ds(TOK * pair, TOK)], h2_t[:, :, :]).then_inc(h2_stored, 16)
                    elif job == "store_logit":
                        wait(work_read[BANK["logits"]], bank_count("logits", it, lag))
                        sp.dma_start(scratch["logit"][:, rows, :], logit[:, :, :]).then_inc(logit_stored, 16)

                for_iterations(sp, step, SCHEDULE["sp"])
                for s in (x2_stored, sum_stored, h2_stored, logit_stored):
                    sp.wait_ge(s, 16 * PAIRS)

            @block.tensor
            def _(pe):
                def split_products(out, lhs, rhs, bias=None):
                    (lh, ll), (rh, rl) = lhs, rhs
                    n = 0
                    for a, b in ((lh, rh), (lh, rl), (ll, rh)):
                        for dk in range(DK):
                            n += 1
                            mm = pe.matmul(out, a(dk), b(dk), start=(n == 1), stop=(n == 3 * DK and not bias))
                    if bias:
                        row, c = BIAS_OF[bias]
                        width = out.shape[-1]
                        for part in (bias_hi, bias_lo):
                            mm = pe.matmul(out, select[:, row, :], part[:, c:c + width], start=False, stop=(part is bias_lo))
                    return mm

                def to_rows(bank, weight, m0, source):
                    for m in range(2):
                        c = (m0 + m) * P
                        mm = split_products(bank[:, m * TOK:(m + 1) * TOK],
                                            [lambda dk, w=w: w[weight][:, dk, c:c + P] for w in (w_hi, w_lo)],
                                            [lambda dk, x=x: x[:, dk, :] for x in parts[source]])
                    return mm

                def to_tokens(bank, weight, source, bias=None):
                    for a in range(2):
                        mm = split_products(bank[:, a * D:(a + 1) * D],
                                            [lambda dk, x=x: x[:, dk, a * S:(a + 1) * S] for x in parts[source]],
                                            [lambda dk, w=w: w[weight][:, dk, :] for w in (w_hi, w_lo)], bias)
                    return mm

                def turn(bank, src):
                    for dk in range(DK):
                        for a in range(2):
                            mm = pe.transpose(bank[:, dk * TOK + a * S:dk * TOK + (a + 1) * S],
                                              src[:, a, dk * P:(dk + 1) * P], ident[:, :])
                    return mm

                def slot_scores(n, pair, it, lag):
                    g = 4 * pair + n
                    a, half = n // 2, n % 2
                    pe.wait_ge(mask_hi_done, g + 1)
                    pe.wait_ge(mask_lo_done, g + 1)
                    job = f"q3_{half}"
                    pe.wait_ge(work_read[BANK[job]], bank_count(job, it, lag))
                    if later(g):
                        pe.wait_ge(exp_done, g)
                    for j in range(2):
                        for part in range(2):
                            mm = pe.matmul(scores[:, j * HG * S:(j + 1) * HG * S],
                                           q_rows[3][:, 2 * half + j, a * S:(a + 1) * S],
                                           key_blocks[:, n % 2, part, j, :, :], start=(part == 0), stop=(part == 1))
                    mm.then_inc(scores_done, 1)

                def slot_turn(n, pair):
                    g = 4 * pair + n
                    pe.wait_ge(exp_done, g + 1)
                    if later(g):
                        pe.wait_ge(probs_lo_done, g)
                    for h in range(HH):
                        mm = pe.transpose(probs_t[:, h * S:(h + 1) * S], probs[:, n % 2, h, :], ident[:, :])
                    mm.then_inc(turned, 1)

                def slot_values(n, pair):
                    g = 4 * pair + n
                    a, half = n // 2, n % 2
                    pe.wait_ge(probs_lo_done, g + 1)
                    pe.wait_ge(v_low_done, pair + 1)
                    if later(g):
                        pe.wait_ge(out_done, g)
                    for h in range(HH):
                        v = values[3][:, a * H + half * HH + h, :]
                        pe.matmul(pv[:, h * VP:(h + 1) * VP], probs_hi[:, h, :], v, start=True, stop=False)
                        mm = pe.matmul(pv[:, h * VP:(h + 1) * VP], probs_lo[:, h, :], v, start=False, stop=True)
                    mm.then_inc(pv_done, 1)

                def work_job(job, pair, it, lag):
                    bank = work[BANK[job]]

                    def wait_read(other):
                        pe.wait_ge(work_read[BANK[other]], bank_count(other, it, lag))

                    uses = bank_count(job, it, lag) - 1
                    if not isinstance(uses, int) or uses > 0:
                        pe.wait_ge(work_read[BANK[job]], uses)
                    if job in ("qk1_0", "qk1_1"):
                        a = int(job[4])
                        pe.wait_ge(lo_done["x"], pair + 1)
                        mm = split_products(bank[:, :],
                                            [lambda dk, x=x: x[:, dk, a * S:(a + 1) * S] for x in parts["x"]],
                                            [lambda dk, w=w: w["wqk1"][:, dk, :] for w in (w_hi, w_lo)], "qk1")
                    elif job == "v1":
                        pe.wait_ge(lo_done["x"], pair + 1)
                        mm = to_tokens(bank, "wv1", "x", "v1")
                    elif job in ("q3_0", "q3_1", "k3_0", "k3_1"):
                        wait_read("turn_h")
                        mm = to_rows(bank, "w" + job[:2], 2 * int(job[3]), "h")
                    elif job == "v3":
                        wait_read("turn_h")
                        mm = to_tokens(bank, "wv3", "h")
                    elif job == "turn_o1":
                        pe.wait_ge(o1_loaded, 32 * (pair + 1))
                        mm = turn(bank, o1_rows)
                    elif job == "out1":
                        wait_read("turn_o1")
                        mm = to_tokens(bank, "wo1", "o1", "o1")
                    elif job == "turn_x1":
                        pe.wait_ge(x1_done, pair + 1)
                        mm = turn(bank, x1)
                    elif job == "kx":
                        pe.wait_ge(lo_done["ctx"], pair + 1)
                        mm = to_rows(bank, "wkx", 0, "ctx")
                    elif job == "vx":
                        pe.wait_ge(lo_done["ctx"], pair + 1)
                        mm = to_tokens(bank, "wvx", "ctx", "vx")
                    elif job == "qx":
                        wait_read("turn_x1")
                        mm = to_rows(bank, "wqx", 0, "x1")
                    elif job == "sx":
                        wait_read("kx")
                        wait_read("qx")
                        for a in range(2):
                            for dk in range(DK):
                                mm = pe.matmul(bank[:, a * S:(a + 1) * S], qx_t[:, dk, a * S:(a + 1) * S],
                                               kx_t[:, dk, a * S:(a + 1) * S], start=(dk == 0), stop=(dk == DK - 1))
                    elif job == "turn_px":
                        wait_read("sx")
                        for a in range(2):
                            mm = pe.transpose(bank[:, a * S:(a + 1) * S], px[:, a, :], ident[:, :])
                    elif job == "pvx":
                        wait_read("turn_px")
                        wait_read("vx")
                        for a in range(2):
                            mm = pe.matmul(bank[:, a * D:(a + 1) * D], px_t[:, a, :], vx[:, a, :], start=True, stop=True)
                    elif job == "turn_cx":
                        wait_read("pvx")
                        mm = turn(bank, cx)
                    elif job == "outx":
                        wait_read("turn_cx")
                        mm = to_tokens(bank, "wox", "cx", "ox")
                    elif job == "turn_h":
                        pe.wait_ge(h_done, pair + 1)
                        mm = turn(bank, h_in)
                    elif job == "turn_o3":
                        pe.wait_ge(out_done, 4 * (pair + 1))
                        mm = turn(bank, att_out[3])
                    elif job == "out3":
                        wait_read("turn_o3")
                        mm = to_tokens(bank, "wo3", "o3")
                    elif job == "turn_h2":
                        pe.wait_ge(h2_done, pair + 1)
                        mm = turn(bank, h2_in)
                    elif job == "logits":
                        wait_read("turn_h2")
                        for a in range(2):
                            for dk in range(DK):
                                mm = pe.matmul(bank[:, a * E:(a + 1) * E], h2_t[:, dk, a * S:(a + 1) * S],
                                               router[:, dk, :], start=(dk == 0), stop=(dk == DK - 1))
                    mm.then_inc(work_ready[BANK[job]], 1)

                pe.wait_ge(const_loaded, 16 * CONSTS)
                pe.wait_ge(raw_lo_done, len(split_order) + 1)
                pe.wait_ge(ones_set, 1)

                def step(job, pair, it, lag):
                    if job.startswith("slot"):
                        slot_scores(int(job[4]), pair, it, lag)
                    elif job in ("turn0", "turn1", "turn2", "turn3"):
                        slot_turn(int(job[4]), pair)
                    elif job.startswith("values"):
                        slot_values(int(job[6]), pair)
                    else:
                        work_job(job, pair, it, lag)

                for_iterations(pe, step, SCHEDULE["pe"])

            @block.scalar
            def _(act):
                act.wait_ge(const_loaded, 16 * CONSTS)
                act.mul(bias_qx[:, :], bias_qx[:, :], D ** -0.5).then_inc(bias_scaled, 1)
                act.wait_ge(bias_scaled, 1)
                for i, n in enumerate(split_order):
                    b = split_buffer[n]
                    act.wait_ge(raw_loaded[b], 16 * (i // 2 + 1))
                    act.activation(w_hi[n][:, :, :], raw[b][:, :, 0:widths[n]], ACT.Copy,
                                   scale=scales.get(n, 1.0)).then_inc(raw_hi_done, 1)
                act.activation(select[:, :, :], raw_select, ACT.Copy)
                act.activation(bias_hi[:, :], raw_bias, ACT.Copy).then_inc(raw_hi_done, 1)
                act.wait_ge(raw_lo_done, len(split_order) + 1)

                def product_ready(job, it, lag):
                    act.wait_ge(work_ready[BANK[job]], bank_count(job, it, lag))

                def last_used(job, pair, it, lag):
                    if later(pair):
                        act.wait_ge(work_ready[BANK[job]], bank_count(job, it, lag + 1))

                def slot_step(kind, n, pair, it, lag):
                    g = 4 * pair + n
                    a, half = n // 2, n % 2
                    if kind == "mask":
                        act.wait_ge(hi_done[f"k3_{half}"], pair + 1)
                        if not isinstance(g, int) or g > 1:
                            act.wait_ge(scores_done, g - 1)
                        for j in range(HG):
                            ins = act.activation(key_blocks[:, n % 2, 0, :, j, :],
                                                 k_parts[3][:, 0, 2 * half:2 * half + 2, a * S:(a + 1) * S].bitcast(F32),
                                                 ACT.Copy, scale=head_mask[:, j:j + 1])
                        ins.then_inc(mask_hi_done, 1)
                    elif kind == "exp":
                        act.wait_ge(max_done, g + 1)
                        if not isinstance(g, int) or g > 1:
                            act.wait_ge(turned, g - 1)
                        for h in range(HH):
                            ins = act.activation(probs[:, n % 2, h, :], scores[:, h * S:(h + 1) * S], ACT.Exp,
                                                 bias=neg_max[:, n % 2, h:h + 1])
                        ins.then_inc(exp_done, 1)
                    elif kind == "hi":
                        act.wait_ge(turned, g + 1)
                        if later(g):
                            act.wait_ge(pv_done, g)
                        act.activation(probs_hi[:, :, :], probs_t[:, :].rearrange("p (h n) -> p h n", h=HH),
                                       ACT.Copy).then_inc(probs_hi_done, 1)

                def step(job, pair, it, lag):
                    bank = work[BANK[job]] if job in BANK else None
                    read = work_read[BANK[job]] if job in BANK else None
                    if job[:-1] in ("mask", "exp", "hi"):
                        slot_step(job[:-1], int(job[-1]), pair, it, lag)
                    elif job in ("x_hi", "ctx_hi"):
                        name, src, loaded, users = (("x", x_t, x_loaded, ("qk1_0", "qk1_1", "v1")) if job == "x_hi" else
                                                    ("ctx", ctx_t, ctx_loaded, ("kx", "vx")))
                        act.wait_ge(loaded, 16 * (pair + 1))
                        for user in users:
                            last_used(user, pair, it, lag)
                        act.activation(parts[name][0][:, :, :], src[:, :, :], ACT.Copy).then_inc(hi_done[name], 1)
                    elif job in ("qk1_0", "qk1_1"):
                        a = int(job[4])
                        product_ready(job, it, lag)
                        if later(pair):
                            act.wait_ge(qk_prod_done, 4 * pair - 2 + 2 * a)
                        act.activation(qk1[:, a, :], bank[:, :], ACT.Copy).then_inc(read, 1)
                    elif job == "v1":
                        product_ready(job, it, lag)
                        if later(pair):
                            act.wait_ge(pv_prod_done, 4 * pair)
                        act.activation(v1[:, :, :], bank[:, :].rearrange("p (a n) -> p a n", a=2), ACT.Copy).then_inc(read, 1)
                    elif job.startswith("head_exp"):
                        n = int(job[8])
                        u = 4 * pair + n
                        act.wait_ge(head_shifted, u + 1)
                        if not isinstance(u, int) or u > 1:
                            act.wait_ge(head_out_done, u - 1)
                        act.activation(head_probs[:, n % 2, :, :], head_scores[:, n % 2, :, :], ACT.Exp,
                                       scale=DH ** -0.5).then_inc(head_exp_done, 1)
                    elif job in ("turn_o1", "turn_x1", "turn_cx", "turn_o3"):
                        src, user = {"turn_o1": ("o1", "out1"), "turn_x1": ("x1", "qx"), "turn_cx": ("cx", "outx"),
                                     "turn_o3": ("o3", "out3")}[job]
                        product_ready(job, it, lag)
                        last_used(user, pair, it, lag)
                        act.activation(parts[src][0][:, :, :], bank[:, :].rearrange("p (d n) -> p d n", d=DK),
                                       ACT.Copy).then_inc(hi_done[job], 1)
                    elif job in ("q3_0", "q3_1", "k3_0", "k3_1"):
                        m = int(job[3])
                        product_ready(job, it, lag)
                        if later(pair):
                            act.wait_ge(scores_done, 4 * pair - 1 + m)
                        dst = q_rows[3] if job[0] == "q" else k_parts[3][:, 0]
                        act.activation(dst[:, 2 * m:2 * m + 2, :], bank[:, :].rearrange("p (g n) -> p g n", g=2),
                                       ACT.Copy).then_inc(hi_done[job], 1)
                    elif job == "v3":
                        product_ready(job, it, lag)
                        if later(pair):
                            act.wait_ge(v_rest_done, pair)
                        act.activation(v_full[:, :, :].rearrange("p (a h) d -> p a (h d)", a=2),
                                       bank[:, :].rearrange("p (a n) -> p a n", a=2), ACT.Copy).then_inc(read, 1)
                    elif job == "v3_hi":
                        act.wait_ge(work_read[BANK["v3"]], bank_count("v3", it, lag))
                        if later(pair):
                            act.wait_ge(pv_done, 4 * pair)
                        act.activation(values[3][:, :, 0:DH], v_full[:, :, :], ACT.Copy).then_inc(hi_done["v3"], 1)
                    elif job == "v3_mid":
                        act.wait_ge(v_rest_done, pair + 1)
                        act.activation(values[3][:, :, DH:2 * DH], v_rest[:, :, :], ACT.Copy).then_inc(v_mid_done, 1)
                    elif job == "turn_h":
                        product_ready(job, it, lag)
                        for user in ("q3_0", "q3_1", "k3_0", "k3_1", "v3"):
                            last_used(user, pair, it, lag)
                        for dk in range(DK):
                            ins = act.activation(parts["h"][0][:, dk, :], bank[:, dk * TOK:(dk + 1) * TOK], ACT.Copy,
                                                 scale=norm1[:, dk:dk + 1])
                        ins.then_inc(hi_done[job], 1)
                    elif job == "turn_h2":
                        product_ready(job, it, lag)
                        last_used("logits", pair, it, lag)
                        if later(pair):
                            act.wait_ge(h2_stored, 16 * pair)
                        for dk in range(DK):
                            ins = act.activation(h2_t[:, dk, :], bank[:, dk * TOK:(dk + 1) * TOK], ACT.Copy,
                                                 scale=norm2[:, dk:dk + 1])
                        ins.then_inc(read, 1)
                    elif job == "kx":
                        product_ready(job, it, lag)
                        last_used("sx", pair, it, lag)
                        act.activation(kx_t[:, :, :], bank[:, :].rearrange("p (d n) -> p d n", d=DK), ACT.Copy).then_inc(read, 1)
                    elif job == "vx":
                        product_ready(job, it, lag)
                        last_used("pvx", pair, it, lag)
                        act.activation(vx[:, :, :], bank[:, :].rearrange("p (a n) -> p a n", a=2), ACT.Copy).then_inc(read, 1)
                    elif job == "qx":
                        product_ready(job, it, lag)
                        last_used("sx", pair, it, lag)
                        for dk in range(DK):
                            ins = act.activation(qx_t[:, dk, :], bank[:, dk * TOK:(dk + 1) * TOK], ACT.Identity,
                                                 bias=bias_qx[:, dk:dk + 1])
                        ins.then_inc(read, 1)
                    elif job == "sx":
                        act.wait_ge(max_x_done, pair + 1)
                        last_used("turn_px", pair, it, lag)
                        if later(pair):
                            act.wait_ge(rden_x_done, pair)
                        for a in range(2):
                            ins = act.activation(px[:, a, :], bank[:, a * S:(a + 1) * S], ACT.Exp,
                                                 bias=neg_max_x[:, a:a + 1], accum_out=den_x[:, a:a + 1])
                        ins.then_inc(read, 1)
                    elif job == "turn_px":
                        product_ready(job, it, lag)
                        last_used("pvx", pair, it, lag)
                        act.activation(px_t[:, :, :], bank[:, 0:TOK].rearrange("p (a n) -> p a n", a=2), ACT.Copy).then_inc(read, 1)
                    elif job == "pvx":
                        product_ready(job, it, lag)
                        act.wait_ge(rden_x_done, pair + 1)
                        last_used("turn_cx", pair, it, lag)
                        for a in range(2):
                            ins = act.activation(cx[:, a, :], bank[:, a * D:(a + 1) * D], ACT.Copy, scale=rden_x[:, a:a + 1])
                        ins.then_inc(read, 1)
                    elif job == "logits":
                        product_ready(job, it, lag)
                        if later(pair):
                            act.wait_ge(logit_stored, 16 * pair)
                        act.activation(logit[:, :, :], bank[:, 0:2 * E].rearrange("p (a n) -> p a n", a=2), ACT.Copy)\
                           .then_inc(read, 1)
                    elif job in ("square_h", "square_h2"):
                        name, src, done = ("h", x2, h_done) if job == "square_h" else ("h2", x3, h2_done)
                        if job == "square_h":
                            act.wait_ge(x2_done, pair + 1)
                        else:
                            act.wait_ge(work_read[BANK["out3"]], bank_count("out3", it, lag))
                        if later(pair):
                            act.wait_ge(done, pair)
                        for a in range(2):
                            ins = act.activation(square_out[:, a, :], src[:, a, :], ACT.Square,
                                                 accum_out=squares[name][:, a:a + 1])
                        ins.then_inc(stat_done[name], 1)
                    elif job in ("norm_h", "norm_h2"):
                        name, src, dst, done, user = (("h", x2, h_in, h_done, "turn_h") if job == "norm_h" else
                                                      ("h2", x3, h2_in, h2_done, "turn_h2"))
                        act.wait_ge(rstd_done[name], pair + 1)
                        last_used(user, pair, it, lag)
                        for a in range(2):
                            ins = act.activation(dst[:, a, :], src[:, a, :], ACT.Copy, scale=rstd[name][:, a:a + 1])
                        ins.then_inc(done, 1)

                for_iterations(act, step, SCHEDULE["act"])

            @block.vector
            def _(dve):
                for i, n in enumerate(split_order):
                    b = split_buffer[n]
                    dve.wait_ge(raw_hi_done, i + 1)
                    dve.scalar_tensor_tensor(out=w_lo[n][:, :, :], in0=raw[b][:, :, 0:widths[n]],
                                             scalar=scales.get(n, 1.0), in1=w_hi[n][:, :, :].bitcast(F32),
                                             op0=ALU.mult, op1=ALU.subtract).then_inc(raw_lo_done, 1)
                dve.wait_ge(raw_hi_done, len(split_order) + 1)
                dve.tensor_tensor(bias_lo[:, :], raw_bias, bias_hi[:, :].bitcast(F32), ALU.subtract).then_inc(raw_lo_done, 1)
                dve.memset(values[3][:, :, VP - 1:VP], 1.0).then_inc(ones_set, 1)

                def product_ready(job, it, lag):
                    dve.wait_ge(work_ready[BANK[job]], bank_count(job, it, lag))

                def residual_stats(job, name, dst, res, done, pair, it, lag):
                    b = BANK[job]
                    product_ready(job, it, lag)
                    if later(pair):
                        dve.wait_ge(done, pair)
                    dve.tensor_tensor(dst[:, :, :], work[b][:, :].rearrange("p (a n) -> p a n", a=2), res[:, :, :],
                                      ALU.add).then_inc(work_read[b], 1)
                    dve.wait_ge(work_read[b], bank_count(job, it, lag))
                    for a in range(2):
                        ins = dve.bn_stats(stats[name][:, a, :], dst[:, a, :])
                    ins.then_inc(stats_done[name], 1)
                    wait_apart(dve, stats_done[name], pair + 1, passed["dve"])
                    for a in range(2):
                        ins = dve.bn_aggr(mean_var[name][:, a, :], stats[name][:, a, :])
                    ins.then_inc(stat_done[name], 1)

                def normalize(src, name, dst, done):
                    for a in range(2):
                        ins = dve.tensor_scalar(dst[:, a, :], src[:, a, :], mean_var[name][:, a, 0:1], rstd[name][:, a:a + 1],
                                                ALU.subtract, ALU.mult)
                    ins.then_inc(done, 1)

                def head_shift(n, pair):
                    u = 4 * pair + n
                    s = head_scores[:, n % 2, :, :]
                    dve.wait_ge(qk_prod_done, u + 1)
                    if not isinstance(u, int) or u > 1:
                        dve.wait_ge(head_exp_done, u - 1)
                    if later(u):
                        dve.wait_ge(head_shifted, u)
                    dve.tensor_reduce(s, qk_prod[:, :, :, :], AX.X, ALU.add).then_inc(head_scores_done, 1)
                    dve.wait_ge(head_scores_done, u + 1)
                    dve.tensor_reduce(head_max[:, :], s, AX.X, ALU.max).then_inc(head_max_done, 1)
                    dve.wait_ge(head_max_done, u + 1)
                    dve.tensor_tensor(s, s, head_max[:, :].unsqueeze(2).to_broadcast([P, HH, H]),
                                      ALU.subtract).then_inc(head_shifted, 1)

                def head_output(n, pair):
                    u = 4 * pair + n
                    a, half = n // 2, n % 2
                    if later(u):
                        wait_apart(dve, head_out_done, u, passed["dve"])
                    dve.wait_ge(head_exp_done, u + 1)
                    dve.tensor_reduce(head_den[:, :], head_probs[:, n % 2, :, :], AX.X, ALU.add).then_inc(head_den_done, 1)
                    dve.wait_ge(head_den_done, 2 * u + 1)
                    dve.reciprocal(head_den[:, :], head_den[:, :]).then_inc(head_den_done, 1)
                    dve.wait_ge(pv_prod_done, u + 1)
                    dve.tensor_reduce(head_sum[:, :, :], pv_prod[:, :, :, :], AX.X, ALU.add).then_inc(head_sum_done, 1)
                    if n == 0 and later(pair):
                        dve.wait_ge(o1_stored, 32 * pair)
                    dve.wait_ge(head_den_done, 2 * u + 2)
                    dve.wait_ge(head_sum_done, u + 1)
                    dve.tensor_tensor(att_out[1][:, a, half * P:(half + 1) * P].rearrange("p (h d) -> p h d", h=HH),
                                      head_sum[:, :, :], head_den[:, :].unsqueeze(2).to_broadcast([P, HH, DH]),
                                      ALU.mult).then_inc(head_out_done, 1)

                def slot_max(n, pair):
                    g = 4 * pair + n
                    dve.wait_ge(scores_done, g + 1)
                    if not isinstance(g, int) or g > 1:
                        dve.wait_ge(exp_done, g - 1)
                    dve.tensor_reduce(neg_max[:, n % 2, :], scores[:, :].rearrange("p (h n) -> p h n", h=HH), AX.X,
                                      ALU.max, negate=True).then_inc(max_done, 1)

                def slot_lo(n, pair):
                    g = 4 * pair + n
                    dve.wait_ge(probs_hi_done, g + 1)
                    dve.tensor_tensor(probs_lo[:, :, :], probs_t[:, :].rearrange("p (h n) -> p h n", h=HH),
                                      probs_hi[:, :, :], ALU.subtract).then_inc(probs_lo_done, 1)

                def slot_out(n, pair, it, lag):
                    g = 4 * pair + n
                    a, half = n // 2, n % 2
                    dve.wait_ge(pv_done, g + 1)
                    if later(g):
                        dve.wait_ge(out_done, g)
                    if n == 0 and later(pair):
                        dve.wait_ge(work_ready[BANK["turn_o3"]], bank_count("turn_o3", it, lag + 1))
                    src = pv[:, 0:HH * VP].rearrange("p (h c) -> p h c", h=HH)
                    dve.reciprocal(rden[:, :].unsqueeze(2), src[:, :, VP - 1:VP])
                    dve.tensor_reduce(osum[:, :, :], src[:, :, 0:3 * DH].rearrange("p h (c d) -> p h d c", c=3), AX.X,
                                      ALU.add).then_inc(osum_done, 1)
                    dve.wait_ge(osum_done, g + 1)
                    dve.tensor_tensor(att_out[3][:, a, half * P:(half + 1) * P].rearrange("p (h d) -> p h d", h=HH),
                                      osum[:, :, :], rden[:, :].unsqueeze(2).to_broadcast([P, HH, DH]),
                                      ALU.mult).then_inc(out_done, 1)

                def step(job, pair, it, lag):
                    bank = work[BANK[job]] if job in BANK else None
                    read = work_read[BANK[job]] if job in BANK else None
                    if job.startswith("head_shift"):
                        head_shift(int(job[-1]), pair)
                    elif job.startswith("head_output"):
                        head_output(int(job[-1]), pair)
                    elif job.startswith("heads_out"):
                        slot_out(int(job[-1]), pair, it, lag)
                    elif job[:-1] == "max":
                        slot_max(int(job[-1]), pair)
                    elif job[:-1] == "lo":
                        slot_lo(int(job[-1]), pair)
                    elif job in ("x_lo", "ctx_lo"):
                        name, src = ("x", x_t) if job == "x_lo" else ("ctx", ctx_t)
                        dve.wait_ge(hi_done[name], pair + 1)
                        hi, lo = parts[name]
                        dve.tensor_tensor(lo[:, :, :], src[:, :, :], hi[:, :, :].bitcast(F32), ALU.subtract)\
                           .then_inc(lo_done[name], 1)
                    elif job in ("turn_o1", "turn_x1", "turn_cx", "turn_o3"):
                        src = {"turn_o1": "o1", "turn_x1": "x1", "turn_cx": "cx", "turn_o3": "o3"}[job]
                        dve.wait_ge(hi_done[job], pair + 1)
                        hi, lo = parts[src]
                        dve.tensor_tensor(lo[:, :, :], bank[:, :].rearrange("p (d n) -> p d n", d=DK),
                                          hi[:, :, :].bitcast(F32), ALU.subtract).then_inc(read, 1)
                    elif job == "turn_h":
                        dve.wait_ge(hi_done[job], pair + 1)
                        hi, lo = parts["h"]
                        for dk in range(DK):
                            ins = dve.scalar_tensor_tensor(out=lo[:, dk, :], in0=bank[:, dk * TOK:(dk + 1) * TOK],
                                                           scalar=norm1[:, dk:dk + 1], in1=hi[:, dk, :].bitcast(F32),
                                                           op0=ALU.mult, op1=ALU.subtract)
                        ins.then_inc(read, 1)
                    elif job in ("q3_0", "q3_1", "k3_0", "k3_1"):
                        m = int(job[3])
                        dve.wait_ge(hi_done[job], pair + 1)
                        src = bank[:, :].rearrange("p (g n) -> p g n", g=2)
                        rows = slice(P // 2, P) if job[0] == "q" else slice(0, P)
                        hi = (q_rows[3] if job[0] == "q" else k_parts[3][:, 0])[rows, 2 * m:2 * m + 2, :]
                        lo = hi if job[0] == "q" else k_parts[3][:, 1, 2 * m:2 * m + 2, :]
                        dve.tensor_tensor(lo, src[rows], hi.bitcast(F32), ALU.subtract).then_inc(read, 1)
                    elif job == "v3_rest":
                        dve.wait_ge(hi_done["v3"], pair + 1)
                        if later(pair):
                            dve.wait_ge(v_low_done, pair)
                        dve.tensor_tensor(v_rest[:, :, :], v_full[:, :, :], values[3][:, :, 0:DH],
                                          ALU.subtract).then_inc(v_rest_done, 1)
                    elif job == "v3_mid":
                        dve.wait_ge(v_mid_done, pair + 1)
                        dve.tensor_tensor(values[3][:, :, 2 * DH:3 * DH], v_rest[:, :, :],
                                          values[3][:, :, DH:2 * DH], ALU.subtract).then_inc(v_low_done, 1)
                    elif job == "out1":
                        dve.wait_ge(o1_loaded, 32 * (pair + 1))
                        residual_stats(job, "y1", y1, x_res, x1_done, pair, it, lag)
                    elif job == "norm_x1":
                        dve.wait_ge(rstd_done["y1"], pair + 1)
                        if later(pair):
                            dve.wait_ge(work_read[BANK["outx"]], bank_count("outx", it, lag + 1))
                            dve.wait_ge(work_ready[BANK["turn_x1"]], bank_count("turn_x1", it, lag + 1))
                        normalize(y1, "y1", x1, x1_done)
                    elif job == "outx":
                        dve.wait_ge(x1_done, pair + 1)
                        residual_stats(job, "z2", z2, x1, x2_done, pair, it, lag)
                    elif job == "norm_x2":
                        dve.wait_ge(rstd_done["z2"], pair + 1)
                        if later(pair):
                            dve.wait_ge(x2_stored, 16 * pair)
                            dve.wait_ge(h_done, pair)
                        normalize(z2, "z2", x2, x2_done)
                    elif job == "out3":
                        product_ready(job, it, lag)
                        dve.wait_ge(x2_res_loaded, 16 * (pair + 1))
                        if later(pair):
                            dve.wait_ge(h2_done, pair)
                            dve.wait_ge(sum_done, pair)
                        dve.tensor_tensor(x3[:, :, :], bank[:, :].rearrange("p (a n) -> p a n", a=2), x2_res[:, :, :],
                                          ALU.add).then_inc(read, 1)
                        if later(pair):
                            dve.wait_ge(sum_stored, 16 * pair)
                        dve.wait_ge(read, bank_count(job, it, lag))
                        dve.tensor_tensor(x2_x3[:, :, :], x3[:, :, :], x2_res[:, :, :], ALU.add).then_inc(sum_done, 1)
                    elif job == "sx":
                        product_ready(job, it, lag)
                        if later(pair):
                            dve.wait_ge(read, bank_count(job, it, lag + 1))
                        dve.tensor_reduce(neg_max_x[:, :], bank[:, 0:TOK].rearrange("p (a n) -> p a n", a=2), AX.X, ALU.max,
                                          negate=True).then_inc(max_x_done, 1)
                    elif job == "recip_x":
                        dve.wait_ge(work_read[BANK["sx"]], bank_count("sx", it, lag))
                        if later(pair):
                            dve.wait_ge(work_read[BANK["pvx"]], bank_count("pvx", it, lag + 1))
                        dve.reciprocal(rden_x[:, :], den_x[:, :]).then_inc(rden_x_done, 1)

                for_iterations(dve, step, SCHEDULE["dve"])

            @block.gpsimd
            def _(pool):
                pool.memset(half_power[:, :], -0.5).then_inc(power_set, 1)
                pool.wait_ge(const_loaded, 16 * CONSTS)
                pool.wait_ge(power_set, 1)
                pool.wait_ge(raw_lo_done, len(split_order) + 1)

                def wait(semaphore, value):
                    wait_apart(pool, semaphore, value, passed["pool"])

                def root(name, src, scale, eps, pair):
                    wait(stat_done[name], pair + 1)
                    pool.tensor_scalar(var_eps[name][:, :], src, scale, eps, ALU.mult, ALU.add).then_inc(eps_done[name], 1)
                    pool.wait_ge(eps_done[name], pair + 1)
                    pool.tensor_tensor(rstd[name][:, :], var_eps[name][:, :], half_power[:, :], ALU.pow)\
                        .then_inc(rstd_done[name], 1)

                def mask_slot(n, pair, it, lag):
                    g = 4 * pair + n
                    a, half = n // 2, n % 2
                    job = f"k3_{half}"
                    wait(work_read[BANK[job]], bank_count(job, it, lag))
                    if not isinstance(g, int) or g > 1:
                        wait(scores_done, g - 1)
                    for j in range(HG):
                        ins = pool.tensor_scalar(key_blocks[:, n % 2, 1, :, j, :],
                                                 k_parts[3][:, 1, 2 * half:2 * half + 2, a * S:(a + 1) * S].bitcast(F32),
                                                 head_mask[:, j:j + 1], 1.0, ALU.mult, ALU.mult)
                    ins.then_inc(mask_lo_done, 1)

                def qk_products(n, pair, it, lag):
                    u = 4 * pair + n
                    a, half = n // 2, n % 2
                    job = f"qk1_{a}"
                    wait(work_read[BANK[job]], bank_count(job, it, lag))
                    if later(u):
                        wait(head_scores_done, u)
                    q = qk1[:, a, half * P:(half + 1) * P].rearrange("p (h d) -> p h d", h=HH)
                    k = qk1[:, a, D:2 * D].rearrange("p (h d) -> p h d", h=H)
                    pool.tensor_tensor(qk_prod[:, :, :, :], q.unsqueeze(2).to_broadcast([P, HH, H, DH]),
                                       k.unsqueeze(1).to_broadcast([P, HH, H, DH]), ALU.mult).then_inc(qk_prod_done, 1)

                def pv_products(n, pair, it, lag):
                    u = 4 * pair + n
                    wait(work_read[BANK["v1"]], bank_count("v1", it, lag))
                    wait(head_exp_done, u + 1)
                    if later(u):
                        wait(head_sum_done, u)
                    v = v1[:, n // 2, :].rearrange("p (h d) -> p d h", h=H)
                    pool.tensor_tensor(pv_prod[:, :, :, :], head_probs[:, n % 2, :, :].unsqueeze(2).to_broadcast([P, HH, DH, H]),
                                       v.unsqueeze(1).to_broadcast([P, HH, DH, H]), ALU.mult).then_inc(pv_prod_done, 1)

                def step(job, pair, it, lag):
                    if job.startswith("mask"):
                        mask_slot(int(job[-1]), pair, it, lag)
                    elif job.startswith("qk_products"):
                        qk_products(int(job[-1]), pair, it, lag)
                    elif job.startswith("pv_products"):
                        pv_products(int(job[-1]), pair, it, lag)
                    elif job in ("root_y1", "root_z2"):
                        root(job[5:], mean_var[job[5:]][:, :, 1], 1.0, 1e-5, pair)
                    elif job in ("root_h", "root_h2"):
                        root(job[5:], squares[job[5:]][:, :], 1.0 / D, 1e-6, pair)

                for_iterations(pool, step, SCHEDULE["pool"])


def phase_b(nc, t, scratch, sem, out):
    ctx = ExitStack()
    NT = B
    TG = GT // P

    def sb(name, shape, dt=F32):
        return ctx.enter_context(nc.sbuf_tensor(name, shape, dt))

    with ctx:
        tok_hi = sb("tok_hi", [P, DK, B * S], F32R)
        tok_lo = sb("tok_lo", [P, DK, B * S], F32R)
        acc = sb("acc", [P, NT, D])
        WC = DK * DFF
        w_raw = sb("w_raw", [P, 3, WC])
        w_hi = sb("we_hi", [P, 2, 3, WC], F32R)
        w_lo = sb("we_lo", [P, 2, 3, WC], F32R)
        silu = sb("silu", [P, 2, GT])
        prod = sb("prod", [P, 2, GT])
        act_hi = sb("act_hi", [P, 2, FT, GT], F32R)
        act_lo = sb("act_lo", [P, 2, FT, GT], F32R)
        h_raw = [x[:, :, :] for x in (silu, prod)]
        combine = sb("combine", [P, NT, NE])
        logit = sb("logit_all", [P, NT, E])
        iota = sb("iota", [P, NT, E])
        pr = sb("pr", [P, NT, E])
        eq = sb("eq", [P, NT, E])
        one_hot = [sb(f"one_hot{i}", [P, NT, E]) for i in range(2)]
        rows = {n: sb(f"row_{n}", [P, NT]) for n in ("max", "sum", "top1", "top2", "at", "ratio", "den", "w1", "w2")}
        stats = sb("stats_b", [P, NT, 6])
        mean_var = sb("mean_var_b", [P, NT, 2])
        var_eps = sb("var_eps_b", [P, NT])
        rstd = sb("rstd_b", [P, NT])
        half_power = sb("half_power_b", [P, NT])

        gate = [ctx.enter_context(nc.psum_tensor(f"gate{i}", [P, GT], F32)) for i in range(2)]
        up = [ctx.enter_context(nc.psum_tensor(f"up{i}", [P, GT], F32)) for i in range(2)]
        down = [ctx.enter_context(nc.psum_tensor(f"down{i}", [P, 512], F32)) for i in range(4)]

        loaded, w_loaded = sem("b_loaded"), sem("w_loaded")
        h_loaded = [sem(f"h_loaded{i}") for i in range(2)]
        h_hi_done, h_lo_done = sem("h_hi_done"), sem("h_lo_done")
        w_hi_done, w_lo_done = sem("w_hi_done"), sem("w_lo_done")
        gate_up_ready, silu_done, prod_done = sem("gate_up_ready"), sem("silu_done"), sem("prod_done")
        act_hi_done, act_lo_done = sem("act_hi_done"), sem("act_lo_done")
        down_ready, down_added = sem("down_ready"), sem("down_added")
        passed_sp = sem("passed_sp_b")
        route, route_max, route_exp, ratio_ready, ratio_exp = (
            sem(n) for n in ("route", "route_max", "route_exp", "ratio_ready", "ratio_exp"))
        pool_own_b, var_done, rstd_b_done, norm_done, out_stored = (
            sem(n) for n in ("pool_own_b", "var_done", "rstd_b_done", "norm_done", "out_stored"))

        def experts(engine, body):
            body(0, 1, True, True)
            with engine.Fori(0, E // 2 - 1) as i:
                body(2 * i + 1, 0, False, True)
                body(2 * i + 2, 1, False, True)
            body(E - 1, 0, False, True)
            body(E, 1, False, False)

        with nc.Block() as block:

            @block.sync
            def _(sp):
                sp.dma_start(logit[:, :, :], scratch["logit"]).then_inc(loaded, 16)
                sp.dma_start(iota[:, :, :], t["iota"]).then_inc(loaded, 16)
                for k, n in enumerate(("w_gate", "w_up", "w_down")):
                    sp.dma_start(w_raw[:, k, :], t[n][0, :, :]).then_inc(w_loaded, 16)
                for g in range(NGT):
                    if g >= 2:
                        sp.wait_ge(h_lo_done, g - 1)
                    sp.dma_start(h_raw[g % 2], scratch["h2_t"][:, :, g * GT:(g + 1) * GT]).then_inc(h_loaded[g % 2], 16)
                    if g == 0:
                        sp.dma_start(acc[:, :, :], scratch["x2_x3"]).then_inc(loaded, 16)

                def expert(x, par, first, more):
                    if more:
                        wait_apart(sp, w_lo_done, 3 * (x + 1), passed_sp)
                        for k, n in enumerate(("w_gate", "w_up", "w_down")):
                            src = t[n][x + 1, :, :] if isinstance(x, int) else t[n][bass.ds(x + 1, 1), :, :].rearrange("a p n -> (a p) n")
                            sp.dma_start(w_raw[:, k, :], src).then_inc(w_loaded, 16)

                experts(sp, expert)
                for n in range(NGT):
                    sp.wait_ge(norm_done, n + 1)
                    sp.dma_start(out[:, n * TG:(n + 1) * TG, :], acc[:, n * TG:(n + 1) * TG, :]).then_inc(out_stored, 16)
                sp.wait_ge(out_stored, 16 * NGT)

            @block.tensor
            def _(pe):
                def piece(w, par, kind, i, c, n):
                    width = DFF if kind < 2 else D
                    return w[:, par, kind, i * width + c:i * width + c + n]

                def gate_up(x, par, g, f):
                    k = (x * NGT + g) * FT + f
                    if not isinstance(k, int) or k > 1:
                        pe.wait_ge(prod_done, k - 1)
                    for kind, bank in ((0, gate[f % 2]), (1, up[f % 2])):
                        n = 0
                        for wp, hp in ((w_hi, tok_hi), (w_hi, tok_lo), (w_lo, tok_hi)):
                            for dk in range(DK):
                                n += 1
                                mm = pe.matmul(bank[:, :], piece(wp, par, kind, dk, f * P, P),
                                               hp[:, dk, g * GT:(g + 1) * GT], start=(n == 1), stop=(n == 3 * DK))
                    mm.then_inc(gate_up_ready, 1)

                def down_tile(x, par, g, j):
                    step = x * NGT + g
                    if j == 0:
                        pe.wait_ge(act_lo_done, FT * (step + 1))
                    if not isinstance(step, int) or step > 0:
                        pe.wait_ge(down_added, FT * (step - 1) + j + 1)
                    n = 0
                    for ap, wp in ((act_hi, w_hi), (act_hi, w_lo), (act_lo, w_hi)):
                        for f in range(FT):
                            n += 1
                            mm = pe.matmul(down[j][:, 0:D], ap[:, g % 2, f, j * P:(j + 1) * P],
                                           piece(wp, par, 2, f, 0, D), start=(n == 1), stop=(n == 3 * FT))
                    mm.then_inc(down_ready, 1)

                def expert(x, par, first, more):
                    pe.wait_ge(w_lo_done, 3 * (x + 1))
                    for g in range(NGT):
                        if first:
                            pe.wait_ge(h_lo_done, g + 1)
                        last = None if first and g == 0 else (x, par, g - 1) if g else (x - 1, 1 - par, NGT - 1)
                        for f in range(FT):
                            gate_up(x, par, g, f)
                            if last:
                                for j in ((), (0,), (1,), (2, 3))[f]:
                                    down_tile(*last, j)

                experts(pe, expert)
                for j in range(TG):
                    down_tile(E, 1, NGT - 1, j)

            @block.scalar
            def _(act):
                def split_weights(x, par, k):
                    act.wait_ge(w_loaded, 48 * (x + 1))
                    act.activation(w_hi[:, par, k, :], w_raw[:, k, :], ACT.Copy).then_inc(w_hi_done, 1)

                for k in range(3):
                    split_weights(0, 1, k)
                for g in range(NGT):
                    act.wait_ge(h_loaded[g % 2], 16 * (g // 2 + 1))
                    act.activation(tok_hi[:, :, g * GT:(g + 1) * GT], h_raw[g % 2], ACT.Copy).then_inc(h_hi_done, 1)
                act.wait_ge(route_max, 1)
                act.activation(pr[:, :, :], logit[:, :, :], ACT.Exp).then_inc(route_exp, 1)
                act.wait_ge(ratio_ready, 1)
                act.activation(rows["ratio"][:, :], rows["ratio"][:, :], ACT.Exp).then_inc(ratio_exp, 1)
                act.wait_ge(h_lo_done, NGT)

                def expert(x, par, first, more):
                    for g in range(NGT):
                        step = x * NGT + g
                        for f in range(FT):
                            k = step * FT + f
                            act.wait_ge(gate_up_ready, k + 1)
                            act.activation(silu[:, f % 2, :], gate[f % 2][:, :], ACT.Silu).then_inc(silu_done, 1)
                            act.wait_ge(prod_done, k + 1)
                            if f == 0 and not (isinstance(step, int) and step < 2):
                                act.wait_ge(down_ready, TG * (step - 1))
                            act.activation(act_hi[:, g % 2, f, :], prod[:, f % 2, :], ACT.Copy).then_inc(act_hi_done, 1)
                        if more and 1 <= g <= 3:
                            if g == 1 and not (isinstance(x, int) and x == 0):
                                act.wait_ge(down_ready, TG * x * NGT)
                            split_weights(x + 1, 1 - par, g - 1)

                experts(act, expert)

            @block.vector
            def _(dve):
                own = [0]

                def step_of_route(instruction):
                    own[0] += 1
                    instruction.then_inc(route, 1)
                    dve.wait_ge(route, own[0])

                def low_weights(x, par, k):
                    dve.wait_ge(w_hi_done, 3 * x + k + 1)
                    dve.tensor_tensor(w_lo[:, par, k, :], w_raw[:, k, :], w_hi[:, par, k, :].bitcast(F32),
                                      ALU.subtract).then_inc(w_lo_done, 1)

                for k in range(3):
                    low_weights(0, 1, k)
                for g in range(NGT):
                    dve.wait_ge(h_hi_done, g + 1)
                    cols = slice(g * GT, (g + 1) * GT)
                    dve.tensor_tensor(tok_lo[:, :, cols], h_raw[g % 2], tok_hi[:, :, cols].bitcast(F32),
                                      ALU.subtract).then_inc(h_lo_done, 1)

                def wide(x):
                    return x[:, :].unsqueeze(2).to_broadcast([P, NT, E])

                dve.wait_ge(loaded, 48)
                step_of_route(dve.tensor_reduce(rows["max"][:, :], logit[:, :, :], AX.X, ALU.max))
                dve.tensor_tensor(logit[:, :, :], logit[:, :, :], wide(rows["max"]), ALU.subtract).then_inc(route_max, 1)
                dve.wait_ge(route_exp, 1)
                step_of_route(dve.tensor_reduce(rows["sum"][:, :], pr[:, :, :], AX.X, ALU.add))
                step_of_route(dve.reciprocal(rows["sum"][:, :], rows["sum"][:, :]))
                step_of_route(dve.tensor_tensor(pr[:, :, :], pr[:, :, :], wide(rows["sum"]), ALU.mult))
                for n, top in enumerate(("top1", "top2")):
                    step_of_route(dve.tensor_reduce(rows[top][:, :], pr[:, :, :], AX.X, ALU.max))
                    step_of_route(dve.tensor_tensor(eq[:, :, :], pr[:, :, :], wide(rows[top]), ALU.is_equal))
                    step_of_route(dve.scalar_tensor_tensor(out=eq[:, :, :], in0=eq[:, :, :], scalar=-float(E),
                                                           in1=iota[:, :, :], op0=ALU.mult, op1=ALU.add))
                    step_of_route(dve.tensor_reduce(rows["at"][:, :], eq[:, :, :], AX.X, ALU.min))
                    step_of_route(dve.tensor_tensor(one_hot[n][:, :, :], eq[:, :, :], wide(rows["at"]), ALU.is_equal))
                    if n == 0:
                        step_of_route(dve.scalar_tensor_tensor(out=pr[:, :, :], in0=one_hot[0][:, :, :], scalar=-2.0,
                                                               in1=pr[:, :, :], op0=ALU.mult, op1=ALU.add))
                dve.tensor_tensor(rows["ratio"][:, :], rows["top2"][:, :], rows["top1"][:, :], ALU.subtract)\
                   .then_inc(ratio_ready, 1)
                dve.wait_ge(ratio_exp, 1)
                step_of_route(dve.tensor_scalar(rows["den"][:, :], rows["ratio"][:, :], 1.0, None, ALU.add))
                step_of_route(dve.reciprocal(rows["w1"][:, :], rows["den"][:, :]))
                step_of_route(dve.tensor_tensor(rows["w2"][:, :], rows["ratio"][:, :], rows["w1"][:, :], ALU.mult))
                step_of_route(dve.tensor_tensor(one_hot[0][:, :, :], one_hot[0][:, :, :], wide(rows["w1"]), ALU.mult))
                step_of_route(dve.tensor_tensor(one_hot[1][:, :, :], one_hot[1][:, :, :], wide(rows["w2"]), ALU.mult))
                dve.memset(combine[:, :, 0:1], 1.0)
                step_of_route(dve.tensor_tensor(combine[:, :, 1:NE], one_hot[0][:, :, :], one_hot[1][:, :, :], ALU.add))

                def product(x, g, f):
                    k = (x * NGT + g) * FT + f
                    dve.wait_ge(silu_done, k + 1)
                    if not isinstance(k, int) or k > 1:
                        dve.wait_ge(act_lo_done, k - 1)
                    dve.tensor_tensor(prod[:, f % 2, :], silu[:, f % 2, :], up[f % 2][:, :], ALU.mult)\
                       .then_inc(prod_done, 1)

                def add_tile(x, g, j):
                    step = x * NGT + g
                    n = g * TG + j
                    dve.wait_ge(down_ready, TG * step + j + 1)
                    weight = combine[:, n, x:x + 1] if isinstance(x, int) else combine[:, n, bass.ds(x, 1)]
                    dve.scalar_tensor_tensor(out=acc[:, n, :], in0=down[j][:, 0:D], scalar=weight, in1=acc[:, n, :],
                                             op0=ALU.mult, op1=ALU.add).then_inc(down_added, 1)

                def expert(x, par, first, more):
                    for g in range(NGT):
                        last = None if first and g == 0 else (x, g - 1) if g else (x - 1, NGT - 1)
                        for f in range(FT):
                            product(x, g, f)
                            if last:
                                for j in ((), (0,), (1,), (2, 3))[f]:
                                    add_tile(*last, j)
                        if more and 1 <= g <= 3:
                            low_weights(x + 1, 1 - par, g - 1)

                experts(dve, expert)
                for j in range(TG):
                    add_tile(E, NGT - 1, j)
                dve.wait_ge(down_added, TG * NGT * NE)
                for n in range(NT):
                    ins = dve.bn_stats(stats[:, n, :], acc[:, n, :])
                step_of_route(ins)
                for n in range(NT):
                    ins = dve.bn_aggr(mean_var[:, n, :], stats[:, n, :])
                ins.then_inc(var_done, 1)
                dve.wait_ge(rstd_b_done, 1)
                for n in range(NT):
                    ins = dve.tensor_scalar(acc[:, n, :], acc[:, n, :], mean_var[:, n, 0:1], rstd[:, n:n + 1],
                                            ALU.subtract, ALU.mult)
                    if n % TG == TG - 1:
                        ins.then_inc(norm_done, 1)

            @block.gpsimd
            def _(pool):
                pool.memset(half_power[:, :], -0.5).then_inc(pool_own_b, 1)

                def expert(x, par, first, more):
                    for g in range(NGT):
                        for f in range(FT):
                            k = (x * NGT + g) * FT + f
                            pool.wait_ge(act_hi_done, k + 1)
                            pool.tensor_tensor(act_lo[:, g % 2, f, :], prod[:, f % 2, :],
                                               act_hi[:, g % 2, f, :].bitcast(F32), ALU.subtract).then_inc(act_lo_done, 1)

                experts(pool, expert)
                pool.wait_ge(var_done, 1)
                pool.tensor_scalar(var_eps[:, :], mean_var[:, :, 1], 1.0, 1e-5, ALU.mult, ALU.add).then_inc(pool_own_b, 1)
                pool.wait_ge(pool_own_b, 2)
                pool.tensor_tensor(rstd[:, :], var_eps[:, :], half_power[:, :], ALU.pow).then_inc(rstd_b_done, 1)


def decoder(nc, t, out):
    scratch = {
        "o1": nc.dram_tensor("o1_scratch", (B, S * D), F32, kind="Internal").ap(),
        "x2": nc.dram_tensor("x2_scratch", (P, B, D), F32, kind="Internal").ap(),
        "x2_x3": nc.dram_tensor("x2_x3_scratch", (P, B, D), F32, kind="Internal").ap(),
        "h2_t": nc.dram_tensor("h2_scratch", (P, DK, B * S), F32, kind="Internal").ap(),
        "logit": nc.dram_tensor("logit_scratch", (P, B, E), F32, kind="Internal").ap(),
    }
    with ExitStack() as ctx:
        def sem(name):
            return ctx.enter_context(nc.semaphore(name))

        phase_a(nc, t, scratch, sem)
        phase_b(nc, t, scratch, sem, out)


def layout(inputs):
    import numpy as np

    def a(name):
        return np.asarray(inputs[name])

    def rows(w):
        return np.ascontiguousarray(w.reshape(-1, P, w.shape[-1]).transpose(1, 0, 2))

    def twice(w):
        w = w.reshape(*w.shape[:-1], NG, HG * DH)
        return np.concatenate([w, w], -1).reshape(*w.shape[:-2], NG * P)

    def column(v):
        return np.ascontiguousarray(v.reshape(-1, P).T)

    def transposed(x):
        return rows(x.reshape(B * S, D).T)

    def experts(shared, routed):
        w = np.concatenate([a(shared)[None], a(routed)])
        return np.ascontiguousarray(np.stack([rows(x).reshape(P, -1) for x in w]))

    p = np.arange(P)
    return {
        "x": np.ascontiguousarray(a("x").transpose(1, 0, 2)),
        "x_t": transposed(a("x")),
        "ctx_t": transposed(a("ctx_1024")),
        "ident": np.eye(P, dtype=np.float32),
        "head_mask": (p[:, None] % (P // 2) // DH == np.arange(HG)).astype(np.float32),
        "iota": np.ascontiguousarray(np.broadcast_to(np.arange(E, dtype=np.float32), (P, B, E))),
        "wqk1": rows(np.concatenate([a("L0_attn_Wq"), a("L0_attn_Wk")]).T),
        "wv1": rows(a("L0_attn_Wv").T), "wo1": rows(a("L0_attn_Wo").T),
        "wkx": rows(a("L0_xattn_Wk").T), "wvx": rows(a("L0_xattn_Wv").T),
        "wqx": rows(a("L0_xattn_Wq").T), "wox": rows(a("L0_xattn_Wo").T),
        "wq3": rows(twice(a("L0_ffn_wq"))), "wk3": rows(twice(a("L0_ffn_wk"))),
        "wv3": rows(a("L0_ffn_wv")), "wo3": rows(a("L0_ffn_wo")),
        "bias_rows": np.stack([np.concatenate([a(n), a(m)]) for n, m in (("L0_attn_bq", "L0_attn_bk"), (
            "L0_attn_bv", "L0_attn_bo"), ("L0_xattn_bv", "L0_xattn_bo"))]),
        "select": np.repeat(np.eye(BIAS_ROWS, dtype=np.float32)[:, :, None], P, 2),
        "bias_qx": column(a("L0_xattn_bq")),
        "norm1": column(a("L0_ffn_norm1_w")), "norm2": column(a("L0_ffn_norm2_w")),
        "router": rows(a("L0_ffn_router_w")),
        "w_gate": experts("L0_ffn_sh_gate", "L0_ffn_e_gate"),
        "w_up": experts("L0_ffn_sh_up", "L0_ffn_e_up"),
        "w_down": experts("L0_ffn_sh_down", "L0_ffn_e_down"),
    }


def kernel(**inputs):
    import numpy as np
    import concourse.bacc as bacc
    from concourse.bass_utils import run_bass_kernel_spmd as run

    nc = bacc.Bacc("TRN2", target_bir_lowering=False, num_devices=1)
    arrays, t = {}, {}
    for name, x in layout(inputs).items():
        arrays[f"in_{name}"] = x
        t[name] = nc.dram_tensor(f"in_{name}", x.shape, mybir.dt.from_np(x.dtype), kind="ExternalInput").ap()
    out = nc.dram_tensor("out", (P, B, D), F32, kind="ExternalOutput").ap()
    decoder(nc, t, out)
    r = run(nc, [arrays], core_ids=[0])
    return np.ascontiguousarray(r.results[0]["out"].transpose(1, 0, 2))
```

```python
from contextlib import ExitStack

import concourse.bass as bass
from concourse import mybir

F32 = mybir.dt.float32
F32R = mybir.dt.float32r
BF16 = mybir.dt.bfloat16
FP16 = mybir.dt.float16
ALU = mybir.AluOpType
ACT = mybir.ActivationFunctionType
AX = mybir.AxisListType

P = 128
B, S, D = 32, 128, 256
H, DH = 16, 16
DK = D // P
PAIRS = B // 2
TOK = 2 * S
HG = 4
NG = H // HG
HH = H // 2
VP = 3 * DH + 1
E, DFF = 8, 512
FT = DFF // P
NE = E + 1
GT = 512
NGT = B * S // GT

SCHEDULE = {
    "sp": [("load_x", 0), ("store_sum", 5), ("load_x2", 4), ("store_h2", 5), ("store_logit", 5),
        ("load_o1", 1), ("load_ctx", 1), ("store_o1", 0), ("store_x2", 2)],
    "pe": [("slot3", 4), ("out3", 5), ("turn2", 4), ("values1", 4), ("turn_x1", 2), ("qk1_0", 0),
        ("qk1_1", 0), ("v1", 0), ("values2", 4), ("turn3", 4), ("qx", 2), ("sx", 2), ("values3", 4),
        ("turn_h2", 5), ("turn_px", 2), ("pvx", 2), ("turn_h", 3), ("turn_cx", 2), ("logits", 5),
        ("q3_0", 3), ("k3_0", 3), ("v3", 3), ("q3_1", 3), ("k3_1", 3), ("outx", 2), ("slot0", 3),
        ("turn_o1", 1), ("turn_o3", 4), ("turn0", 3), ("slot1", 3), ("out1", 1), ("kx", 1), ("slot2", 3),
        ("values0", 3), ("turn1", 3), ("vx", 1)],
    "act": [("hi1", 4), ("vx", 2), ("norm_h", 3), ("x_hi", 0), ("exp3", 4), ("turn_x1", 2), ("qk1_0", 0),
        ("hi2", 4), ("qk1_1", 0), ("square_h2", 5), ("v1", 0), ("hi3", 4), ("qx", 2), ("norm_h2", 5),
        ("head_exp0", 0), ("sx", 2), ("turn_px", 2), ("turn_h2", 5), ("pvx", 2), ("turn_h", 3),
        ("turn_cx", 2), ("head_exp1", 0), ("logits", 5), ("q3_0", 3), ("k3_0", 3), ("v3", 3), ("v3_hi", 3),
        ("q3_1", 3), ("head_exp2", 0), ("k3_1", 3), ("mask0", 3), ("v3_mid", 3), ("mask1", 3),
        ("turn_o1", 1), ("head_exp3", 0), ("mask2", 3), ("exp0", 3), ("ctx_hi", 1), ("turn_o3", 4),
        ("hi0", 3), ("mask3", 3), ("exp1", 3), ("kx", 1), ("square_h", 2), ("exp2", 3)],
    "dve": [("lo1", 4), ("max3", 4), ("out3", 5), ("heads_out1", 4), ("turn_x1", 2), ("lo2", 4),
        ("heads_out2", 4), ("head_shift0", 0), ("lo3", 4), ("sx", 2), ("heads_out3", 4), ("recip_x", 2),
        ("head_shift1", 0), ("turn_h", 3), ("turn_cx", 2), ("head_output0", 0), ("q3_0", 3), ("k3_0", 3),
        ("head_shift2", 0), ("q3_1", 3), ("v3_rest", 3), ("head_output1", 0), ("k3_1", 3), ("v3_mid", 3),
        ("head_shift3", 0), ("max0", 3), ("head_output2", 0), ("turn_o1", 1), ("outx", 2), ("max1", 3),
        ("turn_o3", 4), ("head_output3", 0), ("lo0", 3), ("max2", 3), ("heads_out0", 3), ("out1", 1)],
    "pool": [("root_y1", 2), ("norm_x1", 2), ("x_lo", 0), ("sum", 5), ("qk_products0", 0), ("root_h2", 5),
        ("qk_products1", 0), ("pv_products0", 0), ("qk_products2", 0), ("pv_products1", 0),
        ("qk_products3", 0), ("pv_products2", 0), ("pv_products3", 0), ("ctx_lo", 1), ("root_z2", 2),
        ("norm_x2", 2), ("root_h", 2)],
}
NW = 3
BANK = {
    "qk1_0": 0, "qk1_1": 1, "v1": 0, "turn_h": 0, "q3_0": 0, "k3_0": 1, "v3": 2, "q3_1": 0, "k3_1": 1,
    "turn_o1": 0, "out1": 0, "kx": 1, "vx": 1, "turn_x1": 2, "qx": 0, "sx": 0, "turn_px": 0, "pvx": 1,
    "turn_cx": 1, "outx": 2, "turn_o3": 1, "out3": 0, "turn_h2": 2, "logits": 2
}
LAG = {job: lag for job, lag in SCHEDULE["pe"]}
MAX_LAG = max(lag for steps in SCHEDULE.values() for _, lag in steps)
LOOP = (MAX_LAG + 1, PAIRS)


def active(lag, it):
    return not isinstance(it, int) or 0 <= it - lag < PAIRS


def bank_count(job, it, lag):
    back = lag - LAG[job]
    at = it - back
    n = 1
    seen = False
    for j, l in SCHEDULE["pe"]:
        if j == job:
            seen = True
        if BANK.get(j) == BANK[job]:
            if isinstance(it, int):
                n = n + max(0, min(PAIRS, at - l)) + (not seen and active(l, at))
            else:
                assert LOOP[0] - back - l >= 0 and LOOP[1] - back - l <= PAIRS, (job, j)
                n = n + (at - l) + (not seen)
    return n


def later(pair):
    return not isinstance(pair, int) or pair > 0


def for_iterations(engine, step, schedule, rest_after=None, rest=None):
    def body(it):
        for job, lag in schedule:
            if active(lag, it):
                step(job, it - lag, it, lag)
            if job == rest_after and isinstance(it, int) and it == 0:
                rest()

    for it in range(LOOP[0]):
        body(it)
    with engine.Fori(LOOP[0], LOOP[1]) as it:
        body(it)
    for it in range(LOOP[1], PAIRS + MAX_LAG):
        body(it)


def wait_apart(engine, semaphore, value, passed):
    engine.wait_ge(semaphore, value)
    if not isinstance(value, int):
        engine.sem_inc(passed, 1)


BIAS_ROWS = 3
BIAS_OF = {"qk1": (0, 0), "v1": (1, 0), "o1": (1, D), "vx": (2, 0), "ox": (2, D)}


def phase_a(nc, t, scratch, sem):
    ctx = ExitStack()

    def sb(name, shape, dt=F32):
        return ctx.enter_context(nc.sbuf_tensor(name, shape, dt))

    with ctx:
        ident = sb("ident", [P, P])
        head_mask = sb("head_mask", [P, HG])
        half_power = sb("half_power", [P, 2])
        bias_hi = sb("bias_hi", [BIAS_ROWS, 2 * D], F32R)
        bias_lo = sb("bias_lo", [BIAS_ROWS, 2 * D], F32R)
        select = sb("select", [BIAS_ROWS, BIAS_ROWS, P], F32R)
        bias_qx = sb("bias_qx", [P, DK])
        norm1 = sb("norm1", [P, DK])
        norm2 = sb("norm2", [P, DK])
        router = sb("router", [P, DK, E])
        QW = NG * P
        widths = {"wqk1": 2 * D, "wv1": D, "wo1": D, "wkx": D, "wvx": D, "wqx": D, "wox": D,
                  "wq3": QW, "wk3": QW, "wv3": D, "wo3": D}
        scales = {"wq3": DH ** -0.5, "wqx": D ** -0.5}
        w_hi = {n: sb(f"{n}_hi", [P, DK, w], F32R) for n, w in widths.items()}
        w_lo = {n: sb(f"{n}_lo", [P, DK, w], F32R) for n, w in widths.items()}

        key_blocks = sb("key_blocks", [P, 2, 2, 2, HG, S], F32R)
        probs = sb("probs", [P, 2, HH, S])
        probs_hi = sb("probs_hi", [P, HH, S], FP16)
        probs_lo = sb("probs_lo", [P, HH, S], FP16)
        neg_max = sb("neg_max", [P, 2, HH])
        rden = sb("rden", [P, HH])
        osum = sb("osum", [P, HH, DH])
        v_full = sb("v_full", [P, 2 * H, DH])
        v_rest = sb("v_rest", [P, 2 * H, DH])
        qk1 = sb("qk1", [P, 2, 2 * D])
        v1 = sb("v1", [P, 2, D])
        qk_prod = sb("qk_prod", [P, HH, H, DH])
        pv_prod = sb("pv_prod", [P, HH, H, DH])
        head_scores = sb("head_scores", [P, 2, HH, H])
        head_probs = sb("head_probs", [P, 2, HH, H])
        head_max = sb("head_max", [P, HH])
        head_den = sb("head_den", [P, HH])
        head_sum = sb("head_sum", [P, HH, DH])
        o1_rows = sb("o1_rows", [P, 2, D])
        q_rows = {s: sb(f"q_rows{s}", [P, NG, TOK], F32R) for s in (3,)}
        k_parts = {s: sb(f"k_parts{s}", [P, 2, NG, TOK], F32R) for s in (3,)}
        values = {s: sb(f"values{s}", [P, 2 * H, VP], BF16) for s in (3,)}
        att_out = {s: sb(f"att_out{s}", [P, 2, D]) for s in (1, 3)}
        x_t = sb("x_t", [P, DK, TOK])
        ctx_t = sb("ctx_t", [P, DK, TOK])
        parts = {n: (sb(f"{n}_hi", [P, DK, TOK], F32R), sb(f"{n}_lo", [P, DK, TOK], F32R))
                 for n in ("x", "ctx", "o1", "x1", "cx", "h", "o3")}
        x_res = sb("x_res", [P, 2, D])
        y1 = sb("y1", [P, 2, D])
        x1 = sb("x1", [P, 2, D])
        z2 = sb("z2", [P, 2, D])
        x2 = sb("x2", [P, 2, D])
        h_in = sb("h_in", [P, 2, D])
        x2_res = sb("x2_res", [P, 2, D])
        x3 = sb("x3", [P, 2, D])
        x2_x3 = sb("x2_x3", [P, 2, D])
        h2_in = sb("h2_in", [P, 2, D])
        h2_t = sb("h2_t", [P, DK, TOK])
        logit = sb("logit", [P, 2, E])
        kx_t = sb("kx_t", [P, DK, TOK])
        qx_t = sb("qx_t", [P, DK, TOK])
        vx = sb("vx", [P, 2, D])
        px = sb("px", [P, 2, S])
        px_t = sb("px_t", [P, 2, S])
        cx = sb("cx", [P, 2, D])
        neg_max_x = sb("neg_max_x", [P, 2])
        den_x = sb("den_x", [P, 2])
        rden_x = sb("rden_x", [P, 2])
        stats = {n: sb(f"stats_{n}", [P, 2, 6]) for n in ("y1", "z2")}
        mean_var = {n: sb(f"mean_var_{n}", [P, 2, 2]) for n in ("y1", "z2")}
        var_eps = {n: sb(f"var_eps_{n}", [P, 2]) for n in ("y1", "z2", "h", "h2")}
        rstd = {n: sb(f"rstd_{n}", [P, 2]) for n in ("y1", "z2", "h", "h2")}
        squares = {n: sb(f"squares_{n}", [P, 2]) for n in ("h", "h2")}
        square_out = sb("square_out", [P, 2, D])
        raw = {n: probs[:, i, :, :].rearrange("p h n -> p (h n)").rearrange("p (d n) -> p d n", d=DK)
               for i, n in enumerate("ab")}

        raw_bias = qk_prod[0:BIAS_ROWS, :, :, :].rearrange("p h k d -> p (h k d)")[:, 0:2 * D]
        raw_select = pv_prod[0:BIAS_ROWS, :, :, :].rearrange("p h k d -> p (h k d)")[:, 0:BIAS_ROWS * P]\
            .rearrange("p (r n) -> p r n", r=BIAS_ROWS)

        scores = ctx.enter_context(nc.psum_tensor("scores", [P, HH * S], F32))
        probs_t = ctx.enter_context(nc.psum_tensor("probs_t", [P, HH * S], F32))
        pv = ctx.enter_context(nc.psum_tensor("pv", [P, 512], F32))
        work = [ctx.enter_context(nc.psum_tensor(f"work{i}", [P, 512], F32)) for i in range(NW)]

        const_loaded = sem("const_loaded")
        raw_loaded = {n: sem(f"raw_loaded_{n}") for n in raw}
        raw_hi_done, raw_lo_done = sem("raw_hi_done"), sem("raw_lo_done")
        bias_scaled = sem("bias_scaled")
        ones_set = sem("ones_set")
        x_loaded, ctx_loaded = sem("x_loaded"), sem("ctx_loaded")
        x2_res_loaded = sem("x2_res_loaded")
        x2_stored, sum_stored, h2_stored, logit_stored = (sem(n) for n in ("x2_stored", "sum_stored", "h2_stored", "logit_stored"))
        work_ready = [sem(f"work_ready{i}") for i in range(NW)]
        work_read = [sem(f"work_read{i}") for i in range(NW)]
        hi_done = {j: sem(f"hi_done_{j}") for j in
                   ("q3_0", "q3_1", "k3_0", "k3_1", "v3",
                    "turn_o1", "turn_x1", "turn_cx", "turn_h", "turn_o3", "x", "ctx")}
        lo_done = {j: sem(f"lo_done_{j}") for j in ("x", "ctx")}
        v_low_done = sem("v_low_done")
        v_rest_done = sem("v_rest_done")
        v_mid_done = sem("v_mid_done")
        qk_prod_done = sem("qk_prod_done")
        head_scores_done = sem("head_scores_done")
        head_max_done = sem("head_max_done")
        head_shifted = sem("head_shifted")
        head_exp_done = sem("head_exp_done")
        head_den_done = sem("head_den_done")
        pv_prod_done = sem("pv_prod_done")
        head_sum_done = sem("head_sum_done")
        head_out_done = sem("head_out_done")
        o1_stored, o1_loaded = sem("o1_stored"), sem("o1_loaded")
        mask_done = sem("mask_done")
        scores_done = sem("scores_done")
        max_done = sem("max_done")
        exp_done = sem("exp_done")
        turned = sem("turned")
        probs_hi_done = sem("probs_hi_done")
        probs_lo_done = sem("probs_lo_done")
        pv_done = sem("pv_done")
        out_done = sem("out_done")
        stat_done = {n: sem(f"stat_done_{n}") for n in rstd}
        stats_done = {n: sem(f"stats_done_{n}") for n in stats}
        eps_done = {n: sem(f"eps_done_{n}") for n in rstd}
        rstd_done = {n: sem(f"rstd_done_{n}") for n in rstd}
        x1_done, x2_done, sum_done = sem("x1_done"), sem("x2_done"), sem("sum_done")
        h_done, h2_done = sem("h_done"), sem("h2_done")
        max_x_done, rden_x_done = sem("max_x_done"), sem("rden_x_done")
        osum_done = sem("osum_done")
        power_set = sem("power_set")
        passed = {n: sem(f"passed_{n}") for n in ("sp", "dve", "pool")}

        CONSTS = 8

        split_order = list(widths)
        FIRST = 2
        split_buffer = {n: "ab"[i % 2] for i, n in enumerate(split_order)}

        with nc.Block() as block:

            @block.sync
            def _(sp):
                def load_weights(which):
                    for i in which:
                        n = split_order[i]
                        b = split_buffer[n]
                        if i >= FIRST:
                            sp.wait_ge(raw_lo_done, i)
                        sp.dma_start(raw[b][:, :, 0:widths[n]], t[n]).then_inc(raw_loaded[b], 16)

                load_weights(range(FIRST))
                consts = [(ident, "ident"), (head_mask, "head_mask"), (bias_qx, "bias_qx"), (norm1, "norm1"),
                          (norm2, "norm2")]
                for dst, name in consts:
                    sp.dma_start(dst[:, :], t[name]).then_inc(const_loaded, 16)
                sp.dma_start(router[:, :, :], t["router"]).then_inc(const_loaded, 16)
                sp.dma_start(raw_bias, t["bias_rows"]).then_inc(const_loaded, 16)
                sp.dma_start(raw_select, t["select"]).then_inc(const_loaded, 16)
                o1_write = scratch["o1"].rearrange("b (h s d) -> s b h d", h=H, s=S)
                o1_read = scratch["o1"].rearrange("b (s e) -> s b e", s=S)

                def wait(semaphore, value):
                    wait_apart(sp, semaphore, value, passed["sp"])

                def step(job, pair, it, lag):
                    rows = bass.ds(2 * pair, 2)
                    if job == "load_x":
                        if later(pair):
                            wait(lo_done["x"], pair)
                        sp.dma_start(x_t[:, :, :], t["x_t"][:, :, bass.ds(TOK * pair, TOK)]).then_inc(x_loaded, 16)
                    elif job == "store_o1":
                        wait(head_out_done, 4 * (pair + 1))
                        for a in range(2):
                            sp.dma_start(o1_write[:, bass.ds(2 * pair + a, 1), :, :].rearrange("s b h d -> s (b h) d"),
                                         att_out[1][:, a, :].rearrange("p (h d) -> p h d", h=H)).then_inc(o1_stored, 16)
                    elif job == "load_o1":
                        if later(pair):
                            wait(stat_done["y1"], pair)
                        sp.dma_start(x_res[:, :, :], t["x"][:, rows, :]).then_inc(o1_loaded, 16)
                        wait(o1_stored, 32 * (pair + 1))
                        sp.dma_start(o1_rows[:, :, :], o1_read[:, rows, :]).then_inc(o1_loaded, 16)
                    elif job == "load_ctx":
                        if later(pair):
                            wait(lo_done["ctx"], pair)
                        sp.dma_start(ctx_t[:, :, :], t["ctx_t"][:, :, bass.ds(TOK * pair, TOK)]).then_inc(ctx_loaded, 16)
                    elif job == "load_x2":
                        if later(pair):
                            wait(sum_done, pair)
                        wait(x2_stored, 16 * (pair + 1))
                        sp.dma_start(x2_res[:, :, :], scratch["x2"][:, rows, :]).then_inc(x2_res_loaded, 16)
                    elif job == "store_x2":
                        wait(x2_done, pair + 1)
                        sp.dma_start(scratch["x2"][:, rows, :], x2[:, :, :]).then_inc(x2_stored, 16)
                    elif job == "store_sum":
                        wait(sum_done, pair + 1)
                        sp.dma_start(scratch["x2_x3"][:, rows, :], x2_x3[:, :, :]).then_inc(sum_stored, 16)
                    elif job == "store_h2":
                        wait(work_read[BANK["turn_h2"]], bank_count("turn_h2", it, lag))
                        sp.dma_start(scratch["h2_t"][:, :, bass.ds(TOK * pair, TOK)], h2_t[:, :, :]).then_inc(h2_stored, 16)
                    elif job == "store_logit":
                        wait(work_read[BANK["logits"]], bank_count("logits", it, lag))
                        sp.dma_start(scratch["logit"][:, rows, :], logit[:, :, :]).then_inc(logit_stored, 16)

                for_iterations(sp, step, SCHEDULE["sp"], "load_x", lambda: load_weights(range(FIRST, len(split_order))))
                for s in (x2_stored, sum_stored, h2_stored, logit_stored):
                    sp.wait_ge(s, 16 * PAIRS)

            @block.tensor
            def _(pe):
                def split_products(out, lhs, rhs, bias=None):
                    (lh, ll), (rh, rl) = lhs, rhs
                    n = 0
                    for a, b in ((lh, rh), (lh, rl), (ll, rh)):
                        for dk in range(DK):
                            n += 1
                            mm = pe.matmul(out, a(dk), b(dk), start=(n == 1), stop=(n == 3 * DK and not bias))
                    if bias:
                        row, c = BIAS_OF[bias]
                        width = out.shape[-1]
                        for part in (bias_hi, bias_lo):
                            mm = pe.matmul(out, select[:, row, :], part[:, c:c + width], start=False, stop=(part is bias_lo))
                    return mm

                def to_rows(bank, weight, m0, source):
                    for m in range(2):
                        c = (m0 + m) * P
                        mm = split_products(bank[:, m * TOK:(m + 1) * TOK],
                                            [lambda dk, w=w: w[weight][:, dk, c:c + P] for w in (w_hi, w_lo)],
                                            [lambda dk, x=x: x[:, dk, :] for x in parts[source]])
                    return mm

                def to_tokens(bank, weight, source, bias=None):
                    for a in range(2):
                        mm = split_products(bank[:, a * D:(a + 1) * D],
                                            [lambda dk, x=x: x[:, dk, a * S:(a + 1) * S] for x in parts[source]],
                                            [lambda dk, w=w: w[weight][:, dk, :] for w in (w_hi, w_lo)], bias)
                    return mm

                def turn(bank, src):
                    for dk in range(DK):
                        for a in range(2):
                            mm = pe.transpose(bank[:, dk * TOK + a * S:dk * TOK + (a + 1) * S],
                                              src[:, a, dk * P:(dk + 1) * P], ident[:, :])
                    return mm

                def slot_scores(n, pair, it, lag):
                    g = 4 * pair + n
                    a, half = n // 2, n % 2
                    pe.wait_ge(mask_done, g + 1)
                    job = f"q3_{half}"
                    pe.wait_ge(work_read[BANK[job]], bank_count(job, it, lag))
                    if later(g):
                        pe.wait_ge(exp_done, g)
                    for j in range(2):
                        for part in range(2):
                            mm = pe.matmul(scores[:, j * HG * S:(j + 1) * HG * S],
                                           q_rows[3][:, 2 * half + j, a * S:(a + 1) * S],
                                           key_blocks[:, n % 2, part, j, :, :], start=(part == 0), stop=(part == 1))
                    mm.then_inc(scores_done, 1)

                def slot_turn(n, pair):
                    g = 4 * pair + n
                    pe.wait_ge(exp_done, g + 1)
                    if later(g):
                        pe.wait_ge(probs_lo_done, g)
                    for h in range(HH):
                        mm = pe.transpose(probs_t[:, h * S:(h + 1) * S], probs[:, n % 2, h, :], ident[:, :])
                    mm.then_inc(turned, 1)

                def slot_values(n, pair):
                    g = 4 * pair + n
                    a, half = n // 2, n % 2
                    pe.wait_ge(probs_lo_done, g + 1)
                    pe.wait_ge(v_low_done, pair + 1)
                    if later(g):
                        pe.wait_ge(out_done, g)
                    for h in range(HH):
                        v = values[3][:, a * H + half * HH + h, :]
                        pe.matmul(pv[:, h * VP:(h + 1) * VP], probs_hi[:, h, :], v, start=True, stop=False)
                        mm = pe.matmul(pv[:, h * VP:(h + 1) * VP], probs_lo[:, h, :], v, start=False, stop=True)
                    mm.then_inc(pv_done, 1)

                def work_job(job, pair, it, lag):
                    bank = work[BANK[job]]

                    def wait_read(other):
                        pe.wait_ge(work_read[BANK[other]], bank_count(other, it, lag))

                    uses = bank_count(job, it, lag) - 1
                    if not isinstance(uses, int) or uses > 0:
                        pe.wait_ge(work_read[BANK[job]], uses)
                    if job in ("qk1_0", "qk1_1"):
                        a = int(job[4])
                        pe.wait_ge(lo_done["x"], pair + 1)
                        mm = split_products(bank[:, :],
                                            [lambda dk, x=x: x[:, dk, a * S:(a + 1) * S] for x in parts["x"]],
                                            [lambda dk, w=w: w["wqk1"][:, dk, :] for w in (w_hi, w_lo)], "qk1")
                    elif job == "v1":
                        pe.wait_ge(lo_done["x"], pair + 1)
                        mm = to_tokens(bank, "wv1", "x", "v1")
                    elif job in ("q3_0", "q3_1", "k3_0", "k3_1"):
                        wait_read("turn_h")
                        mm = to_rows(bank, "w" + job[:2], 2 * int(job[3]), "h")
                    elif job == "v3":
                        wait_read("turn_h")
                        mm = to_tokens(bank, "wv3", "h")
                    elif job == "turn_o1":
                        pe.wait_ge(o1_loaded, 32 * (pair + 1))
                        mm = turn(bank, o1_rows)
                    elif job == "out1":
                        wait_read("turn_o1")
                        mm = to_tokens(bank, "wo1", "o1", "o1")
                    elif job == "turn_x1":
                        pe.wait_ge(x1_done, pair + 1)
                        mm = turn(bank, x1)
                    elif job == "kx":
                        pe.wait_ge(lo_done["ctx"], pair + 1)
                        mm = to_rows(bank, "wkx", 0, "ctx")
                    elif job == "vx":
                        pe.wait_ge(lo_done["ctx"], pair + 1)
                        mm = to_tokens(bank, "wvx", "ctx", "vx")
                    elif job == "qx":
                        wait_read("turn_x1")
                        mm = to_rows(bank, "wqx", 0, "x1")
                    elif job == "sx":
                        wait_read("kx")
                        wait_read("qx")
                        for a in range(2):
                            for dk in range(DK):
                                mm = pe.matmul(bank[:, a * S:(a + 1) * S], qx_t[:, dk, a * S:(a + 1) * S],
                                               kx_t[:, dk, a * S:(a + 1) * S], start=(dk == 0), stop=(dk == DK - 1))
                    elif job == "turn_px":
                        wait_read("sx")
                        for a in range(2):
                            mm = pe.transpose(bank[:, a * S:(a + 1) * S], px[:, a, :], ident[:, :])
                    elif job == "pvx":
                        wait_read("turn_px")
                        wait_read("vx")
                        for a in range(2):
                            mm = pe.matmul(bank[:, a * D:(a + 1) * D], px_t[:, a, :], vx[:, a, :], start=True, stop=True)
                    elif job == "turn_cx":
                        wait_read("pvx")
                        mm = turn(bank, cx)
                    elif job == "outx":
                        wait_read("turn_cx")
                        mm = to_tokens(bank, "wox", "cx", "ox")
                    elif job == "turn_h":
                        pe.wait_ge(h_done, pair + 1)
                        mm = turn(bank, h_in)
                    elif job == "turn_o3":
                        pe.wait_ge(out_done, 4 * (pair + 1))
                        mm = turn(bank, att_out[3])
                    elif job == "out3":
                        wait_read("turn_o3")
                        mm = to_tokens(bank, "wo3", "o3")
                    elif job == "turn_h2":
                        pe.wait_ge(h2_done, pair + 1)
                        mm = turn(bank, h2_in)
                    elif job == "logits":
                        wait_read("turn_h2")
                        for a in range(2):
                            for dk in range(DK):
                                mm = pe.matmul(bank[:, a * E:(a + 1) * E], h2_t[:, dk, a * S:(a + 1) * S],
                                               router[:, dk, :], start=(dk == 0), stop=(dk == DK - 1))
                    mm.then_inc(work_ready[BANK[job]], 1)

                pe.wait_ge(const_loaded, 16 * CONSTS)
                pe.wait_ge(raw_lo_done, FIRST + 1)
                pe.wait_ge(ones_set, 1)

                def step(job, pair, it, lag):
                    if job.startswith("slot"):
                        slot_scores(int(job[4]), pair, it, lag)
                    elif job in ("turn0", "turn1", "turn2", "turn3"):
                        slot_turn(int(job[4]), pair)
                    elif job.startswith("values"):
                        slot_values(int(job[6]), pair)
                    else:
                        work_job(job, pair, it, lag)

                def rest_split():
                    pe.wait_ge(raw_lo_done, len(split_order) + 1)

                for_iterations(pe, step, SCHEDULE["pe"], SCHEDULE["pe"][-1][0], rest_split)

            @block.scalar
            def _(act):
                act.wait_ge(const_loaded, 16 * CONSTS)
                act.mul(bias_qx[:, :], bias_qx[:, :], D ** -0.5).then_inc(bias_scaled, 1)
                act.wait_ge(bias_scaled, 1)
                def split_weights(which):
                    for i in which:
                        n = split_order[i]
                        b = split_buffer[n]
                        act.wait_ge(raw_loaded[b], 16 * (i // 2 + 1))
                        act.activation(w_hi[n][:, :, :], raw[b][:, :, 0:widths[n]], ACT.Copy,
                                       scale=scales.get(n, 1.0)).then_inc(raw_hi_done, 1)

                split_weights(range(FIRST))
                act.activation(select[:, :, :], raw_select, ACT.Copy)
                act.activation(bias_hi[:, :], raw_bias, ACT.Copy).then_inc(raw_hi_done, 1)

                def split_rest():
                    split_weights(range(FIRST, len(split_order)))
                    act.wait_ge(raw_lo_done, len(split_order) + 1)

                def product_ready(job, it, lag):
                    act.wait_ge(work_ready[BANK[job]], bank_count(job, it, lag))

                def last_used(job, pair, it, lag):
                    if later(pair):
                        act.wait_ge(work_ready[BANK[job]], bank_count(job, it, lag + 1))

                def slot_step(kind, n, pair, it, lag):
                    g = 4 * pair + n
                    a, half = n // 2, n % 2
                    if kind == "mask":
                        act.wait_ge(work_read[BANK[f"k3_{half}"]], bank_count(f"k3_{half}", it, lag))
                        if not isinstance(g, int) or g > 1:
                            act.wait_ge(scores_done, g - 1)
                        for j in range(HG):
                            ins = act.activation(key_blocks[:, n % 2, :, :, j, :],
                                                 k_parts[3][:, :, 2 * half:2 * half + 2, a * S:(a + 1) * S].bitcast(F32),
                                                 ACT.Copy, scale=head_mask[:, j:j + 1])
                        ins.then_inc(mask_done, 1)
                    elif kind == "exp":
                        act.wait_ge(max_done, g + 1)
                        if not isinstance(g, int) or g > 1:
                            act.wait_ge(turned, g - 1)
                        for h in range(HH):
                            ins = act.activation(probs[:, n % 2, h, :], scores[:, h * S:(h + 1) * S], ACT.Exp,
                                                 bias=neg_max[:, n % 2, h:h + 1])
                        ins.then_inc(exp_done, 1)
                    elif kind == "hi":
                        act.wait_ge(turned, g + 1)
                        if later(g):
                            act.wait_ge(pv_done, g)
                        act.activation(probs_hi[:, :, :], probs_t[:, :].rearrange("p (h n) -> p h n", h=HH),
                                       ACT.Copy).then_inc(probs_hi_done, 1)

                def step(job, pair, it, lag):
                    bank = work[BANK[job]] if job in BANK else None
                    read = work_read[BANK[job]] if job in BANK else None
                    if job[:-1] in ("mask", "exp", "hi"):
                        slot_step(job[:-1], int(job[-1]), pair, it, lag)
                    elif job in ("x_hi", "ctx_hi"):
                        name, src, loaded, users = (("x", x_t, x_loaded, ("qk1_0", "qk1_1", "v1")) if job == "x_hi" else
                                                    ("ctx", ctx_t, ctx_loaded, ("kx", "vx")))
                        act.wait_ge(loaded, 16 * (pair + 1))
                        for user in users:
                            last_used(user, pair, it, lag)
                        act.activation(parts[name][0][:, :, :], src[:, :, :], ACT.Copy).then_inc(hi_done[name], 1)
                    elif job in ("qk1_0", "qk1_1"):
                        a = int(job[4])
                        product_ready(job, it, lag)
                        if later(pair):
                            act.wait_ge(qk_prod_done, 4 * pair - 2 + 2 * a)
                        act.activation(qk1[:, a, :], bank[:, :], ACT.Copy).then_inc(read, 1)
                    elif job == "v1":
                        product_ready(job, it, lag)
                        if later(pair):
                            act.wait_ge(pv_prod_done, 4 * pair)
                        act.activation(v1[:, :, :], bank[:, :].rearrange("p (a n) -> p a n", a=2), ACT.Copy).then_inc(read, 1)
                    elif job.startswith("head_exp"):
                        n = int(job[8])
                        u = 4 * pair + n
                        act.wait_ge(head_shifted, u + 1)
                        if not isinstance(u, int) or u > 1:
                            act.wait_ge(head_out_done, u - 1)
                        act.activation(head_probs[:, n % 2, :, :], head_scores[:, n % 2, :, :], ACT.Exp,
                                       scale=DH ** -0.5).then_inc(head_exp_done, 1)
                    elif job in ("turn_o1", "turn_x1", "turn_cx", "turn_o3"):
                        src, user = {"turn_o1": ("o1", "out1"), "turn_x1": ("x1", "qx"), "turn_cx": ("cx", "outx"),
                                     "turn_o3": ("o3", "out3")}[job]
                        product_ready(job, it, lag)
                        last_used(user, pair, it, lag)
                        act.activation(parts[src][0][:, :, :], bank[:, :].rearrange("p (d n) -> p d n", d=DK),
                                       ACT.Copy).then_inc(hi_done[job], 1)
                    elif job in ("q3_0", "q3_1", "k3_0", "k3_1"):
                        m = int(job[3])
                        product_ready(job, it, lag)
                        if later(pair):
                            act.wait_ge(scores_done, 4 * pair - 1 + m)
                        dst = q_rows[3] if job[0] == "q" else k_parts[3][:, 0]
                        act.activation(dst[:, 2 * m:2 * m + 2, :], bank[:, :].rearrange("p (g n) -> p g n", g=2),
                                       ACT.Copy).then_inc(hi_done[job], 1)
                    elif job == "v3":
                        product_ready(job, it, lag)
                        if later(pair):
                            act.wait_ge(v_rest_done, pair)
                        act.activation(v_full[:, :, :].rearrange("p (a h) d -> p a (h d)", a=2),
                                       bank[:, :].rearrange("p (a n) -> p a n", a=2), ACT.Copy).then_inc(read, 1)
                    elif job == "v3_hi":
                        act.wait_ge(work_read[BANK["v3"]], bank_count("v3", it, lag))
                        if later(pair):
                            act.wait_ge(pv_done, 4 * pair)
                        act.activation(values[3][:, :, 0:DH], v_full[:, :, :], ACT.Copy).then_inc(hi_done["v3"], 1)
                    elif job == "v3_mid":
                        act.wait_ge(v_rest_done, pair + 1)
                        act.activation(values[3][:, :, DH:2 * DH], v_rest[:, :, :], ACT.Copy).then_inc(v_mid_done, 1)
                    elif job == "turn_h":
                        product_ready(job, it, lag)
                        for user in ("q3_0", "q3_1", "k3_0", "k3_1", "v3"):
                            last_used(user, pair, it, lag)
                        for dk in range(DK):
                            ins = act.activation(parts["h"][0][:, dk, :], bank[:, dk * TOK:(dk + 1) * TOK], ACT.Copy,
                                                 scale=norm1[:, dk:dk + 1])
                        ins.then_inc(hi_done[job], 1)
                    elif job == "turn_h2":
                        product_ready(job, it, lag)
                        last_used("logits", pair, it, lag)
                        if later(pair):
                            act.wait_ge(h2_stored, 16 * pair)
                        for dk in range(DK):
                            ins = act.activation(h2_t[:, dk, :], bank[:, dk * TOK:(dk + 1) * TOK], ACT.Copy,
                                                 scale=norm2[:, dk:dk + 1])
                        ins.then_inc(read, 1)
                    elif job == "kx":
                        product_ready(job, it, lag)
                        last_used("sx", pair, it, lag)
                        act.activation(kx_t[:, :, :], bank[:, :].rearrange("p (d n) -> p d n", d=DK), ACT.Copy).then_inc(read, 1)
                    elif job == "vx":
                        product_ready(job, it, lag)
                        last_used("pvx", pair, it, lag)
                        act.activation(vx[:, :, :], bank[:, :].rearrange("p (a n) -> p a n", a=2), ACT.Copy).then_inc(read, 1)
                    elif job == "qx":
                        product_ready(job, it, lag)
                        last_used("sx", pair, it, lag)
                        for dk in range(DK):
                            ins = act.activation(qx_t[:, dk, :], bank[:, dk * TOK:(dk + 1) * TOK], ACT.Identity,
                                                 bias=bias_qx[:, dk:dk + 1])
                        ins.then_inc(read, 1)
                    elif job == "sx":
                        act.wait_ge(max_x_done, pair + 1)
                        last_used("turn_px", pair, it, lag)
                        if later(pair):
                            act.wait_ge(rden_x_done, pair)
                        for a in range(2):
                            ins = act.activation(px[:, a, :], bank[:, a * S:(a + 1) * S], ACT.Exp,
                                                 bias=neg_max_x[:, a:a + 1], accum_out=den_x[:, a:a + 1])
                        ins.then_inc(read, 1)
                    elif job == "turn_px":
                        product_ready(job, it, lag)
                        last_used("pvx", pair, it, lag)
                        act.activation(px_t[:, :, :], bank[:, 0:TOK].rearrange("p (a n) -> p a n", a=2), ACT.Copy).then_inc(read, 1)
                    elif job == "pvx":
                        product_ready(job, it, lag)
                        act.wait_ge(rden_x_done, pair + 1)
                        last_used("turn_cx", pair, it, lag)
                        for a in range(2):
                            ins = act.activation(cx[:, a, :], bank[:, a * D:(a + 1) * D], ACT.Copy, scale=rden_x[:, a:a + 1])
                        ins.then_inc(read, 1)
                    elif job == "logits":
                        product_ready(job, it, lag)
                        if later(pair):
                            act.wait_ge(logit_stored, 16 * pair)
                        act.activation(logit[:, :, :], bank[:, 0:2 * E].rearrange("p (a n) -> p a n", a=2), ACT.Copy)\
                           .then_inc(read, 1)
                    elif job in ("square_h", "square_h2"):
                        name, src, done = ("h", x2, h_done) if job == "square_h" else ("h2", x3, h2_done)
                        if job == "square_h":
                            act.wait_ge(x2_done, pair + 1)
                        else:
                            act.wait_ge(work_read[BANK["out3"]], bank_count("out3", it, lag))
                        if later(pair):
                            act.wait_ge(done, pair)
                        for a in range(2):
                            ins = act.activation(square_out[:, a, :], src[:, a, :], ACT.Square,
                                                 accum_out=squares[name][:, a:a + 1])
                        ins.then_inc(stat_done[name], 1)
                    elif job in ("norm_h", "norm_h2"):
                        name, src, dst, done, user = (("h", x2, h_in, h_done, "turn_h") if job == "norm_h" else
                                                      ("h2", x3, h2_in, h2_done, "turn_h2"))
                        act.wait_ge(rstd_done[name], pair + 1)
                        last_used(user, pair, it, lag)
                        for a in range(2):
                            ins = act.activation(dst[:, a, :], src[:, a, :], ACT.Copy, scale=rstd[name][:, a:a + 1])
                        ins.then_inc(done, 1)

                for_iterations(act, step, SCHEDULE["act"], "v1", split_rest)

            @block.vector
            def _(dve):
                def low_weights(which):
                    for i in which:
                        n = split_order[i]
                        b = split_buffer[n]
                        dve.wait_ge(raw_hi_done, i + 1 + (i >= FIRST))
                        dve.scalar_tensor_tensor(out=w_lo[n][:, :, :], in0=raw[b][:, :, 0:widths[n]],
                                                 scalar=scales.get(n, 1.0), in1=w_hi[n][:, :, :].bitcast(F32),
                                                 op0=ALU.mult, op1=ALU.subtract).then_inc(raw_lo_done, 1)

                low_weights(range(FIRST))
                dve.wait_ge(raw_hi_done, FIRST + 1)
                dve.tensor_tensor(bias_lo[:, :], raw_bias, bias_hi[:, :].bitcast(F32), ALU.subtract).then_inc(raw_lo_done, 1)
                dve.memset(values[3][:, :, VP - 1:VP], 1.0).then_inc(ones_set, 1)

                def product_ready(job, it, lag):
                    dve.wait_ge(work_ready[BANK[job]], bank_count(job, it, lag))

                def residual_stats(job, name, dst, res, done, pair, it, lag):
                    b = BANK[job]
                    product_ready(job, it, lag)
                    if later(pair):
                        dve.wait_ge(done, pair)
                    dve.tensor_tensor(dst[:, :, :], work[b][:, :].rearrange("p (a n) -> p a n", a=2), res[:, :, :],
                                      ALU.add).then_inc(work_read[b], 1)
                    dve.wait_ge(work_read[b], bank_count(job, it, lag))
                    for a in range(2):
                        ins = dve.bn_stats(stats[name][:, a, :], dst[:, a, :])
                    ins.then_inc(stats_done[name], 1)
                    wait_apart(dve, stats_done[name], pair + 1, passed["dve"])
                    for a in range(2):
                        ins = dve.bn_aggr(mean_var[name][:, a, :], stats[name][:, a, :])
                    ins.then_inc(stat_done[name], 1)

                def head_shift(n, pair):
                    u = 4 * pair + n
                    s = head_scores[:, n % 2, :, :]
                    dve.wait_ge(qk_prod_done, u + 1)
                    if not isinstance(u, int) or u > 1:
                        dve.wait_ge(head_exp_done, u - 1)
                    if later(u):
                        dve.wait_ge(head_shifted, u)
                    dve.tensor_reduce(s, qk_prod[:, :, :, :], AX.X, ALU.add).then_inc(head_scores_done, 1)
                    dve.wait_ge(head_scores_done, u + 1)
                    dve.tensor_reduce(head_max[:, :], s, AX.X, ALU.max).then_inc(head_max_done, 1)
                    dve.wait_ge(head_max_done, u + 1)
                    dve.tensor_tensor(s, s, head_max[:, :].unsqueeze(2).to_broadcast([P, HH, H]),
                                      ALU.subtract).then_inc(head_shifted, 1)

                def head_output(n, pair):
                    u = 4 * pair + n
                    a, half = n // 2, n % 2
                    if later(u):
                        wait_apart(dve, head_out_done, u, passed["dve"])
                    dve.wait_ge(head_exp_done, u + 1)
                    dve.tensor_reduce(head_den[:, :], head_probs[:, n % 2, :, :], AX.X, ALU.add).then_inc(head_den_done, 1)
                    dve.wait_ge(head_den_done, 2 * u + 1)
                    dve.reciprocal(head_den[:, :], head_den[:, :]).then_inc(head_den_done, 1)
                    dve.wait_ge(pv_prod_done, u + 1)
                    dve.tensor_reduce(head_sum[:, :, :], pv_prod[:, :, :, :].rearrange("p q k d -> p q d k"), AX.X, ALU.add).then_inc(head_sum_done, 1)
                    if n == 0 and later(pair):
                        dve.wait_ge(o1_stored, 32 * pair)
                    dve.wait_ge(head_den_done, 2 * u + 2)
                    dve.wait_ge(head_sum_done, u + 1)
                    dve.tensor_tensor(att_out[1][:, a, half * P:(half + 1) * P].rearrange("p (h d) -> p h d", h=HH),
                                      head_sum[:, :, :], head_den[:, :].unsqueeze(2).to_broadcast([P, HH, DH]),
                                      ALU.mult).then_inc(head_out_done, 1)

                def slot_max(n, pair):
                    g = 4 * pair + n
                    dve.wait_ge(scores_done, g + 1)
                    if not isinstance(g, int) or g > 1:
                        dve.wait_ge(exp_done, g - 1)
                    dve.tensor_reduce(neg_max[:, n % 2, :], scores[:, :].rearrange("p (h n) -> p h n", h=HH), AX.X,
                                      ALU.max, negate=True).then_inc(max_done, 1)

                def slot_lo(n, pair):
                    g = 4 * pair + n
                    dve.wait_ge(probs_hi_done, g + 1)
                    dve.tensor_tensor(probs_lo[:, :, :], probs_t[:, :].rearrange("p (h n) -> p h n", h=HH),
                                      probs_hi[:, :, :], ALU.subtract).then_inc(probs_lo_done, 1)

                def slot_out(n, pair, it, lag):
                    g = 4 * pair + n
                    a, half = n // 2, n % 2
                    dve.wait_ge(pv_done, g + 1)
                    if later(g):
                        dve.wait_ge(out_done, g)
                    if n == 0 and later(pair):
                        dve.wait_ge(work_ready[BANK["turn_o3"]], bank_count("turn_o3", it, lag + 1))
                    src = pv[:, 0:HH * VP].rearrange("p (h c) -> p h c", h=HH)
                    dve.reciprocal(rden[:, :].unsqueeze(2), src[:, :, VP - 1:VP])
                    dve.tensor_reduce(osum[:, :, :], src[:, :, 0:3 * DH].rearrange("p h (c d) -> p h d c", c=3), AX.X,
                                      ALU.add).then_inc(osum_done, 1)
                    dve.wait_ge(osum_done, g + 1)
                    dve.tensor_tensor(att_out[3][:, a, half * P:(half + 1) * P].rearrange("p (h d) -> p h d", h=HH),
                                      osum[:, :, :], rden[:, :].unsqueeze(2).to_broadcast([P, HH, DH]),
                                      ALU.mult).then_inc(out_done, 1)

                def step(job, pair, it, lag):
                    bank = work[BANK[job]] if job in BANK else None
                    read = work_read[BANK[job]] if job in BANK else None
                    if job.startswith("head_shift"):
                        head_shift(int(job[-1]), pair)
                    elif job.startswith("head_output"):
                        head_output(int(job[-1]), pair)
                    elif job.startswith("heads_out"):
                        slot_out(int(job[-1]), pair, it, lag)
                    elif job[:-1] == "max":
                        slot_max(int(job[-1]), pair)
                    elif job[:-1] == "lo":
                        slot_lo(int(job[-1]), pair)
                    elif job in ("turn_o1", "turn_x1", "turn_cx", "turn_o3"):
                        src = {"turn_o1": "o1", "turn_x1": "x1", "turn_cx": "cx", "turn_o3": "o3"}[job]
                        dve.wait_ge(hi_done[job], pair + 1)
                        hi, lo = parts[src]
                        dve.tensor_tensor(lo[:, :, :], bank[:, :].rearrange("p (d n) -> p d n", d=DK),
                                          hi[:, :, :].bitcast(F32), ALU.subtract).then_inc(read, 1)
                    elif job == "turn_h":
                        dve.wait_ge(hi_done[job], pair + 1)
                        hi, lo = parts["h"]
                        for dk in range(DK):
                            ins = dve.scalar_tensor_tensor(out=lo[:, dk, :], in0=bank[:, dk * TOK:(dk + 1) * TOK],
                                                           scalar=norm1[:, dk:dk + 1], in1=hi[:, dk, :].bitcast(F32),
                                                           op0=ALU.mult, op1=ALU.subtract)
                        ins.then_inc(read, 1)
                    elif job in ("q3_0", "q3_1", "k3_0", "k3_1"):
                        m = int(job[3])
                        dve.wait_ge(hi_done[job], pair + 1)
                        src = bank[:, :].rearrange("p (g n) -> p g n", g=2)
                        rows = slice(P // 2, P) if job[0] == "q" else slice(0, P)
                        hi = (q_rows[3] if job[0] == "q" else k_parts[3][:, 0])[rows, 2 * m:2 * m + 2, :]
                        lo = hi if job[0] == "q" else k_parts[3][:, 1, 2 * m:2 * m + 2, :]
                        dve.tensor_tensor(lo, src[rows], hi.bitcast(F32), ALU.subtract).then_inc(read, 1)
                    elif job == "v3_rest":
                        dve.wait_ge(hi_done["v3"], pair + 1)
                        if later(pair):
                            dve.wait_ge(v_low_done, pair)
                        dve.tensor_tensor(v_rest[:, :, :], v_full[:, :, :], values[3][:, :, 0:DH],
                                          ALU.subtract).then_inc(v_rest_done, 1)
                    elif job == "v3_mid":
                        dve.wait_ge(v_mid_done, pair + 1)
                        dve.tensor_tensor(values[3][:, :, 2 * DH:3 * DH], v_rest[:, :, :],
                                          values[3][:, :, DH:2 * DH], ALU.subtract).then_inc(v_low_done, 1)
                    elif job == "out1":
                        dve.wait_ge(o1_loaded, 32 * (pair + 1))
                        residual_stats(job, "y1", y1, x_res, x1_done, pair, it, lag)
                    elif job == "outx":
                        dve.wait_ge(x1_done, pair + 1)
                        residual_stats(job, "z2", z2, x1, x2_done, pair, it, lag)
                    elif job == "out3":
                        product_ready(job, it, lag)
                        dve.wait_ge(x2_res_loaded, 16 * (pair + 1))
                        if later(pair):
                            dve.wait_ge(h2_done, pair)
                            dve.wait_ge(sum_done, pair)
                        dve.tensor_tensor(x3[:, :, :], bank[:, :].rearrange("p (a n) -> p a n", a=2), x2_res[:, :, :],
                                          ALU.add).then_inc(read, 1)
                    elif job == "sx":
                        product_ready(job, it, lag)
                        if later(pair):
                            dve.wait_ge(read, bank_count(job, it, lag + 1))
                        dve.tensor_reduce(neg_max_x[:, :], bank[:, 0:TOK].rearrange("p (a n) -> p a n", a=2), AX.X, ALU.max,
                                          negate=True).then_inc(max_x_done, 1)
                    elif job == "recip_x":
                        dve.wait_ge(work_read[BANK["sx"]], bank_count("sx", it, lag))
                        if later(pair):
                            dve.wait_ge(work_read[BANK["pvx"]], bank_count("pvx", it, lag + 1))
                        dve.reciprocal(rden_x[:, :], den_x[:, :]).then_inc(rden_x_done, 1)

                low_weights(range(FIRST, len(split_order)))
                for_iterations(dve, step, SCHEDULE["dve"])

            @block.gpsimd
            def _(pool):
                pool.memset(half_power[:, :], -0.5).then_inc(power_set, 1)
                pool.wait_ge(const_loaded, 16 * CONSTS)
                pool.wait_ge(power_set, 1)
                pool.wait_ge(raw_lo_done, FIRST + 1)

                def wait(semaphore, value):
                    wait_apart(pool, semaphore, value, passed["pool"])

                def root(name, src, scale, eps, pair):
                    wait(stat_done[name], pair + 1)
                    pool.tensor_scalar(var_eps[name][:, :], src, scale, eps, ALU.mult, ALU.add).then_inc(eps_done[name], 1)
                    pool.wait_ge(eps_done[name], pair + 1)
                    pool.tensor_tensor(rstd[name][:, :], var_eps[name][:, :], half_power[:, :], ALU.pow)\
                        .then_inc(rstd_done[name], 1)

                def normalize(src, name, dst, done, pair):
                    wait(rstd_done[name], pair + 1)
                    for a in range(2):
                        ins = pool.tensor_scalar(dst[:, a, :], src[:, a, :], mean_var[name][:, a, 0:1], rstd[name][:, a:a + 1],
                                                 ALU.subtract, ALU.mult)
                    ins.then_inc(done, 1)

                def qk_products(n, pair, it, lag):
                    u = 4 * pair + n
                    a, half = n // 2, n % 2
                    job = f"qk1_{a}"
                    wait(work_read[BANK[job]], bank_count(job, it, lag))
                    if later(u):
                        wait(head_scores_done, u)
                    q = qk1[:, a, half * P:(half + 1) * P].rearrange("p (h d) -> p h d", h=HH)
                    k = qk1[:, a, D:2 * D].rearrange("p (h d) -> p h d", h=H)
                    pool.tensor_tensor(qk_prod[:, :, :, :], q.unsqueeze(2).to_broadcast([P, HH, H, DH]),
                                       k.unsqueeze(1).to_broadcast([P, HH, H, DH]), ALU.mult).then_inc(qk_prod_done, 1)

                def pv_products(n, pair, it, lag):
                    u = 4 * pair + n
                    wait(work_read[BANK["v1"]], bank_count("v1", it, lag))
                    wait(head_exp_done, u + 1)
                    if later(u):
                        wait(head_sum_done, u)
                    v = v1[:, n // 2, :].rearrange("p (h d) -> p h d", h=H)
                    pool.tensor_tensor(pv_prod[:, :, :, :], head_probs[:, n % 2, :, :].unsqueeze(3).to_broadcast([P, HH, H, DH]),
                                       v.unsqueeze(1).to_broadcast([P, HH, H, DH]), ALU.mult).then_inc(pv_prod_done, 1)

                def step(job, pair, it, lag):
                    if job.startswith("qk_products"):
                        qk_products(int(job[-1]), pair, it, lag)
                    elif job.startswith("pv_products"):
                        pv_products(int(job[-1]), pair, it, lag)
                    elif job in ("root_y1", "root_z2"):
                        root(job[5:], mean_var[job[5:]][:, :, 1], 1.0, 1e-5, pair)
                    elif job in ("root_h", "root_h2"):
                        root(job[5:], squares[job[5:]][:, :], 1.0 / D, 1e-6, pair)
                    elif job in ("x_lo", "ctx_lo"):
                        name, src = ("x", x_t) if job == "x_lo" else ("ctx", ctx_t)
                        wait(hi_done[name], pair + 1)
                        hi, lo = parts[name]
                        pool.tensor_tensor(lo[:, :, :], src[:, :, :], hi[:, :, :].bitcast(F32), ALU.subtract)\
                            .then_inc(lo_done[name], 1)
                    elif job == "sum":
                        wait(work_read[BANK["out3"]], bank_count("out3", it, lag))
                        if later(pair):
                            wait(sum_stored, 16 * pair)
                        pool.tensor_tensor(x2_x3[:, :, :], x3[:, :, :], x2_res[:, :, :], ALU.add).then_inc(sum_done, 1)
                    elif job == "norm_x1":
                        if later(pair):
                            wait(work_read[BANK["outx"]], bank_count("outx", it, lag + 1))
                            wait(work_ready[BANK["turn_x1"]], bank_count("turn_x1", it, lag + 1))
                        normalize(y1, "y1", x1, x1_done, pair)
                    elif job == "norm_x2":
                        if later(pair):
                            wait(x2_stored, 16 * pair)
                            wait(h_done, pair)
                        normalize(z2, "z2", x2, x2_done, pair)

                for_iterations(pool, step, SCHEDULE["pool"])


def phase_b(nc, t, scratch, sem, out):
    ctx = ExitStack()
    NT = B
    TG = GT // P

    def sb(name, shape, dt=F32):
        return ctx.enter_context(nc.sbuf_tensor(name, shape, dt))

    with ctx:
        tok_hi = sb("tok_hi", [P, DK, B * S], F32R)
        tok_lo = sb("tok_lo", [P, DK, B * S], F32R)
        acc = sb("acc", [P, NT, D])
        WC = DK * DFF
        w_raw = sb("w_raw", [P, 3, WC])
        w_hi = sb("we_hi", [P, 2, 3, WC], F32R)
        w_lo = sb("we_lo", [P, 2, 3, WC], F32R)
        silu = sb("silu", [P, 2, GT])
        prod = sb("prod", [P, 2, GT])
        act_hi = sb("act_hi", [P, 2, FT, GT], F32R)
        act_lo = sb("act_lo", [P, 2, FT, GT], F32R)
        h_raw = [w[:, 0, k, :].bitcast(F32).rearrange("p (d n) -> p d n", d=DK) for w in (w_hi, w_lo) for k in range(3)]
        NR = len(h_raw)
        combine = sb("combine", [P, NT, NE])
        logit = sb("logit_all", [P, NT, E])
        iota = sb("iota", [P, NT, E])
        pr = sb("pr", [P, NT, E])
        eq = sb("eq", [P, NT, E])
        one_hot = [sb(f"one_hot{i}", [P, NT, E]) for i in range(2)]
        rows = {n: sb(f"row_{n}", [P, NT]) for n in ("max", "sum", "top1", "top2", "at", "ratio", "den", "w1", "w2")}
        stats = sb("stats_b", [P, NT, 6])
        mean_var = sb("mean_var_b", [P, NT, 2])
        var_eps = sb("var_eps_b", [P, NT])
        rstd = sb("rstd_b", [P, NT])
        half_power = sb("half_power_b", [P, NT])

        gate = [ctx.enter_context(nc.psum_tensor(f"gate{i}", [P, GT], F32)) for i in range(2)]
        up = [ctx.enter_context(nc.psum_tensor(f"up{i}", [P, GT], F32)) for i in range(2)]
        down = [ctx.enter_context(nc.psum_tensor(f"down{i}", [P, 512], F32)) for i in range(4)]

        loaded, w_loaded = sem("b_loaded"), sem("w_loaded")
        h_loaded = [sem(f"h_loaded{i}") for i in range(NR)]
        acc_loaded = [sem(f"acc_loaded{g}") for g in range(NGT)]
        SPLIT_AT = {0: (1,), 1: (2,), 2: (3, 4), 3: (5, 6), 4: (7,)}
        def weights_at(first):
            return (5, 6, 7) if first else (1, 2, 3)
        h_hi_done, h_lo_done = sem("h_hi_done"), sem("h_lo_done")
        w_hi_done, w_lo_done = sem("w_hi_done"), sem("w_lo_done")
        gate_up_ready, silu_done, prod_done = sem("gate_up_ready"), sem("silu_done"), sem("prod_done")
        act_hi_done, act_lo_done = sem("act_hi_done"), sem("act_lo_done")
        down_ready, down_added = sem("down_ready"), sem("down_added")
        passed_sp = sem("passed_sp_b")
        route, route_max, route_exp, ratio_ready, ratio_exp = (
            sem(n) for n in ("route", "route_max", "route_exp", "ratio_ready", "ratio_exp"))
        pool_own_b, var_done, rstd_b_done, norm_done, out_stored = (
            sem(n) for n in ("pool_own_b", "var_done", "rstd_b_done", "norm_done", "out_stored"))

        def experts(engine, body):
            body(0, 1, True, True)
            with engine.Fori(0, E // 2 - 1) as i:
                body(2 * i + 1, 0, False, True)
                body(2 * i + 2, 1, False, True)
            body(E - 1, 0, False, True)
            body(E, 1, False, False)

        with nc.Block() as block:

            @block.sync
            def _(sp):
                sp.dma_start(logit[:, :, :], scratch["logit"]).then_inc(loaded, 16)
                sp.dma_start(iota[:, :, :], t["iota"]).then_inc(loaded, 16)
                for k, n in enumerate(("w_gate", "w_up", "w_down")):
                    sp.dma_start(w_raw[:, k, :], t[n][0, :, :]).then_inc(w_loaded, 16)
                for g in range(NGT):
                    if g >= NR:
                        sp.wait_ge(h_lo_done, g - NR + 1)
                    sp.dma_start(h_raw[g % NR], scratch["h2_t"][:, :, g * GT:(g + 1) * GT]).then_inc(h_loaded[g % NR], 16)
                    for n in {0: (), NGT - 1: (g - 1, g)}.get(g, (g - 1,)):
                        sp.dma_start(acc[:, n * TG:(n + 1) * TG, :], scratch["x2_x3"][:, n * TG:(n + 1) * TG, :])\
                          .then_inc(acc_loaded[n], 16)

                def expert(x, par, first, more):
                    if more:
                        wait_apart(sp, w_lo_done, 3 * (x + 1), passed_sp)
                        for k, n in enumerate(("w_gate", "w_up", "w_down")):
                            src = t[n][x + 1, :, :] if isinstance(x, int) else t[n][bass.ds(x + 1, 1), :, :].rearrange("a p n -> (a p) n")
                            sp.dma_start(w_raw[:, k, :], src).then_inc(w_loaded, 16)

                experts(sp, expert)
                for n in range(NGT):
                    sp.wait_ge(norm_done, n + 1)
                    sp.dma_start(out[:, n * TG:(n + 1) * TG, :], acc[:, n * TG:(n + 1) * TG, :]).then_inc(out_stored, 16)
                sp.wait_ge(out_stored, 16 * NGT)

            @block.tensor
            def _(pe):
                def piece(w, par, kind, i, c, n):
                    width = DFF if kind < 2 else D
                    return w[:, par, kind, i * width + c:i * width + c + n]

                def gate_up(x, par, g, f):
                    k = (x * NGT + g) * FT + f
                    if not isinstance(k, int) or k > 1:
                        pe.wait_ge(prod_done, k - 1)
                    for kind, bank in ((0, gate[f % 2]), (1, up[f % 2])):
                        n = 0
                        for wp, hp in ((w_hi, tok_hi), (w_hi, tok_lo), (w_lo, tok_hi)):
                            for dk in range(DK):
                                n += 1
                                mm = pe.matmul(bank[:, :], piece(wp, par, kind, dk, f * P, P),
                                               hp[:, dk, g * GT:(g + 1) * GT], start=(n == 1), stop=(n == 3 * DK))
                    mm.then_inc(gate_up_ready, 1)

                def down_tile(x, par, g, j):
                    step = x * NGT + g
                    if j == 0:
                        pe.wait_ge(act_lo_done, FT * (step + 1))
                    if not isinstance(step, int) or step > 0:
                        pe.wait_ge(down_added, FT * (step - 1) + j + 1)
                    n = 0
                    for ap, wp in ((act_hi, w_hi), (act_hi, w_lo), (act_lo, w_hi)):
                        for f in range(FT):
                            n += 1
                            mm = pe.matmul(down[j][:, 0:D], ap[:, g % 2, f, j * P:(j + 1) * P],
                                           piece(wp, par, 2, f, 0, D), start=(n == 1), stop=(n == 3 * FT))
                    mm.then_inc(down_ready, 1)

                def expert(x, par, first, more):
                    pe.wait_ge(w_lo_done, 3 * (x + 1))
                    for g in range(NGT):
                        if first:
                            pe.wait_ge(h_lo_done, g + 1)
                        last = None if first and g == 0 else (x, par, g - 1) if g else (x - 1, 1 - par, NGT - 1)
                        for f in range(FT):
                            gate_up(x, par, g, f)
                            if last:
                                for j in ((), (0,), (1,), (2, 3))[f]:
                                    down_tile(*last, j)

                experts(pe, expert)
                for j in range(TG):
                    down_tile(E, 1, NGT - 1, j)

            @block.scalar
            def _(act):
                def split_weights(x, par, k):
                    act.wait_ge(w_loaded, 48 * (x + 1))
                    act.activation(w_hi[:, par, k, :], w_raw[:, k, :], ACT.Copy).then_inc(w_hi_done, 1)

                for k in range(3):
                    split_weights(0, 1, k)
                def split_tokens(g):
                    act.wait_ge(h_loaded[g % NR], 16 * (g // NR + 1))
                    act.activation(tok_hi[:, :, g * GT:(g + 1) * GT], h_raw[g % NR], ACT.Copy).then_inc(h_hi_done, 1)

                split_tokens(0)

                def expert(x, par, first, more):
                    for g in range(NGT):
                        step = x * NGT + g
                        if first:
                            for n in SPLIT_AT.get(g, ()):
                                split_tokens(n)
                            if g == 2:
                                act.wait_ge(route_max, 1)
                                act.activation(pr[:, :, :], logit[:, :, :], ACT.Exp).then_inc(route_exp, 1)
                            if g == 5:
                                act.wait_ge(ratio_ready, 1)
                                act.activation(rows["ratio"][:, :], rows["ratio"][:, :], ACT.Exp).then_inc(ratio_exp, 1)
                        for f in range(FT):
                            k = step * FT + f
                            act.wait_ge(gate_up_ready, k + 1)
                            act.activation(silu[:, f % 2, :], gate[f % 2][:, :], ACT.Silu).then_inc(silu_done, 1)
                            act.wait_ge(prod_done, k + 1)
                            if f == 0 and not (isinstance(step, int) and step < 2):
                                act.wait_ge(down_ready, TG * (step - 1))
                            act.activation(act_hi[:, g % 2, f, :], prod[:, f % 2, :], ACT.Copy).then_inc(act_hi_done, 1)
                        if more and g in weights_at(first):
                            if first:
                                act.wait_ge(h_lo_done, NGT)
                            elif g == 1:
                                act.wait_ge(down_ready, TG * x * NGT)
                            split_weights(x + 1, 1 - par, weights_at(first).index(g))

                experts(act, expert)

            @block.vector
            def _(dve):
                own = [0]

                def step_of_route(instruction):
                    own[0] += 1
                    instruction.then_inc(route, 1)
                    dve.wait_ge(route, own[0])

                def low_weights(x, par, k):
                    dve.wait_ge(w_hi_done, 3 * x + k + 1)
                    dve.tensor_tensor(w_lo[:, par, k, :], w_raw[:, k, :], w_hi[:, par, k, :].bitcast(F32),
                                      ALU.subtract).then_inc(w_lo_done, 1)

                for k in range(3):
                    low_weights(0, 1, k)
                def low_tokens(g):
                    dve.wait_ge(h_hi_done, g + 1)
                    cols = slice(g * GT, (g + 1) * GT)
                    dve.tensor_tensor(tok_lo[:, :, cols], h_raw[g % NR], tok_hi[:, :, cols].bitcast(F32),
                                      ALU.subtract).then_inc(h_lo_done, 1)

                low_tokens(0)

                def wide(x):
                    return x[:, :].unsqueeze(2).to_broadcast([P, NT, E])

                def best(n):
                    top = f"top{n + 1}"
                    step_of_route(dve.tensor_reduce(rows[top][:, :], pr[:, :, :], AX.X, ALU.max))
                    step_of_route(dve.tensor_tensor(eq[:, :, :], pr[:, :, :], wide(rows[top]), ALU.is_equal))
                    step_of_route(dve.scalar_tensor_tensor(out=eq[:, :, :], in0=eq[:, :, :], scalar=-float(E),
                                                           in1=iota[:, :, :], op0=ALU.mult, op1=ALU.add))
                    step_of_route(dve.tensor_reduce(rows["at"][:, :], eq[:, :, :], AX.X, ALU.min))
                    step_of_route(dve.tensor_tensor(one_hot[n][:, :, :], eq[:, :, :], wide(rows["at"]), ALU.is_equal))

                def router(part):
                    if part == 1:
                        dve.wait_ge(loaded, 32)
                        step_of_route(dve.tensor_reduce(rows["max"][:, :], logit[:, :, :], AX.X, ALU.max))
                        dve.tensor_tensor(logit[:, :, :], logit[:, :, :], wide(rows["max"]), ALU.subtract).then_inc(route_max, 1)
                    elif part == 2:
                        dve.wait_ge(route_exp, 1)
                        step_of_route(dve.tensor_reduce(rows["sum"][:, :], pr[:, :, :], AX.X, ALU.add))
                        step_of_route(dve.reciprocal(rows["sum"][:, :], rows["sum"][:, :]))
                        step_of_route(dve.tensor_tensor(pr[:, :, :], pr[:, :, :], wide(rows["sum"]), ALU.mult))
                    elif part == 3:
                        best(0)
                        step_of_route(dve.scalar_tensor_tensor(out=pr[:, :, :], in0=one_hot[0][:, :, :], scalar=-2.0,
                                                               in1=pr[:, :, :], op0=ALU.mult, op1=ALU.add))
                    elif part == 4:
                        best(1)
                        dve.tensor_tensor(rows["ratio"][:, :], rows["top2"][:, :], rows["top1"][:, :], ALU.subtract)\
                           .then_inc(ratio_ready, 1)
                    elif part == 5:
                        dve.wait_ge(ratio_exp, 1)
                        step_of_route(dve.tensor_scalar(rows["den"][:, :], rows["ratio"][:, :], 1.0, None, ALU.add))
                        step_of_route(dve.reciprocal(rows["w1"][:, :], rows["den"][:, :]))
                        step_of_route(dve.tensor_tensor(rows["w2"][:, :], rows["ratio"][:, :], rows["w1"][:, :], ALU.mult))
                        step_of_route(dve.tensor_tensor(one_hot[0][:, :, :], one_hot[0][:, :, :], wide(rows["w1"]), ALU.mult))
                        step_of_route(dve.tensor_tensor(one_hot[1][:, :, :], one_hot[1][:, :, :], wide(rows["w2"]), ALU.mult))
                        step_of_route(dve.tensor_tensor(combine[:, :, 1:NE], one_hot[0][:, :, :], one_hot[1][:, :, :], ALU.add))

                step_of_route(dve.memset(combine[:, :, 0:1], 1.0))

                def product(x, g, f):
                    k = (x * NGT + g) * FT + f
                    dve.wait_ge(silu_done, k + 1)
                    if not isinstance(k, int) or k > 1:
                        dve.wait_ge(act_lo_done, k - 1)
                    dve.tensor_tensor(prod[:, f % 2, :], silu[:, f % 2, :], up[f % 2][:, :], ALU.mult)\
                       .then_inc(prod_done, 1)

                def add_tile(x, g, j):
                    step = x * NGT + g
                    n = g * TG + j
                    dve.wait_ge(down_ready, TG * step + j + 1)
                    if j == 0 and isinstance(x, int) and x == 0:
                        dve.wait_ge(acc_loaded[g], 16)
                    weight = combine[:, n, x:x + 1] if isinstance(x, int) else combine[:, n, bass.ds(x, 1)]
                    dve.scalar_tensor_tensor(out=acc[:, n, :], in0=down[j][:, 0:D], scalar=weight, in1=acc[:, n, :],
                                             op0=ALU.mult, op1=ALU.add).then_inc(down_added, 1)

                def row_stats(g):
                    dve.wait_ge(down_added, TG * (E * NGT + g + 1))
                    tiles = range(g * TG, (g + 1) * TG)
                    for n in tiles:
                        ins = dve.bn_stats(stats[:, n, :], acc[:, n, :])
                    step_of_route(ins)
                    for n in tiles:
                        ins = dve.bn_aggr(mean_var[:, n, :], stats[:, n, :])
                    ins.then_inc(var_done, 1)

                def normalize(g):
                    dve.wait_ge(rstd_b_done, g + 1)
                    for n in range(g * TG, (g + 1) * TG):
                        ins = dve.tensor_scalar(acc[:, n, :], acc[:, n, :], mean_var[:, n, 0:1], rstd[:, n:n + 1],
                                                ALU.subtract, ALU.mult)
                    ins.then_inc(norm_done, 1)

                def expert(x, par, first, more):
                    for g in range(NGT):
                        last = None if first and g == 0 else (x, g - 1) if g else (x - 1, NGT - 1)
                        if first:
                            for n in SPLIT_AT.get(g, ()):
                                low_tokens(n)
                            router(g)
                        for f in range(FT):
                            product(x, g, f)
                            if last:
                                for j in ((), (0,), (1,), (2, 3))[f]:
                                    add_tile(*last, j)
                            if not more and f == 1 and g >= 2:
                                normalize(g - 2)
                        if not more and g >= 1:
                            row_stats(g - 1)
                        if more and g in weights_at(first):
                            if first:
                                dve.wait_ge(h_lo_done, NGT)
                            low_weights(x + 1, 1 - par, weights_at(first).index(g))

                experts(dve, expert)
                normalize(NGT - 2)
                for j in range(TG):
                    add_tile(E, NGT - 1, j)
                row_stats(NGT - 1)
                normalize(NGT - 1)

            @block.gpsimd
            def _(pool):
                pool.memset(half_power[:, :], -0.5).then_inc(pool_own_b, 1)

                def root(g):
                    n = slice(g * TG, (g + 1) * TG)
                    pool.wait_ge(var_done, g + 1)
                    pool.tensor_scalar(var_eps[:, n], mean_var[:, n, 1], 1.0, 1e-5, ALU.mult, ALU.add).then_inc(pool_own_b, 1)
                    pool.wait_ge(pool_own_b, g + 2)
                    pool.tensor_tensor(rstd[:, n], var_eps[:, n], half_power[:, n], ALU.pow).then_inc(rstd_b_done, 1)

                def expert(x, par, first, more):
                    for g in range(NGT):
                        for f in range(FT):
                            k = (x * NGT + g) * FT + f
                            pool.wait_ge(act_hi_done, k + 1)
                            pool.tensor_tensor(act_lo[:, g % 2, f, :], prod[:, f % 2, :],
                                               act_hi[:, g % 2, f, :].bitcast(F32), ALU.subtract).then_inc(act_lo_done, 1)
                        if not more and g >= 1:
                            root(g - 1)

                experts(pool, expert)
                root(NGT - 1)


def decoder(nc, t, out):
    scratch = {
        "o1": nc.dram_tensor("o1_scratch", (B, S * D), F32, kind="Internal").ap(),
        "x2": nc.dram_tensor("x2_scratch", (P, B, D), F32, kind="Internal").ap(),
        "x2_x3": nc.dram_tensor("x2_x3_scratch", (P, B, D), F32, kind="Internal").ap(),
        "h2_t": nc.dram_tensor("h2_scratch", (P, DK, B * S), F32, kind="Internal").ap(),
        "logit": nc.dram_tensor("logit_scratch", (P, B, E), F32, kind="Internal").ap(),
    }
    with ExitStack() as ctx:
        def sem(name):
            return ctx.enter_context(nc.semaphore(name))

        phase_a(nc, t, scratch, sem)
        phase_b(nc, t, scratch, sem, out)


def layout(inputs):
    import numpy as np

    def a(name):
        return np.asarray(inputs[name])

    def rows(w):
        return np.ascontiguousarray(w.reshape(-1, P, w.shape[-1]).transpose(1, 0, 2))

    def twice(w):
        w = w.reshape(*w.shape[:-1], NG, HG * DH)
        return np.concatenate([w, w], -1).reshape(*w.shape[:-2], NG * P)

    def column(v):
        return np.ascontiguousarray(v.reshape(-1, P).T)

    def transposed(x):
        return rows(x.reshape(B * S, D).T)

    def experts(shared, routed):
        w = np.concatenate([a(shared)[None], a(routed)])
        return np.ascontiguousarray(np.stack([rows(x).reshape(P, -1) for x in w]))

    p = np.arange(P)
    return {
        "x": np.ascontiguousarray(a("x").transpose(1, 0, 2)),
        "x_t": transposed(a("x")),
        "ctx_t": transposed(a("ctx_1024")),
        "ident": np.eye(P, dtype=np.float32),
        "head_mask": (p[:, None] % (P // 2) // DH == np.arange(HG)).astype(np.float32),
        "iota": np.ascontiguousarray(np.broadcast_to(np.arange(E, dtype=np.float32), (P, B, E))),
        "wqk1": rows(np.concatenate([a("L0_attn_Wq"), a("L0_attn_Wk")]).T),
        "wv1": rows(a("L0_attn_Wv").T), "wo1": rows(a("L0_attn_Wo").T),
        "wkx": rows(a("L0_xattn_Wk").T), "wvx": rows(a("L0_xattn_Wv").T),
        "wqx": rows(a("L0_xattn_Wq").T), "wox": rows(a("L0_xattn_Wo").T),
        "wq3": rows(twice(a("L0_ffn_wq"))), "wk3": rows(twice(a("L0_ffn_wk"))),
        "wv3": rows(a("L0_ffn_wv")), "wo3": rows(a("L0_ffn_wo")),
        "bias_rows": np.stack([np.concatenate([a(n), a(m)]) for n, m in (("L0_attn_bq", "L0_attn_bk"), (
            "L0_attn_bv", "L0_attn_bo"), ("L0_xattn_bv", "L0_xattn_bo"))]),
        "select": np.repeat(np.eye(BIAS_ROWS, dtype=np.float32)[:, :, None], P, 2),
        "bias_qx": column(a("L0_xattn_bq")),
        "norm1": column(a("L0_ffn_norm1_w")), "norm2": column(a("L0_ffn_norm2_w")),
        "router": rows(a("L0_ffn_router_w")),
        "w_gate": experts("L0_ffn_sh_gate", "L0_ffn_e_gate"),
        "w_up": experts("L0_ffn_sh_up", "L0_ffn_e_up"),
        "w_down": experts("L0_ffn_sh_down", "L0_ffn_e_down"),
    }


def kernel(**inputs):
    import numpy as np
    import concourse.bacc as bacc
    from concourse.bass_utils import run_bass_kernel_spmd as run

    nc = bacc.Bacc("TRN2", target_bir_lowering=False, num_devices=1)
    arrays, t = {}, {}
    for name, x in layout(inputs).items():
        arrays[f"in_{name}"] = x
        t[name] = nc.dram_tensor(f"in_{name}", x.shape, mybir.dt.from_np(x.dtype), kind="ExternalInput").ap()
    out = nc.dram_tensor("out", (P, B, D), F32, kind="ExternalOutput").ap()
    decoder(nc, t, out)
    r = run(nc, [arrays], core_ids=[0])
    return np.ascontiguousarray(r.results[0]["out"].transpose(1, 0, 2))
```
